# Optimizing a Trainium2 kernel written in Bass

```python
import numpy as np
import jax
import jax.numpy as jnp

def _softmax(x, axis=-1):
    return jax.nn.softmax(x, axis=axis)

def _gelu(x):
    return jax.nn.gelu(x, approximate=True)

def _silu(x):
    return jax.nn.silu(x)

def _sigmoid(x):
    return jax.nn.sigmoid(x)

def _layernorm(x, axis=-1, eps=1e-05):
    m = jnp.mean(x, axis=axis, keepdims=True)
    v = jnp.var(x, axis=axis, keepdims=True)
    return (x - m) / jnp.sqrt(v + eps)

def _scatter_add(tgt, idx, src, axis=0):
    return tgt.at[idx].add(src)

def _segment_sum(src, seg, n):
    return jax.ops.segment_sum(src, seg, n)
kernel_name = 'mk_macaron_d2_jaxref_r4_f19e78'

def setup_inputs(seed: int=0):
    np.random.seed(seed)
    _w = jnp.asarray

    def _L0_attn_setup():
        import jax, jax.numpy as jnp
        import numpy as np
        B, T, HS, H, R = (4, 512, 256, 16, 16)
        D = HS // H
        LOGIT_01 = float(np.log(0.1 / 0.9))
        LOGIT_098 = float(np.log(0.98 / 0.02))

        def _rope_cos_sin(seq_len, dim, base=10000.0):
            half = dim // 2
            inv_freq = 1.0 / base ** (jnp.arange(half, dtype=jnp.float32) / half)
            freqs = jnp.arange(seq_len, dtype=jnp.float32)[:, None] * inv_freq[None, :]
            return (jnp.cos(freqs), jnp.sin(freqs))

        def _apply_rope(x, cos, sin):
            c = cos[None, :, None, :]
            s = sin[None, :, None, :]
            x1 = x[..., 0::2]
            x2 = x[..., 1::2]
            r1 = x1 * c - x2 * s
            r2 = x1 * s + x2 * c
            return jnp.stack((r1, r2), axis=-1).reshape(x.shape)
        key = jax.random.key(seed)
        ks = jax.random.split(key, 10)

        def rn(k, shape, s=0.02):
            return jax.random.normal(k, shape, dtype=jnp.float32) * s
        return {'x': jax.random.normal(ks[0], (B, T, HS), dtype=jnp.float32), 'q_w': rn(ks[1], (HS, HS)), 'k_w': rn(ks[2], (HS, HS)), 'v_w': rn(ks[3], (HS, HS)), 'Wq': rn(ks[4], (H, R, D), 0.05), 'Wk': rn(ks[5], (H, R, D), 0.05), 'g_w': rn(ks[6], (H * R, HS)), 'g_b': jnp.full((H * R,), LOGIT_01, dtype=jnp.float32), 'base_decay_logits': jnp.full((H, R), LOGIT_098, dtype=jnp.float32), 'out_w': rn(ks[7], (HS, HS)), 'out_b': jnp.zeros((HS,), dtype=jnp.float32), 'ln_g': jnp.ones((HS,), dtype=jnp.float32), 'ln_b': jnp.zeros((HS,), dtype=jnp.float32)}
    _L0_attn_in = _L0_attn_setup()

    def _L0_ffn_setup():
        import jax, jax.numpy as jnp
        import numpy as np
        D_MODEL = 256
        M = 64
        INNER = 16
        key = jax.random.key(seed)
        ks = jax.random.split(key, 9)

        def init(k, shape, fan_in):
            bound = 1.0 / np.sqrt(fan_in)
            return jax.random.uniform(k, shape, jnp.float32, -bound, bound)
        x = jax.random.normal(ks[0], (16, 1024, D_MODEL), dtype=jnp.float32)
        Win = init(ks[1], (D_MODEL, M), D_MODEL)
        bin_ = init(ks[2], (M,), D_MODEL)
        W1 = init(ks[3], (M, INNER), 1)
        b1 = init(ks[4], (M, INNER), 1)
        W2 = init(ks[5], (M, INNER), INNER)
        b2 = init(ks[6], (M,), INNER)
        Wout = init(ks[7], (M, D_MODEL), M)
        bout = init(ks[8], (D_MODEL,), M)
        return {'x': x, 'Win': Win, 'bin_': bin_, 'W1': W1, 'b1': b1, 'W2': W2, 'b2': b2, 'Wout': Wout, 'bout': bout}
    _L0_ffn_in = _L0_ffn_setup()

    def _L1_attn_setup():
        import jax, jax.numpy as jnp
        import numpy as np
        D_MODEL = 256
        NUM_HEADS = 16
        HEAD_DIM = D_MODEL // NUM_HEADS
        EPS = 1e-08
        key = jax.random.key(seed)
        ks = jax.random.split(key, 6)
        B, T = (4, 512)
        s = 0.02
        return {'x': jax.random.normal(ks[0], (B, T, D_MODEL), dtype=jnp.float32), 'Wq': jax.random.normal(ks[1], (D_MODEL, D_MODEL), dtype=jnp.float32) * s, 'Wk': jax.random.normal(ks[2], (D_MODEL, D_MODEL), dtype=jnp.float32) * s, 'Wv': jax.random.normal(ks[3], (D_MODEL, D_MODEL), dtype=jnp.float32) * s, 'Wo': jax.random.normal(ks[4], (D_MODEL, D_MODEL), dtype=jnp.float32) * s, 'bo': jnp.zeros((D_MODEL,), dtype=jnp.float32)}
    _L1_attn_in = _L1_attn_setup()

    def _L1_ffn_setup():
        import jax, jax.numpy as jnp
        import numpy as np
        DIM = 256
        DEPTH = 2
        HEADS = 8
        DIM_HEAD = 64
        WINDOW = 128
        INNER = HEADS * DIM_HEAD
        HID = int(DIM * 4 * 2 / 3)
        B, N = (2, 2048)
        QK_SCALE = 8.0

        def shift_token(t):
            t1, t2 = jnp.split(t, 2, axis=-1)
            t2 = jnp.pad(t2, ((0, 0), (1, 0), (0, 0)))[:, :-1]
            return jnp.concatenate([t1, t2], axis=-1)

        def l2norm(t):
            return t / jnp.clip(jnp.linalg.norm(t, axis=-1, keepdims=True), 1e-12)

        def rotate_half(x):
            x1, x2 = jnp.split(x, 2, axis=-1)
            return jnp.concatenate([-x2, x1], axis=-1)

        def rotary_xpos(q, k):
            n = q.shape[-2]
            half_idx = jnp.arange(0, DIM_HEAD, 2, dtype=jnp.float32)
            inv_freq = 1.0 / 10000.0 ** (half_idx / DIM_HEAD)
            t = jnp.arange(n, dtype=jnp.float32)
            freqs = t[:, None] * inv_freq[None, :]
            freqs = jnp.concatenate([freqs, freqs], axis=-1)
            base = (half_idx + 0.4 * DIM_HEAD) / (1.4 * DIM_HEAD)
            power = (t - n // 2) / float(WINDOW // 2)
            scale = base[None, :] ** power[:, None]
            scale = jnp.concatenate([scale, scale], axis=-1)
            cos, sin = (jnp.cos(freqs), jnp.sin(freqs))
            q = q * cos * scale + rotate_half(q) * sin * scale
            k = k * cos / scale + rotate_half(k) * sin / scale
            return (q, k)

        def local_attention(q, k, v):
            b, h, n, d = q.shape
            w = n // WINDOW
            bq = q.reshape(b, h, w, WINDOW, d) * QK_SCALE
            bk = k.reshape(b, h, w, WINDOW, d)
            bv = v.reshape(b, h, w, WINDOW, d)

            def look_around(t):
                p = jnp.pad(t, ((0, 0), (0, 0), (1, 0), (0, 0), (0, 0)))
                return jnp.concatenate([p[:, :, :w], p[:, :, 1:]], axis=3)
            bk, bv = (look_around(bk), look_around(bv))
            bt = jnp.arange(n).reshape(w, WINDOW)
            btp = jnp.pad(bt, ((1, 0), (0, 0)), constant_values=-1)
            btk = jnp.concatenate([btp[:w], btp[1:]], axis=1)
            sim = jnp.einsum('bhwid,bhwjd->bhwij', bq, bk)
            i = bt[:, :, None]
            j = btk[:, None, :]
            mask = (i < j) | (i > j + WINDOW) | (j == -1)
            sim = jnp.where(mask, -jnp.finfo(sim.dtype).max, sim)
            attn = jax.nn.softmax(sim, axis=-1)
            out = jnp.einsum('bhwij,bhwjd->bhwid', attn, bv)
            return out.reshape(b, h, n, d)

        def _layer(x, wqkv, qs, ksc, wo, lg, lb, w1, b1, w2, b2):
            b, n, _ = x.shape
            h = shift_token(x)
            qkv = h @ wqkv
            q, k, v = jnp.split(qkv, 3, axis=-1)
            to_heads = lambda t: t.reshape(b, n, HEADS, DIM_HEAD).transpose(0, 2, 1, 3)
            q, k, v = (to_heads(q), to_heads(k), to_heads(v))
            q = l2norm(q) * qs
            k = l2norm(k) * ksc
            q, k = rotary_xpos(q, k)
            o = local_attention(q, k, v)
            o = o.transpose(0, 2, 1, 3).reshape(b, n, INNER)
            x = x + o @ wo
            h = shift_token(x)
            mu = h.mean(-1, keepdims=True)
            var = h.var(-1, keepdims=True)
            h = (h - mu) / jnp.sqrt(var + 1e-05) * lg + lb
            h = h @ w1 + b1
            a, g = jnp.split(h, 2, axis=-1)
            h = a * jax.nn.gelu(g, approximate=False)
            x = x + h @ w2 + b2
            return x
        key = jax.random.key(seed)
        ks = jax.random.split(key, 6)
        return {'x': jax.random.normal(ks[0], (B, N, DIM), jnp.float32), 'wqkv': jax.random.normal(ks[1], (DEPTH, DIM, 3 * INNER), jnp.float32) * 0.02, 'q_scale': jnp.ones((DEPTH, DIM_HEAD), jnp.float32), 'k_scale': jnp.ones((DEPTH, DIM_HEAD), jnp.float32), 'wo': jax.random.normal(ks[2], (DEPTH, INNER, DIM), jnp.float32) * 0.02, 'ln_g': jnp.ones((DEPTH, DIM), jnp.float32), 'ln_b': jnp.zeros((DEPTH, DIM), jnp.float32), 'w1': jax.random.normal(ks[3], (DEPTH, DIM, 2 * HID), jnp.float32) * 0.02, 'b1': jnp.zeros((DEPTH, 2 * HID), jnp.float32), 'w2': jax.random.normal(ks[4], (DEPTH, HID, DIM), jnp.float32) * 0.02, 'b2': jnp.zeros((DEPTH, DIM), jnp.float32)}
    _L1_ffn_in = _L1_ffn_setup()
    _d = {'L0_attn_x': _L0_attn_in['x'], 'L0_attn_q_w': _L0_attn_in['q_w'], 'L0_attn_k_w': _L0_attn_in['k_w'], 'L0_attn_v_w': _L0_attn_in['v_w'], 'L0_attn_Wq': _L0_attn_in['Wq'], 'L0_attn_Wk': _L0_attn_in['Wk'], 'L0_attn_g_w': _L0_attn_in['g_w'], 'L0_attn_g_b': _L0_attn_in['g_b'], 'L0_attn_base_decay_logits': _L0_attn_in['base_decay_logits'], 'L0_attn_out_w': _L0_attn_in['out_w'], 'L0_attn_out_b': _L0_attn_in['out_b'], 'L0_attn_ln_g': _L0_attn_in['ln_g'], 'L0_attn_ln_b': _L0_attn_in['ln_b'], 'L0_ffn_Win': _L0_ffn_in['Win'], 'L0_ffn_bin_': _L0_ffn_in['bin_'], 'L0_ffn_W1': _L0_ffn_in['W1'], 'L0_ffn_b1': _L0_ffn_in['b1'], 'L0_ffn_W2': _L0_ffn_in['W2'], 'L0_ffn_b2': _L0_ffn_in['b2'], 'L0_ffn_Wout': _L0_ffn_in['Wout'], 'L0_ffn_bout': _L0_ffn_in['bout'], 'L1_attn_Wq': _L1_attn_in['Wq'], 'L1_attn_Wk': _L1_attn_in['Wk'], 'L1_attn_Wv': _L1_attn_in['Wv'], 'L1_attn_Wo': _L1_attn_in['Wo'], 'L1_attn_bo': _L1_attn_in['bo'], 'L1_ffn_wqkv': _L1_ffn_in['wqkv'], 'L1_ffn_q_scale': _L1_ffn_in['q_scale'], 'L1_ffn_k_scale': _L1_ffn_in['k_scale'], 'L1_ffn_wo': _L1_ffn_in['wo'], 'L1_ffn_ln_g': _L1_ffn_in['ln_g'], 'L1_ffn_ln_b': _L1_ffn_in['ln_b'], 'L1_ffn_w1': _L1_ffn_in['w1'], 'L1_ffn_b1': _L1_ffn_in['b1'], 'L1_ffn_w2': _L1_ffn_in['w2'], 'L1_ffn_b2': _L1_ffn_in['b2']}
    _x0 = _d['L0_attn_x']
    _d['L0_attn_x'] = jax.random.normal(jax.random.fold_in(jax.random.key(seed), 1), (2, 2048, 256), dtype=_x0.dtype)
    del _x0
    return _d

def reference(L0_attn_x, L0_attn_q_w, L0_attn_k_w, L0_attn_v_w, L0_attn_Wq, L0_attn_Wk, L0_attn_g_w, L0_attn_g_b, L0_attn_base_decay_logits, L0_attn_out_w, L0_attn_out_b, L0_attn_ln_g, L0_attn_ln_b, L0_ffn_Win, L0_ffn_bin_, L0_ffn_W1, L0_ffn_b1, L0_ffn_W2, L0_ffn_b2, L0_ffn_Wout, L0_ffn_bout, L1_attn_Wq, L1_attn_Wk, L1_attn_Wv, L1_attn_Wo, L1_attn_bo, L1_ffn_wqkv, L1_ffn_q_scale, L1_ffn_k_scale, L1_ffn_wo, L1_ffn_ln_g, L1_ffn_ln_b, L1_ffn_w1, L1_ffn_b1, L1_ffn_w2, L1_ffn_b2):

    def _L0_attn_ref(x, q_w, k_w, v_w, Wq, Wk, g_w, g_b, base_decay_logits, out_w, out_b, ln_g, ln_b):
        import jax, jax.numpy as jnp
        import numpy as np
        B, T, HS, H, R = (4, 512, 256, 16, 16)
        D = HS // H
        LOGIT_01 = float(np.log(0.1 / 0.9))
        LOGIT_098 = float(np.log(0.98 / 0.02))

        def _rope_cos_sin(seq_len, dim, base=10000.0):
            half = dim // 2
            inv_freq = 1.0 / base ** (jnp.arange(half, dtype=jnp.float32) / half)
            freqs = jnp.arange(seq_len, dtype=jnp.float32)[:, None] * inv_freq[None, :]
            return (jnp.cos(freqs), jnp.sin(freqs))

        def _apply_rope(x, cos, sin):
            c = cos[None, :, None, :]
            s = sin[None, :, None, :]
            x1 = x[..., 0::2]
            x2 = x[..., 1::2]
            r1 = x1 * c - x2 * s
            r2 = x1 * s + x2 * c
            return jnp.stack((r1, r2), axis=-1).reshape(x.shape)
        b, t, hs = x.shape
        h, r, d = Wq.shape
        q = (x @ q_w.T).reshape(b, t, h, d)
        k = (x @ k_w.T).reshape(b, t, h, d)
        v = (x @ v_w.T).reshape(b, t, h, d)
        cos, sin = _rope_cos_sin(t, d)
        q = _apply_rope(q, cos, sin)
        k = _apply_rope(k, cos, sin)
        q_r = jnp.einsum('bthd,hrd->bthr', q, Wq)
        k_r = jnp.einsum('bthd,hrd->bthr', k, Wk)
        g = jax.nn.sigmoid((x @ g_w.T + g_b).reshape(b, t, h, r))
        decay = jax.nn.sigmoid(base_decay_logits)[None, :, :, None]
        scale = 1.0 / jnp.sqrt(jnp.asarray(d, dtype=x.dtype))

        def step(M, inp):
            q_t, k_t, v_t, g_t = inp
            M = M * decay + jnp.einsum('bhr,bhd->bhrd', g_t * k_t * scale, v_t)
            y = jnp.einsum('bhr,bhrd->bhd', q_t, M)
            return (M, y)
        xs = (q_r.transpose(1, 0, 2, 3), k_r.transpose(1, 0, 2, 3), v.transpose(1, 0, 2, 3), g.transpose(1, 0, 2, 3))
        M0 = jnp.zeros((b, h, r, d), dtype=x.dtype)
        _, Y = jax.lax.scan(step, M0, xs)
        Y = Y.transpose(1, 0, 2, 3).reshape(b, t, hs)
        out = Y @ out_w.T + out_b
        hres = x + out
        mu = jnp.mean(hres, axis=-1, keepdims=True)
        var = jnp.mean((hres - mu) ** 2, axis=-1, keepdims=True)
        return (hres - mu) / jnp.sqrt(var + 1e-05) * ln_g + ln_b

    def _L0_ffn_ref(x, Win, bin_, W1, b1, W2, b2, Wout, bout):
        import jax, jax.numpy as jnp
        import numpy as np
        D_MODEL = 256
        M = 64
        INNER = 16
        s = jnp.einsum('btd,dm->btm', x, Win) + bin_
        h = jax.nn.relu(s[..., None] * W1 + b1)
        g = jnp.einsum('btmh,mh->btm', h, W2) + b2
        out = jnp.einsum('btm,md->btd', g, Wout) + bout
        return out

    def _L1_attn_ref(x, Wq, Wk, Wv, Wo, bo):
        import jax, jax.numpy as jnp
        import numpy as np
        D_MODEL = 256
        NUM_HEADS = 16
        HEAD_DIM = D_MODEL // NUM_HEADS
        EPS = 1e-08
        B, T, _ = x.shape
        H, D = (NUM_HEADS, HEAD_DIM)
        scale = jnp.sqrt(jnp.asarray(D, dtype=x.dtype))
        q = (x @ Wq.T).reshape(B, T, H, D).transpose(0, 2, 1, 3)
        k = (x @ Wk.T).reshape(B, T, H, D).transpose(0, 2, 1, 3)
        v = (x @ Wv.T).reshape(B, T, H, D).transpose(0, 2, 1, 3)
        s = jnp.einsum('bhtd,bhsd->bhts', q, k) / scale
        m = jnp.max(s, axis=-1, keepdims=True)
        e = jnp.exp(s - m)
        num = jnp.einsum('bhts,bhsd->bhtd', e, v)
        den = jnp.sum(e, axis=-1, keepdims=True) + EPS
        out = (num / den).transpose(0, 2, 1, 3).reshape(B, T, H * D)
        return out @ Wo.T + bo

    def _L1_ffn_ref(x, wqkv, q_scale, k_scale, wo, ln_g, ln_b, w1, b1, w2, b2):
        import jax, jax.numpy as jnp
        import numpy as np
        DIM = 256
        DEPTH = 2
        HEADS = 8
        DIM_HEAD = 64
        WINDOW = 128
        INNER = HEADS * DIM_HEAD
        HID = int(DIM * 4 * 2 / 3)
        B, N = (2, 2048)
        QK_SCALE = 8.0

        def shift_token(t):
            t1, t2 = jnp.split(t, 2, axis=-1)
            t2 = jnp.pad(t2, ((0, 0), (1, 0), (0, 0)))[:, :-1]
            return jnp.concatenate([t1, t2], axis=-1)

        def l2norm(t):
            return t / jnp.clip(jnp.linalg.norm(t, axis=-1, keepdims=True), 1e-12)

        def rotate_half(x):
            x1, x2 = jnp.split(x, 2, axis=-1)
            return jnp.concatenate([-x2, x1], axis=-1)

        def rotary_xpos(q, k):
            n = q.shape[-2]
            half_idx = jnp.arange(0, DIM_HEAD, 2, dtype=jnp.float32)
            inv_freq = 1.0 / 10000.0 ** (half_idx / DIM_HEAD)
            t = jnp.arange(n, dtype=jnp.float32)
            freqs = t[:, None] * inv_freq[None, :]
            freqs = jnp.concatenate([freqs, freqs], axis=-1)
            base = (half_idx + 0.4 * DIM_HEAD) / (1.4 * DIM_HEAD)
            power = (t - n // 2) / float(WINDOW // 2)
            scale = base[None, :] ** power[:, None]
            scale = jnp.concatenate([scale, scale], axis=-1)
            cos, sin = (jnp.cos(freqs), jnp.sin(freqs))
            q = q * cos * scale + rotate_half(q) * sin * scale
            k = k * cos / scale + rotate_half(k) * sin / scale
            return (q, k)

        def local_attention(q, k, v):
            b, h, n, d = q.shape
            w = n // WINDOW
            bq = q.reshape(b, h, w, WINDOW, d) * QK_SCALE
            bk = k.reshape(b, h, w, WINDOW, d)
            bv = v.reshape(b, h, w, WINDOW, d)

            def look_around(t):
                p = jnp.pad(t, ((0, 0), (0, 0), (1, 0), (0, 0), (0, 0)))
                return jnp.concatenate([p[:, :, :w], p[:, :, 1:]], axis=3)
            bk, bv = (look_around(bk), look_around(bv))
            bt = jnp.arange(n).reshape(w, WINDOW)
            btp = jnp.pad(bt, ((1, 0), (0, 0)), constant_values=-1)
            btk = jnp.concatenate([btp[:w], btp[1:]], axis=1)
            sim = jnp.einsum('bhwid,bhwjd->bhwij', bq, bk)
            i = bt[:, :, None]
            j = btk[:, None, :]
            mask = (i < j) | (i > j + WINDOW) | (j == -1)
            sim = jnp.where(mask, -jnp.finfo(sim.dtype).max, sim)
            attn = jax.nn.softmax(sim, axis=-1)
            out = jnp.einsum('bhwij,bhwjd->bhwid', attn, bv)
            return out.reshape(b, h, n, d)

        def _layer(x, wqkv, qs, ksc, wo, lg, lb, w1, b1, w2, b2):
            b, n, _ = x.shape
            h = shift_token(x)
            qkv = h @ wqkv
            q, k, v = jnp.split(qkv, 3, axis=-1)
            to_heads = lambda t: t.reshape(b, n, HEADS, DIM_HEAD).transpose(0, 2, 1, 3)
            q, k, v = (to_heads(q), to_heads(k), to_heads(v))
            q = l2norm(q) * qs
            k = l2norm(k) * ksc
            q, k = rotary_xpos(q, k)
            o = local_attention(q, k, v)
            o = o.transpose(0, 2, 1, 3).reshape(b, n, INNER)
            x = x + o @ wo
            h = shift_token(x)
            mu = h.mean(-1, keepdims=True)
            var = h.var(-1, keepdims=True)
            h = (h - mu) / jnp.sqrt(var + 1e-05) * lg + lb
            h = h @ w1 + b1
            a, g = jnp.split(h, 2, axis=-1)
            h = a * jax.nn.gelu(g, approximate=False)
            x = x + h @ w2 + b2
            return x
        for l in range(DEPTH):
            x = _layer(x, wqkv[l], q_scale[l], k_scale[l], wo[l], ln_g[l], ln_b[l], w1[l], b1[l], w2[l], b2[l])
        return x
    x = L0_attn_x
    x = x + 0.5 * _L0_ffn_ref(_layernorm(x, axis=-1), L0_ffn_Win, L0_ffn_bin_, L0_ffn_W1, L0_ffn_b1, L0_ffn_W2, L0_ffn_b2, L0_ffn_Wout, L0_ffn_bout)
    x = x + _L0_attn_ref(_layernorm(x, axis=-1), L0_attn_q_w, L0_attn_k_w, L0_attn_v_w, L0_attn_Wq, L0_attn_Wk, L0_attn_g_w, L0_attn_g_b, L0_attn_base_decay_logits, L0_attn_out_w, L0_attn_out_b, L0_attn_ln_g, L0_attn_ln_b)
    x = x + 0.5 * _L0_ffn_ref(_layernorm(x, axis=-1), L0_ffn_Win, L0_ffn_bin_, L0_ffn_W1, L0_ffn_b1, L0_ffn_W2, L0_ffn_b2, L0_ffn_Wout, L0_ffn_bout)
    x = x + 0.5 * _L1_ffn_ref(_layernorm(x, axis=-1), L1_ffn_wqkv, L1_ffn_q_scale, L1_ffn_k_scale, L1_ffn_wo, L1_ffn_ln_g, L1_ffn_ln_b, L1_ffn_w1, L1_ffn_b1, L1_ffn_w2, L1_ffn_b2)
    x = x + _L1_attn_ref(_layernorm(x, axis=-1), L1_attn_Wq, L1_attn_Wk, L1_attn_Wv, L1_attn_Wo, L1_attn_bo)
    x = x + 0.5 * _L1_ffn_ref(_layernorm(x, axis=-1), L1_ffn_wqkv, L1_ffn_q_scale, L1_ffn_k_scale, L1_ffn_wo, L1_ffn_ln_g, L1_ffn_ln_b, L1_ffn_w1, L1_ffn_b1, L1_ffn_w2, L1_ffn_b2)
    return x

_drawn_inputs = setup_inputs


def setup_inputs(seed=0):
    import zlib

    import numpy as np

    out = dict(_drawn_inputs(seed))
    spreads = {'L0_attn_g_b': (-2.1972246170043945, 0.6),
     'L0_attn_base_decay_logits': (3.891820192337036, 0.6),
     'L0_attn_out_b': (0.0, 0.8),
     'L0_attn_ln_g': (1.0, 0.2),
     'L0_attn_ln_b': (0.0, 0.1),
     'L1_attn_bo': (0.0, 0.474),
     'L1_ffn_q_scale': (1.0, 0.6),
     'L1_ffn_k_scale': (1.0, 0.6),
     'L1_ffn_ln_g': (1.0, 0.6),
     'L1_ffn_ln_b': (0.0, 0.8),
     'L1_ffn_b1': (0.0, 0.8),
     'L1_ffn_b2': (0.0, 0.1)}
    factors = {'L0_attn_q_w': 8.0,
     'L0_attn_k_w': 8.0,
     'L0_attn_v_w': 8.0,
     'L0_attn_Wq': 8.0,
     'L0_attn_Wk': 8.0,
     'L0_attn_g_w': 8.0,
     'L0_attn_out_w': 8.0,
     'L0_ffn_bin_': 8.0,
     'L1_attn_Wq': 8.0,
     'L1_attn_Wk': 8.0,
     'L1_attn_Wv': 8.0,
     'L1_attn_Wo': 8.0,
     'L1_ffn_wqkv': 3.401,
     'L1_ffn_wo': 3.651,
     'L1_ffn_w1': 3.238,
     'L1_ffn_w2': 3.207}
    for name, (base, spread) in spreads.items():
        noise = np.random.default_rng([zlib.crc32(name.encode()), seed]).standard_normal(out[name].shape)
        drawn = base * np.exp(spread * noise) if base else spread * noise
        out[name] = jnp.asarray(drawn.astype(out[name].dtype))
    for name, factor in factors.items():
        out[name] = (out[name] * factor).astype(out[name].dtype)
    return out
```

```python
from contextlib import ExitStack

import numpy as np

import concourse.bass as bass
from concourse import mybir

ACT = mybir.ActivationFunctionType
ALU = mybir.AluOpType
AX_X = mybir.AxisListType.X
F32 = mybir.dt.float32
BF16 = mybir.dt.bfloat16

P = 128
B, T, D = 2, 2048, 256
NT = B * T // P
WT = T // P
KD = D // P
G = 4
GT = G * P
NG = NT // G
EPS = 1e-5


def ds(start, size):
    return bass.ds(start, size)


def pipeline(units, unroll, stages, depth=2):

    def program(eng):
        last_lag = max(lag for lag, _ in stages)
        first = -(-(last_lag + depth) // unroll) * unroll
        first = min(first, units)
        end = max(first, units // unroll * unroll)

        def peeled(n):
            for lag, stage in stages:
                if 0 <= n - lag < units:
                    stage(n - lag, (n - lag) % unroll)

        for n in range(first):
            peeled(n)
        if end > first:
            with eng.Fori(first // unroll, end // unroll) as i:
                for u in range(unroll):
                    for lag, stage in stages:
                        stage(i * unroll + (u - lag), (u - lag) % unroll)
        for n in range(end, units + last_lag):
            peeled(n)

    return program


def wait_reuse(eng, sem, unit, depth, per=1):
    if isinstance(unit, int) and unit < depth:
        return
    eng.wait_ge(sem, (unit - (depth - 1)) * per)


def wait_apart(eng, settled, *waits):
    if any(not isinstance(count, int) for _, count in waits):
        waits = [(sem, count if isinstance(count, int) else eng.to_reg(count)) for sem, count in waits]
        eng.wait_ge(*settled)
    for sem, count in waits:
        if not isinstance(count, int) or count > 0:
            eng.wait_ge(sem, count)


class Sems:

    phases = 0

    def __init__(self, nc):
        self.nc, self.made = nc, []
        Sems.phases += 1

    def __call__(self, name):
        s = self.nc.alloc_semaphore(f"{name}_{Sems.phases}")
        self.made.append(s)
        return s

    def close(self):
        self.nc.clear_and_free_semaphores(self.made)
        self.nc.all_engine_barrier()


class LnBuffers:

    def __init__(self, sb, name):
        self.parts = sb(f"{name}_ln_parts", [P, 2, G, 6])
        self.mean_var = sb(f"{name}_ln_mv", [P, 2, G, 2])
        self.var_eps = sb(f"{name}_ln_ve", [P, 2, G])
        self.rstd = sb(f"{name}_ln_rstd", [P, 2, G])


class LnSems:
    def __init__(self, S, name="ln"):
        self.parts, self.mean_var, self.var_eps, self.rstd = (
            S(f"{name}_{x}") for x in ("parts", "mean_var", "var_eps", "rstd"))


def ln_stats(nc, dve, b, s, x, n, p):
    for j in range(G):
        nc.vector.bn_stats(b.parts[:, p, j, :], x[:, ds(n * (G * D) + j * D, D)]).then_inc(s.parts, 1)
    wait_apart(dve, (s.parts, G), (s.parts, n * G + G))
    for j in range(G):
        nc.vector.bn_aggr(b.mean_var[:, p, j, :], b.parts[:, p, j, :]).then_inc(s.mean_var, 1)


def ln_scale(nc, pool, b, s, consts, n, p):
    pool.wait_ge(s.mean_var, n * G + G)
    nc.gpsimd.tensor_tensor(b.var_eps[:, p, :], b.mean_var[:, p, :, 1], consts[:, 1, 0:G], ALU.add).then_inc(s.var_eps, 1)
    pool.wait_ge(s.var_eps, n + 1)
    nc.gpsimd.tensor_tensor(b.rstd[:, p, :], b.var_eps[:, p, :], consts[:, 0, 0:G], ALU.pow).then_inc(s.rstd, 1)


def ln_apply(nc, dve, b, s, x, z, n, p, z_ready):
    dve.wait_ge(s.rstd, n + 1)
    for j in range(G):
        nc.vector.tensor_scalar(z[:, p, j, :], x[:, ds(n * (G * D) + j * D, D)], b.mean_var[:, p, j, 0:1],
                                b.rstd[:, p, j:j + 1], ALU.subtract, ALU.mult).then_inc(z_ready, 1)


def token_wise_kan(nc, x, ident, w, consts):
    NF = 64
    MT = 8
    with ExitStack() as c:
        sb = lambda name, shape, dt=F32: c.enter_context(nc.sbuf_tensor(f"ff{Sems.phases}_{name}", shape, dt))
        ps = lambda name, n: c.enter_context(nc.psum_tensor(f"ff{Sems.phases}_{name}", [P, n, 512], F32))
        win = sb("kan_win", [P, KD, P])
        wout = sb("kan_wout", [P, D])
        cols = sb("kan_cols", [P, 2 * MT + 2 + MT])
        b_in, g_bias = cols[:, 0:1], cols[:, 1:2]
        w1c, b1c, w2c = (cols[:, 2 + MT * i:2 + MT * (i + 1)] for i in range(3))
        w2m = sb("kan_w2m", [P, MT, 32])
        w2b = sb("kan_w2b", [P, MT, 32])
        sel_f = sb("kan_self", [P, MT, P])
        sel = sb("kan_sel", [P, MT, P], BF16)
        ln = LnBuffers(sb, "k")
        z = sb("kan_z", [P, 2, G, D])
        zT = sb("kan_zT", [P, 2, KD, GT])
        s32 = sb("kan_s32", [P, 2, GT])
        s_rest = sb("kan_srest", [P, 2, GT])
        s_top = sb("kan_stop", [P, 2, GT], BF16)
        s_mid = sb("kan_smid", [P, 2, GT], BF16)
        s_low = sb("kan_slow", [P, 2, GT], BF16)
        h = sb("kan_h", [P, 4, GT])
        g = sb("kan_g", [P, 2, GT])
        ps_t, ps_s, ps_b, ps_g, ps_o = ps("kan_pt", KD), ps("kan_ps", 1), ps("kan_pb", 2), ps("kan_pg", 1), ps("kan_po", 2)

        S = Sems(nc)
        loaded, sel_ready, w2_built = S("loaded"), S("sel_ready"), S("w2_built")
        stats = LnSems(S)
        z_ready, z_turned, zT_ready = S("z_ready"), S("z_turned"), S("zT_ready")
        s_done, s_ready, split_a, split_ready = S("s_done"), S("s_ready"), S("split_a"), S("split_ready")
        spread_done, relu_done, g_halves, g_ready = S("spread_done"), S("relu_done"), S("g_done"), S("g_ready")
        out_done, x_done = S("out_done"), S("x_done")
        with nc.Block() as block:

            @block.sync
            def _(sp):
                sp.dma_start(win[:, :, 0:NF], w["win"]).then_inc(loaded, 16)
                sp.dma_start(win[:, :, NF:P], w["win"]).then_inc(loaded, 16)
                sp.dma_start(cols[:, :], w["cols"]).then_inc(loaded, 16)
                sp.dma_start(sel_f[:, :, :], w["sel"]).then_inc(loaded, 16)
                sp.dma_start(w2m[:, :, :], w["w2_mask"]).then_inc(loaded, 16)
                sp.dma_start(wout[:, :], w["wout"]).then_inc(loaded, 16)

            @block.gpsimd
            def _(pool):
                pool.wait_ge(loaded, 96)
                nc.gpsimd.tensor_copy(sel[:, :, :], sel_f[:, :, :]).then_inc(sel_ready, 1)
                pipeline(NG, 2, [(0, lambda n, p: ln_scale(nc, pool, ln, stats, consts, n, p))])(pool)

            @block.vector
            def _(dve):
                dve.wait_ge(loaded, 96)
                for j in range(MT):
                    nc.vector.tensor_scalar(w2b[:, j, :], w2m[:, j, :], w2c[:, j:j + 1], None,
                                            ALU.mult).then_inc(w2_built, 1)

                def normalise(n, p):
                    wait_reuse(dve, z_turned, n, 2)
                    ln_apply(nc, dve, ln, stats, x, z, n, p, z_ready)

                def split(n, p):
                    dve.wait_ge(s_ready, n + 1)
                    wait_reuse(dve, spread_done, n, 2, MT)
                    nc.vector.tensor_copy(s_top[:, p, :], s32[:, p, :]).then_inc(split_a, 1)
                    dve.wait_ge(split_a, n * 3 + 1)
                    nc.vector.tensor_tensor(s_rest[:, p, :], s32[:, p, :], s_top[:, p, :],
                                            ALU.subtract).then_inc(split_a, 1)
                    dve.wait_ge(split_a, n * 3 + 2)
                    nc.vector.tensor_copy(s_mid[:, p, :], s_rest[:, p, :]).then_inc(split_a, 1)
                    dve.wait_ge(split_a, n * 3 + 3)
                    nc.vector.tensor_copy(s_top[NF:P, p, :], s_mid[NF:P, p, :]).then_inc(split_ready, 1)
                    nc.vector.tensor_tensor(s_low[0:NF, p, :], s_rest[0:NF, p, :], s_mid[0:NF, p, :],
                                            ALU.subtract).then_inc(split_ready, 1)

                def g_out(n, p):
                    dve.wait_ge(g_halves, n * 2 + 2)
                    wait_reuse(dve, out_done, n, 2, 2)
                    nc.vector.tensor_scalar(g[:, p, :], ps_g[:, 0, :], g_bias, None, ALU.add).then_inc(g_ready, 1)

                def residual(n, p):
                    for j in range(2):
                        dve.wait_ge(out_done, n * 2 + j + 1)
                        xs = x[:, ds(n * (G * D) + j * 2 * D, 2 * D)]
                        nc.vector.scalar_tensor_tensor(xs, ps_o[:, j, :], 0.5, xs, ALU.mult,
                                                       ALU.add).then_inc(x_done, 1)

                pipeline(NG, 2, [(4, residual), (1, normalise), (2, split),
                                 (0, lambda n, p: ln_stats(nc, dve, ln, stats, x, n, p)), (3, g_out)])(dve)

            @block.scalar
            def _(act):
                act.wait_ge(loaded, 96)

                def turned(n, p):
                    wait_reuse(act, s_done, n, 2)
                    act.wait_ge(z_turned, n + 1)
                    for k in range(KD):
                        nc.scalar.activation(zT[:, p, k, :], ps_t[:, k, :], ACT.Identity).then_inc(zT_ready, 1)

                def s_out(n, p):
                    act.wait_ge(s_done, n + 1)
                    wait_reuse(act, split_ready, n, 2, 2)
                    nc.scalar.activation(s32[:, p, :], ps_s[:, 0, :], ACT.Identity, bias=b_in).then_inc(s_ready, 1)

                def relus(n, p):
                    for j in range(MT):
                        act.wait_ge(spread_done, n * MT + j + 1)
                        if j >= 4:
                            act.wait_ge(g_halves, n * 2 + 1)
                        else:
                            wait_reuse(act, g_halves, n, 1, 2)
                        nc.scalar.activation(h[:, j % 4, :], ps_b[:, j % 2, :], ACT.Relu, bias=b1c[:, j:j + 1],
                                             scale=w1c[:, j:j + 1]).then_inc(relu_done, 1)

                pipeline(NG, 2, [(1, turned), (2, s_out), (3, relus)])(act)

            @block.tensor
            def _(pe):
                pe.wait_ge(loaded, 96)
                pe.wait_ge(sel_ready, 1)
                pe.wait_ge(w2_built, MT)

                def turn(n, p):
                    wait_reuse(pe, zT_ready, n, 1, KD)
                    pe.wait_ge(z_ready, n * G + G)
                    for j in range(G):
                        for k in range(KD):
                            last = nc.tensor.transpose(ps_t[:, k, j * P:(j + 1) * P],
                                                       z[:, p, j, k * P:(k + 1) * P], ident[:, :])
                    last.then_inc(z_turned, 1)

                def project(n, p):
                    wait_reuse(pe, s_ready, n, 1)
                    pe.wait_ge(zT_ready, n * KD + KD)
                    for k in range(KD):
                        last = nc.tensor.matmul(ps_s[:, 0, :], win[:, k, :], zT[:, p, k, :],
                                                start=(k == 0), stop=(k == KD - 1))
                    last.then_inc(s_done, 1)

                def hidden(n, p):
                    pe.wait_ge(split_ready, n * 2 + 2)
                    wait_reuse(pe, g_ready, n, 1)

                    def spread(j):
                        if j >= 2:
                            pe.wait_ge(relu_done, n * MT + j - 1)
                        else:
                            wait_reuse(pe, relu_done, n, 1, MT)
                        nc.tensor.matmul(ps_b[:, j % 2, :], sel[:, j, :], s_top[:, p, :], start=True, stop=False)
                        nc.tensor.matmul(ps_b[:, j % 2, :], sel[0:NF, j, :], s_low[0:NF, p, :],
                                         start=False, stop=True).then_inc(spread_done, 1)

                    def over_h(half):
                        pe.wait_ge(relu_done, n * MT + half * 4 + 4)
                        for q in range(4):
                            j = half * 4 + q
                            last = nc.tensor.matmul(ps_g[32 * q:32 * q + 32, 0, :], w2b[:, j, :], h[:, q, :],
                                                    start=(half == 0), stop=(half == 1))
                        last.then_inc(g_halves, 1)

                    for j in range(6):
                        spread(j)
                    over_h(0)
                    spread(6)
                    spread(7)
                    over_h(1)

                def outwards(n, p):
                    pe.wait_ge(g_ready, n + 1)
                    for j in range(G):
                        if j % 2 == 0:
                            wait_reuse(pe, x_done, n, 1, 2)
                        last = nc.tensor.matmul(ps_o[:, j // 2, (j % 2) * D:(j % 2 + 1) * D],
                                                g[:, p, j * P:(j + 1) * P], wout[:, :], start=True, stop=True)
                        if j % 2 == 1:
                            last.then_inc(out_done, 1)

                pipeline(NG, 2, [(4, outwards), (1, turn), (2, project), (3, hidden)])(pe)

        S.close()


def decay_memory(nc, x, ident, consts, w):
    H, R, DH = 16, 16, 16
    HH = 8
    with ExitStack() as c:
        sb = lambda name, shape, dt=F32: c.enter_context(nc.sbuf_tensor("mem_" + name, shape, dt))
        q_r = sb("q_r", [P, 2 * B * T])
        k_g = sb("k_g", [P, 2 * B * T])
        v_p = [sb(f"v{i}", [P, 2 * B * T], BF16) for i in range(3)]
        decay = sb("decay", [P, 2 * B])

        with ExitStack() as c2:
            sb2 = lambda name, shape, dt=F32: c2.enter_context(nc.sbuf_tensor("mem_" + name, shape, dt))
            ps = lambda name, n: c2.enter_context(nc.psum_tensor("mem_" + name, [P, n, 512], F32))
            wp = sb2("wp", [P, KD, 4, D])
            rank = sb2("rank", [P, 8, P])
            cols = sb2("cols", [P, 2 + 2 * B])
            rope = sb2("rope", [P, 2, GT])
            ln = LnBuffers(sb2, "mem")
            z = sb2("z", [P, 2, G, D])
            zT = sb2("zT", [P, 2, KD, GT])
            qc = sb2("qc", [P, 4, 2, GT])
            gate = sb2("gate", [P, 2, GT])
            v32 = sb2("v32", [P, 2, GT])
            v_rest = sb2("v_rest", [P, 2, GT])
            ps_t, ps_q, ps_r, ps_v, = ps("pt", KD), ps("pq", 2), ps("pr", 2), ps("pv", 2)
            S = Sems(nc)
            loaded, rope_in, decay_a = S("loaded"), S("rope_in"), S("decay_a")
            stats = LnSems(S)
            z_ready, z_turned, zT_ready = S("z_ready"), S("z_turned"), S("zT_ready")
            qk_done, roped, rank_done, rank_out = S("qk_done"), S("roped"), S("rank_done"), S("rank_out")
            gv_done, gate_ready, v_copied, v_split = S("gv_done"), S("gate_ready"), S("v_copied"), S("v_split")
            with nc.Block() as block:

                @block.sync
                def _(sp):
                    sp.dma_start(wp[:, :, :, :], w["proj"]).then_inc(loaded, 16)
                    sp.dma_start(rank[:, :, :], w["rank"]).then_inc(loaded, 16)
                    sp.dma_start(cols[:, :], w["cols"]).then_inc(loaded, 16)

                    def load_rope(n, p):
                        wait_reuse(sp, roped, n, 1, 8)
                        at = n % (NG // B)
                        sp.dma_start(rope[:, :, :], w["rope"][:, :, ds(at * GT, GT)]).then_inc(rope_in, 16)

                    for n in range(NG):
                        load_rope(n, n % 2)

                @block.gpsimd
                def _(pool):
                    pipeline(NG, 2, [(0, lambda n, p: ln_scale(nc, pool, ln, stats, consts, n, p))])(pool)

                @block.scalar
                def _(act):
                    act.wait_ge(loaded, 48)
                    nc.scalar.activation(decay[:, :], cols[:, 2:2 + 2 * B], ACT.Sigmoid).then_inc(decay_a, 1)

                    def turned(n, p):
                        wait_reuse(act, gv_done, n, 2, 4)
                        act.wait_ge(z_turned, n + 1)
                        for k in range(KD):
                            nc.scalar.activation(zT[:, p, k, :], ps_t[:, k, :], ACT.Identity).then_inc(zT_ready, 1)

                    def gates(n, p):
                        for hf in range(2):
                            act.wait_ge(gv_done, n * 4 + hf + 1)
                            wait_reuse(act, rank_out, n, 1, 4)
                            nc.scalar.activation(gate[:, hf, :], ps_v[:, hf, :], ACT.Sigmoid,
                                                 bias=cols[:, hf:hf + 1]).then_inc(gate_ready, 1)
                        for hf in range(2):
                            act.wait_ge(gv_done, n * 4 + hf + 3)
                            wait_reuse(act, v_split, n, 1, 10)
                            nc.scalar.activation(v32[:, hf, :], ps_v[:, hf, :], ACT.Identity).then_inc(v_copied, 1)

                    pipeline(NG, 2, [(1, turned), (2, gates)])(act)

                @block.vector
                def _(dve):
                    dve.wait_ge(loaded, 48)

                    def normalise(n, p):
                        wait_reuse(dve, z_turned, n, 2)
                        ln_apply(nc, dve, ln, stats, x, z, n, p, z_ready)

                    def turn_qk(n, p):
                        dve.wait_ge(rope_in, n * 16 + 16)
                        for m in range(4):
                            dve.wait_ge(qk_done, n * 4 + m + 1)
                            wait_reuse(dve, rank_done, n, 1, 4)
                            for cs in range(2):
                                nc.vector.tensor_tensor(qc[:, m, cs, :], ps_q[:, m % 2, :], rope[:, cs, :],
                                                        ALU.mult).then_inc(roped, 1)

                    def ranks(n, p):
                        for m in range(4):
                            hf, tok = m % 2, ds(n * GT, GT)
                            wait_apart(dve, (loaded, 48), (rank_done, n * 4 + m + 1))
                            if m < 2:
                                nc.vector.tensor_copy(q_r[:, ds(n * GT + hf * B * T, GT)], ps_r[:, m % 2, :]).then_inc(rank_out, 1)
                            else:
                                dve.wait_ge(gate_ready, n * 2 + 2)
                                nc.vector.scalar_tensor_tensor(k_g[:, ds(n * GT + hf * B * T, GT)], ps_r[:, m % 2, :],
                                                               DH ** -0.5, gate[:, hf, :], ALU.mult,
                                                               ALU.mult).then_inc(rank_out, 1)

                    def split_v(n, p):
                        for hf in range(2):
                            tok = lambda i: v_p[i][:, ds(n * GT + hf * B * T, GT)]
                            base = n * 10 + hf * 5
                            wait_apart(dve, (loaded, 48), (v_copied, n * 2 + hf + 1))
                            nc.vector.tensor_copy(tok(0), v32[:, hf, :]).then_inc(v_split, 1)
                            dve.wait_ge(v_split, base + 1)
                            nc.vector.tensor_tensor(v_rest[:, hf, :], v32[:, hf, :], tok(0), ALU.subtract).then_inc(v_split, 1)
                            wait_apart(dve, (loaded, 48), (v_split, base + 2))
                            nc.vector.tensor_copy(tok(1), v_rest[:, hf, :]).then_inc(v_split, 1)
                            dve.wait_ge(v_split, base + 3)
                            nc.vector.tensor_tensor(tok(2), v_rest[:, hf, :], tok(1), ALU.subtract).then_inc(v_split, 2)

                    pipeline(NG, 2, [(1, normalise), (0, lambda n, p: ln_stats(nc, dve, ln, stats, x, n, p)),
                                     (2, turn_qk), (2, ranks), (2, split_v)])(dve)

                @block.tensor
                def _(pe):
                    pe.wait_ge(loaded, 48)

                    def turn(n, p):
                        wait_reuse(pe, zT_ready, n, 1, KD)
                        pe.wait_ge(z_ready, n * G + G)
                        turn_group(nc, ps_t, z, ident, p).then_inc(z_turned, 1)

                    def products(n, p):
                        pe.wait_ge(zT_ready, n * KD + KD)

                        def proj(out, which, hf):
                            for k in range(KD):
                                last = nc.tensor.matmul(out, wp[:, k, which, hf * P:(hf + 1) * P], zT[:, p, k, :],
                                                        start=(k == 0), stop=(k == KD - 1))
                            return last

                        def qk(m):
                            if m >= 2:
                                pe.wait_ge(roped, n * 8 + 2 * (m - 1))
                            else:
                                wait_reuse(pe, roped, n, 1, 8)
                            proj(ps_q[:, m % 2, :], m // 2, m % 2).then_inc(qk_done, 1)

                        def to_ranks(m):
                            pe.wait_ge(roped, n * 8 + 2 * (m + 1))
                            if m >= 2:
                                pe.wait_ge(rank_out, n * 4 + m - 1)
                            else:
                                wait_reuse(pe, rank_out, n, 1, 4)
                            for cs in range(2):
                                last = nc.tensor.matmul(ps_r[:, m % 2, :], rank[:, m + 4 * cs, :], qc[:, m, cs, :],
                                                        start=(cs == 0), stop=(cs == 1))
                            last.then_inc(rank_done, 1)

                        qk(0)
                        qk(1)
                        for hf in range(2):
                            wait_reuse(pe, v_copied, n, 1, 2)
                            proj(ps_v[:, hf, :], 3, hf).then_inc(gv_done, 1)
                        qk(2)
                        to_ranks(0)
                        qk(3)
                        to_ranks(1)
                        for hf in range(2):
                            pe.wait_ge(gate_ready, n * 2 + hf + 1)
                            proj(ps_v[:, hf, :], 2, hf).then_inc(gv_done, 1)
                        to_ranks(2)
                        to_ranks(3)

                    pipeline(NG, 2, [(1, turn), (2, products)])(pe)

            S.close()
        memory_scan(nc, q_r, k_g, v_p, decay, w)
        memory_out(nc, x, ident, consts, k_g, w)


def turn_group(nc, ps_t, z, ident, p):
    for j in range(G):
        for k in range(KD):
            last = nc.tensor.transpose(ps_t[:, k, j * P:(j + 1) * P], z[:, p, j, k * P:(k + 1) * P], ident[:, :])
    return last


def memory_scan(nc, q_r, k_g, v_p, decay, w):
    NC = T // GT
    UN = 4 * NC
    with ExitStack() as c:
        sb = lambda name, shape, dt=F32: c.enter_context(nc.sbuf_tensor("scan_" + name, shape, dt))
        ps = lambda name, n: c.enter_context(nc.psum_tensor("scan_" + name, [P, n, 512], F32))
        sel_f = sb("self", [P, 16, P])
        sel = sb("sel", [P, 16, P], BF16)
        red = sb("red", [P, 4, 32])
        kv = sb("kv", [P, 2, GT])
        mem = sb("mem", [P, 8, GT])
        qm = sb("qm", [P, 8, GT])
        ps_v, ps_y = ps("pv", 4), ps("py", NC)
        S = Sems(nc)
        loaded, sel_ready, spread, kv_done, scanned, qm_done, summed, y_done = (
            S(x) for x in ("loaded", "sel_ready", "spread", "kv_done", "scanned", "qm_done", "summed", "y_done"))
        with nc.Block() as block:

            @block.sync
            def _(sp):
                sp.dma_start(sel_f[:, :, :], w["spread"]).then_inc(loaded, 16)
                sp.dma_start(red[:, :, :], w["sum_r"]).then_inc(loaded, 16)

            @block.gpsimd
            def _(pool):
                pool.wait_ge(loaded, 32)
                nc.gpsimd.tensor_copy(sel[:, :, :], sel_f[:, :, :]).then_inc(sel_ready, 1)
                with pool.Fori(0, 2 * B) as i:
                    for u in range(4 * UN):
                        cc, dd = u // 4 % NC, u % 4
                        if u >= 8:
                            pool.wait_ge(summed, i * UN + (u - 8) // 4 + 1)
                        wait_apart(pool, (loaded, 32), (scanned, i * (4 * UN) + u + 1))
                        nc.gpsimd.tensor_tensor(qm[:, u % 8, :], mem[:, u % 8, :], q_r[:, ds(i * T + cc * GT, GT)],
                                                ALU.mult).then_inc(qm_done, 1)
                    pool.wait_ge(summed, i * UN + UN)

            @block.vector
            def _(dve):
                with dve.Fori(0, 2 * B) as i:
                    for u in range(4 * UN):
                        cc, dd = u // 4 % NC, u % 4
                        dve.wait_ge(spread, i * (4 * UN) + u + 1)
                        nc.vector.tensor_tensor(kv[:, u % 2, :], ps_v[:, u % 4, :],
                                                k_g[:, ds(i * T + cc * GT, GT)], ALU.mult).then_inc(kv_done, 1)
                        dve.wait_ge(kv_done, i * (4 * UN) + u + 1)
                        if u >= 8:
                            dve.wait_ge(qm_done, i * (4 * UN) + u - 7)
                        start = 0.0 if cc == 0 else mem[:, (u - 4) % 8, GT - 1:GT]
                        if cc:
                            dve.wait_ge(scanned, i * (4 * UN) + u - 3)
                        nc.vector.tensor_tensor_scan(mem[:, u % 8, :], decay[:, ds(i, 1)].to_broadcast([P, GT]), kv[:, u % 2, :], start, ALU.mult,
                                                     ALU.add).then_inc(scanned, 1)
                    for cc in range(NC):
                        wait_apart(dve, (loaded, 32), (summed, i * UN + UN))
                        nc.vector.tensor_copy(k_g[:, ds(i * T + cc * GT, GT)], ps_y[:, cc, :]).then_inc(y_done, 1)

            @block.tensor
            def _(pe):
                pe.wait_ge(loaded, 32)
                pe.wait_ge(sel_ready, 1)
                with pe.Fori(0, 2 * B) as i:
                    def spread_v(u):
                        cc, d = u // 4 % NC, u // UN * 4 + u % 4
                        if u >= 4:
                            pe.wait_ge(kv_done, i * (4 * UN) + u - 3)
                        for part in range(3):
                            last = nc.tensor.matmul(ps_v[:, u % 4, :], sel[:, d, :],
                                                    v_p[part][:, ds(i * T + cc * GT, GT)],
                                                    start=(part == 0), stop=(part == 2))
                        last.then_inc(spread, 1)

                    def sum_r(n):
                        cc, dg = n % NC, n // NC
                        pe.wait_ge(qm_done, i * (4 * UN) + n * 4 + 4)
                        for dd in range(4):
                            last = nc.tensor.matmul(ps_y[32 * dd:32 * dd + 32, cc, :], red[:, dg, :],
                                                    qm[:, (n * 4 + dd) % 8, :], start=(dg == 0), stop=(dg == 3))
                        last.then_inc(summed, 1)

                    for u in range(4 * UN):
                        spread_v(u)
                        if u % 4 == 3 and u >= 7:
                            sum_r(u // 4 - 1)
                    sum_r(UN - 1)
                    pe.wait_ge(y_done, i * NC + NC)

        S.close()


def memory_out(nc, x, ident, consts, y, w):
    with ExitStack() as c:
        sb = lambda name, shape, dt=F32: c.enter_context(nc.sbuf_tensor("mo_" + name, shape, dt))
        w_out = sb("w_out", [P, 2, D])
        bc = sb("bc", [P, 3, D])
        y2 = sb("y2", [P, 2, 2, P])
        ln1, ln2 = TileLn(sb, "mo1"), TileLn(sb, "mo2")
        zb = sb("zb", [P, 2, D])
        hres = sb("hres", [P, 2, D])
        t1 = sb("t1", [P, 2, D])
        t2 = sb("t2", [P, 2, D])
        ps_o = [c.enter_context(nc.psum_tensor(f"mo_po{i}", [P, 512], F32)) for i in range(2)]
        S = Sems(nc)
        loaded, y_copied, out_done, z_done, zb_done, h_done, d1, d2, x_done = (
            S(s) for s in ("loaded", "y_copied", "out_done", "z_done", "zb_done", "h_done", "d1", "d2", "x_done"))
        s1, s2 = LnSems(S, "ln1"), LnSems(S, "ln2")
        with nc.Block() as block:

            @block.sync
            def _(sp):
                sp.dma_start(w_out[:, :, :], w["out_w"]).then_inc(loaded, 16)
                for i, name in enumerate(("out_b", "ln_g", "ln_b")):
                    sp.dma_start(bc[:, i, :], w[name].to_broadcast([P, D])).then_inc(loaded, 16)

            @block.gpsimd
            def _(pool):
                pipeline(NT, 2, [(0, lambda n, p: tile_scale(nc, pool, ln1, s1, consts, n, p)),
                                 (2, lambda n, p: tile_scale(nc, pool, ln2, s2, consts, n, p))])(pool)

            @block.scalar
            def _(act):
                def copy_y(n, p):
                    wait_reuse(act, out_done, n, 2)
                    for hf in range(2):
                        nc.scalar.activation(y2[:, p, hf, :], y[:, ds(n * P + hf * B * T, P)],
                                             ACT.Identity).then_inc(y_copied, 1)

                pipeline(NT, 2, [(0, copy_y)])(act)

            @block.tensor
            def _(pe):
                pe.wait_ge(loaded, 64)

                def out(n, p):
                    pe.wait_ge(y_copied, n * 2 + 2)
                    wait_reuse(pe, h_done, n, 2)
                    for hf in range(2):
                        last = nc.tensor.matmul(ps_o[p][:, 0:D], y2[:, p, hf, :], w_out[:, hf, :],
                                                start=(hf == 0), stop=(hf == 1))
                    last.then_inc(out_done, 1)

                pipeline(NT, 2, [(0, out)])(pe)

            @block.vector
            def _(dve):
                dve.wait_ge(loaded, 64)

                def stats1(n, p):
                    tile_stats(nc, dve, ln1, s1, x[:, ds(n * D, D)], n, p)

                def add_out(n, p):
                    xs = x[:, ds(n * D, D)]
                    dve.wait_ge(s1.rstd, n + 1)
                    nc.vector.tensor_scalar(zb[:, p, :], xs, ln1.mean_var[:, p, 0:1], ln1.rstd[:, p:p + 1],
                                            ALU.subtract, ALU.mult).then_inc(z_done, 1)
                    dve.wait_ge(z_done, n + 1)
                    nc.vector.tensor_tensor(t1[:, p, :], zb[:, p, :], bc[:, 0, :], ALU.add).then_inc(zb_done, 1)
                    dve.wait_ge(zb_done, n + 1)
                    dve.wait_ge(out_done, n + 1)
                    nc.vector.tensor_tensor(hres[:, p, :], ps_o[p][:, 0:D], t1[:, p, :], ALU.add).then_inc(h_done, 1)
                    dve.wait_ge(h_done, n + 1)
                    tile_stats(nc, dve, ln2, s2, hres[:, p, :], n, p)

                def add_ln(n, p):
                    xs = x[:, ds(n * D, D)]
                    dve.wait_ge(s2.rstd, n + 1)
                    nc.vector.scalar_tensor_tensor(zb[:, p, :], hres[:, p, :], ln2.mean_var[:, p, 0:1], bc[:, 1, :],
                                                   ALU.subtract, ALU.mult).then_inc(d1, 1)
                    dve.wait_ge(d1, n + 1)
                    nc.vector.scalar_tensor_tensor(t2[:, p, :], zb[:, p, :], ln2.rstd[:, p:p + 1], bc[:, 2, :],
                                                   ALU.mult, ALU.add).then_inc(d2, 1)
                    dve.wait_ge(d2, n + 1)
                    nc.vector.tensor_tensor(xs, xs, t2[:, p, :], ALU.add).then_inc(x_done, 1)

                pipeline(NT, 2, [(0, stats1), (1, add_out), (2, add_ln)])(dve)

        S.close()


class TileLn:

    def __init__(self, sb, name):
        self.parts = sb(f"{name}_parts", [P, 2, 6])
        self.mean_var = sb(f"{name}_mv", [P, 2, 2])
        self.var_eps = sb(f"{name}_ve", [P, 2])
        self.rstd = sb(f"{name}_rstd", [P, 2])


def tile_stats(nc, dve, b, s, src, n, p):
    nc.vector.bn_stats(b.parts[:, p, :], src).then_inc(s.parts, 1)
    wait_apart(dve, (s.parts, 1), (s.parts, n + 1))
    nc.vector.bn_aggr(b.mean_var[:, p, :], b.parts[:, p, :]).then_inc(s.mean_var, 1)


def tile_scale(nc, pool, b, s, consts, n, p):
    pool.wait_ge(s.mean_var, n + 1)
    nc.gpsimd.tensor_tensor(b.var_eps[:, p:p + 1], b.mean_var[:, p, 1:2], consts[:, 1, 0:1],
                            ALU.add).then_inc(s.var_eps, 1)
    pool.wait_ge(s.var_eps, n + 1)
    nc.gpsimd.tensor_tensor(b.rstd[:, p:p + 1], b.var_eps[:, p:p + 1], consts[:, 0, 0:1],
                            ALU.pow).then_inc(s.rstd, 1)


HL, DL = 8, 64
SLOTS = WT + 1


def at_inner(n, u):
    return n * (D // 2) + (u % 2) * (SLOTS * D - D // 2) + D


def local_transformer(nc, x, ident, consts, w):
    with ExitStack() as c:
        inner = c.enter_context(nc.sbuf_tensor(f"inner_{Sems.phases}", [P, B * SLOTS * D], F32))
        enter_inner(nc, x, inner, consts)
        for layer in range(2):
            window_attention(nc, inner, ident, consts, w, layer)
            gated_mlp(nc, inner, ident, consts, w, layer)
        S = Sems(nc)
        added = S("added")
        with nc.Block() as block:

            @block.vector
            def _(dve):
                for b in range(B):
                    for q in range(4):
                        xs = x[:, (b * 4 + q) * G * D:(b * 4 + q + 1) * G * D]
                        at = (b * SLOTS + 1 + q * G) * D
                        nc.vector.scalar_tensor_tensor(xs, inner[:, at:at + G * D], 0.5, xs, ALU.mult,
                                                       ALU.add).then_inc(added, 1)

        S.close()


def enter_inner(nc, x, inner, consts):
    with ExitStack() as c:
        ln = LnBuffers(lambda name, shape: c.enter_context(nc.sbuf_tensor(name, shape, F32)), f"in{Sems.phases}")
        S = Sems(nc)
        s = LnSems(S)
        z_done = S("z_done")
        with nc.Block() as block:

            @block.gpsimd
            def _(pool):
                for b in range(B):
                    nc.gpsimd.memset(inner[:, b * SLOTS * D:(b * SLOTS + 1) * D], 0.0)
                pipeline(NG, 2, [(0, lambda n, p: ln_scale(nc, pool, ln, s, consts, n, p))])(pool)

            @block.vector
            def _(dve):
                def apply(n, p):
                    dve.wait_ge(s.rstd, n + 1)
                    for j in range(G):
                        at = (n * G + j + 1 + n // (NG // B)) * D
                        nc.vector.tensor_scalar(inner[:, at:at + D], x[:, ds(n * (G * D) + j * D, D)],
                                                ln.mean_var[:, p, j, 0:1], ln.rstd[:, p, j:j + 1],
                                                ALU.subtract, ALU.mult).then_inc(z_done, 1)

                for n in range(NG + 1):
                    if n < NG:
                        ln_stats(nc, dve, ln, s, x, n, n % 2)
                    if n:
                        apply(n - 1, (n - 1) % 2)

        S.close()


def bank_free(pe, users, i, unit, units):
    for back in range(1, len(users) + 1):
        k = (i - back) % len(users)
        sem, per, nth, lag = users[k]
        other = unit + (users[i][3] - lag) - (1 if back > i else 0)
        if isinstance(unit, int):
            other = min(other, units - 1)
            if other >= 0:
                pe.wait_ge(sem, other * per + nth)
        else:
            pe.wait_ge(sem, other * per + nth)
            return


def window_attention(nc, inner, ident, consts, w, layer):
    L_TURN, L_PROJ, L_QK, L_ATT, L_OUT, L_WO = 0, 1, 2, 3, 4, 5
    tag = f"wa{Sems.phases}_"
    IN = HL * DL
    with ExitStack() as c:
        sb = lambda name, shape, dt=F32: c.enter_context(nc.sbuf_tensor(tag + name, shape, dt))
        wqkv = sb("wqkv", [P, KD, 3 * IN])
        wo = sb("wo", [P, 4, D])
        table = sb("table", [P, WT, 2, 2 * DL])
        scales = sb("scales", [P, 2, 2 * DL])
        mask = sb("mask", [P, 3, 2 * P])
        h = sb("h", [P, 2, D])
        hT = sb("hT", [P, 4, KD, P + 4])
        squares = sb("squares", [P, 2, IN])
        ss = sb("ss", [P, 2, 16])
        ssm = sb("ssm", [P, 2, 16])
        rn = sb("rn", [P, 2, 16])
        by_cos = sb("by_cos", [P, 2, IN])
        by_sin = sb("by_sin", [P, 2, IN])
        turned = sb("turned", [P, 2, IN])
        qk = sb("qk", [P, 2, 2, IN])
        v_new = sb("v_new", [P, 2, IN])
        v = sb("v", [P, 4, IN])
        qT = sb("qT", [P, 2, 4, P])
        kT = sb("kT", [P, 2, HL, 2, P])
        sm = sb("sm", [P, 4, 2 * P])
        mx = sb("mx", [P, 2, HL])
        nmx = sb("nmx", [P, 2, HL])
        sums = sb("sums", [P, 2, HL])
        rsum = sb("rsum", [P, 2, HL])
        pr = sb("pr", [P, 4, 2 * P])
        pT = sb("pT", [P, 2, 4, P])
        o = sb("o", [P, 2, IN])
        oT = sb("oT", [P, 2, 4, P])
        bank = [c.enter_context(nc.psum_tensor(f"{tag}bank{i}", [P, 512], F32)) for i in range(3)]
        ps_qk = c.enter_context(nc.psum_tensor(f"{tag}ps_qk", [P, 2, 512], F32))
        ps_vo = c.enter_context(nc.psum_tensor(f"{tag}ps_vo", [P, 512], F32))
        ps_s = [c.enter_context(nc.psum_tensor(f"{tag}ps_s{i}", [P, 2, 256], F32)) for i in range(2)]

        S = Sems(nc)
        loaded, cleared, table_done = S("loaded"), S("cleared"), S("table_done")
        h_ready, h_turned, hT_ready = S("h_ready"), S("h_turned"), S("hT_ready")
        q_done, k_done, v_done, v_copied, v_ready = S("q_done"), S("k_done"), S("v_done"), S("v_copied"), S("v_ready")
        squared, ss_done, ss_max, rn_ready = S("squared"), S("ss_done"), S("ss_max"), S("rn_ready")
        cos_done, sin_done, sum_done, qk_ready = S("cos_done"), S("sin_done"), S("sum_done"), S("qk_ready")
        q_turned, k_turned, qT_ready, kT_ready = S("q_turned"), S("k_turned"), S("qT_ready"), S("kT_ready")
        s_done, max_done, nmx_ready, p_ready = S("s_done"), S("max_done"), S("nmx_ready"), S("p_ready")
        p_turned, pT_even, pT_odd, pv_done = S("p_turned"), S("pT_even"), S("pT_odd"), S("pv_done")
        rsum_ready, o_ready, o_turned, oT_ready = S("rsum_ready"), S("o_ready"), S("o_turned"), S("oT_ready")
        wo_done, inner_done = S("wo_done"), S("inner_done")
        T = [(pT_even, 2, 1, L_ATT), (pT_odd, 2, 1, L_ATT), (pT_even, 2, 2, L_ATT), (pT_odd, 2, 2, L_ATT)]
        users = [[T[0], T[2], (qT_ready, 1, 1, L_QK)], [T[1], (inner_done, 1, 1, L_WO), (kT_ready, 2, 2, L_QK)],
                 [(hT_ready, 3, 3, L_TURN), T[3], (oT_ready, 1, 1, L_OUT)]]
        free = lambda pe, b, i, n: bank_free(pe, users[b], i, n, NT)

        with nc.Block() as block:

            @block.sync
            def _(sp):
                for dst, src in ((wqkv[:, :, :], w["wqkv"][layer]), (wo[:, :, :], w["wo"][layer]),
                                 (table[:, :, :, :], w["table"]), (mask[:, :, :], w["mask"]),
                                 (scales[:, :, :], w["scales"][layer].to_broadcast([P, 2, 2 * DL]))):
                    sp.dma_start(dst, src).then_inc(loaded, 16)

            @block.gpsimd
            def _(pool):
                nc.gpsimd.memset(kT[:, :, :, :, :], 0.0).then_inc(cleared, 1)
                nc.gpsimd.memset(v[:, :, :], 0.0).then_inc(cleared, 1)
                nc.gpsimd.memset(hT[:, :, :, :], 0.0).then_inc(cleared, 1)
                pool.wait_ge(cleared, 3)

                def copy_h(n, u):
                    wait_reuse(pool, h_turned, n, 2)
                    nc.gpsimd.tensor_copy(h[:, u % 2, :], inner[:, ds(at_inner(n, u), D)]).then_inc(h_ready, 1)

                def norms(n, u):
                    wait_apart(pool, (cleared, 3), (ss_done, n + 1), (qk_ready, n - 1))
                    nc.gpsimd.tensor_scalar(ssm[:, u % 2, :], ss[:, u % 2, :], 1e-24, None,
                                            ALU.max).then_inc(ss_max, 1)
                    pool.wait_ge(ss_max, n + 1)
                    nc.gpsimd.tensor_tensor(rn[:, u % 2, :], ssm[:, u % 2, :], consts[:, 0, :],
                                            ALU.pow).then_inc(rn_ready, 1)

                def add_turned(n, u):
                    pool.wait_ge(sin_done, n * 2 + 2)
                    wait_reuse(pool, qk_ready, n, 1)
                    nc.gpsimd.tensor_tensor(turned[:, :, :], by_cos[:, :, :], by_sin[:, :, :],
                                            ALU.add).then_inc(sum_done, 1)

                def place_v(n, u):
                    wait_apart(pool, (cleared, 3), (v_copied, n + 1), (pv_done, (n - 1) * 4))
                    nc.gpsimd.tensor_copy(v[:, u, :], v_new[:, u % 2, :]).then_inc(v_ready, 1)

                pipeline(NT, 4, [(L_TURN, copy_h), (L_QK, place_v), (L_PROJ, norms), (L_PROJ, add_turned)], 4)(pool)

            @block.scalar
            def _(act):
                act.wait_ge(cleared, 3)

                def turned_h(n, u):
                    wait_reuse(act, k_done, n, 2)
                    act.wait_ge(h_turned, n + 1)
                    nc.scalar.activation(hT[:, u, 0, 0:P], bank[2][:, 0:P], ACT.Identity).then_inc(hT_ready, 1)
                    nc.scalar.activation(hT[:, u, 1, 1:P + 1], bank[2][:, P:2 * P], ACT.Identity).then_inc(hT_ready, 1)
                    nc.scalar.activation(hT[:, (u + 2) % 4, 1, 0:1], bank[2][:, 2 * P - 1:2 * P],
                                         ACT.Identity).then_inc(hT_ready, 1)

                def copy_v(n, u):
                    act.wait_ge(v_done, n + 1)
                    wait_reuse(act, v_ready, n, 2)
                    nc.scalar.activation(v_new[:, u % 2, :], ps_vo[:, :], ACT.Identity).then_inc(v_copied, 1)

                def square(n, u):
                    wait_reuse(act, ss_done, n, 1)
                    for i, done in enumerate((q_done, k_done)):
                        act.wait_ge(done, n + 1)
                        nc.scalar.activation(squares[:, i, :], ps_qk[:, i, :], ACT.Square).then_inc(squared, 1)

                def turned_qk(n, u):
                    act.wait_ge(q_turned, n + 1)
                    wait_reuse(act, s_done, n, 2, 4)
                    nc.scalar.activation(qT[:, u % 2, :, :], bank[0][:, :].rearrange("p (j t) -> p j t", j=4),
                                         ACT.Identity).then_inc(qT_ready, 1)
                    act.wait_ge(k_turned, n + 1)
                    for e in range(2):
                        rows = slice(64 * e, 64 * e + 64)
                        nc.scalar.activation(kT[rows, u % 2, e:HL:2, u // 2, :],
                                             bank[1][rows, :].rearrange("p (j t) -> p j t", j=4),
                                             ACT.Identity).then_inc(kT_ready, 1)

                def exp_of(j):
                    def stage(n, u):
                        act.wait_ge(nmx_ready, n * 4 + j + 1)
                        if j >= 2:
                            act.wait_ge(p_turned, n * 4 + j - 1)
                        else:
                            wait_reuse(act, p_turned, n, 1, 4)
                        for e in range(2):
                            hd = 2 * j + e
                            nc.scalar.activation(pr[:, hd % 4, :], sm[:, hd % 4, :], ACT.Exp,
                                                 bias=nmx[:, u % 2, hd:hd + 1],
                                                 accum_out=sums[:, u % 2, hd:hd + 1]).then_inc(p_ready, 1)
                    return stage

                def p_out(j):
                    def stage(n, u):
                        act.wait_ge(p_turned, n * 4 + j + 1)
                        if j >= 2:
                            act.wait_ge(pv_done, n * 4 + j - 1)
                        else:
                            wait_reuse(act, pv_done, n, 1, 4)
                        nc.scalar.activation(pT[:, j % 2, :, :], bank[1 if j == 1 else 2][:, :].rearrange(
                            "p (j t) -> p j t", j=4), ACT.Identity).then_inc(pT_odd, 1)
                    return stage

                def turned_o(n, u):
                    act.wait_ge(o_turned, n + 1)
                    wait_reuse(act, wo_done, n, 2)
                    nc.scalar.activation(oT[:, u % 2, :, :], bank[2][:, :].rearrange("p (j t) -> p j t", j=4),
                                         ACT.Identity).then_inc(oT_ready, 1)

                pipeline(NT, 4, [(L_ATT, exp_of(0)), (L_PROJ, copy_v), (L_ATT, exp_of(1)), (L_ATT, exp_of(2)),
                                 (L_ATT, p_out(1)), (L_PROJ, square), (L_ATT, exp_of(3)), (L_TURN, turned_h),
                                 (L_ATT, p_out(3)), (L_QK, turned_qk), (L_OUT, turned_o)], 4)(act)

            @block.vector
            def _(dve):
                dve.wait_ge(loaded, 80)
                nc.vector.tensor_tensor(
                    table[:, :, :, :].rearrange("p w c d -> p w (c d)"),
                    table[:, :, :, :].rearrange("p w c d -> p w (c d)"),
                    scales[:, :, :].rearrange("p c d -> p (c d)").unsqueeze(1).to_broadcast([P, WT, 4 * DL]),
                    ALU.mult).then_inc(table_done, 1)
                dve.wait_ge(table_done, 1)
                flat = table[:, :, :, :].rearrange("p w c d -> p (w c d)")

                def rotate(n, u):
                    row = n * (2 * DL) - (u % 2) * (2 * DL)
                    heads = lambda a: a.rearrange("p (h d) -> p h d", h=HL)
                    wait_reuse(dve, sum_done, n, 1)
                    for i in range(2):
                        dve.wait_ge(squared, n * 2 + i + 1)
                        cos = flat[:, ds(row + i * DL, DL)].unsqueeze(1).to_broadcast([P, HL, DL])
                        nc.vector.tensor_tensor(heads(by_cos[:, i, :]), heads(ps_qk[:, i, :]), cos,
                                                ALU.mult).then_inc(cos_done, 1)
                    for i in range(2):
                        sin = flat[:, ds(row + 2 * DL + i * DL, DL)].rearrange("p (e d) -> p e d", e=2)
                        halves = lambda a: a.rearrange("p (h e d) -> p h e d", h=HL, e=2)
                        for e in range(2):
                            op = nc.vector.tensor_tensor(
                                halves(by_sin[:, i, :])[:, :, e, :], halves(ps_qk[:, i, :])[:, :, 1 - e, :],
                                sin[:, e, :].unsqueeze(1).to_broadcast([P, HL, DL // 2]), ALU.mult)
                        op.then_inc(sin_done, 1)
                    wait_reuse(dve, ss_max, n, 2)
                    nc.vector.reduce_sum(ss[:, u % 2, :], squares[:, :, :].rearrange("p i (h d) -> p (i h) d", h=HL),
                                         AX_X).then_inc(ss_done, 1)

                def scale_qk(n, u):
                    dve.wait_ge(rn_ready, n + 1)
                    dve.wait_ge(sum_done, n + 1)
                    wait_reuse(dve, k_turned, n, 2)
                    nc.vector.tensor_tensor(
                        qk[:, u % 2, :, :].rearrange("p i (h d) -> p (i h) d", h=HL),
                        turned[:, :, :].rearrange("p i (h d) -> p (i h) d", h=HL),
                        rn[:, u % 2, :].unsqueeze(2).to_broadcast([P, 2 * HL, DL]), ALU.mult).then_inc(qk_ready, 1)

                def mask_max(j):
                    def stage(n, u):
                        which = 2 if isinstance(n, int) and n < B else u // 2
                        wait_apart(dve, (loaded, 80), (s_done, n * 4 + j + 1),
                                   (p_ready, n * 8 + (2 * j - 2 if j >= 2 else 0)))
                        for e in range(2):
                            hd = 2 * j + e
                            nc.vector.tensor_tensor_reduce(out=sm[:, hd % 4, :], in0=ps_s[j % 2][:, e, :],
                                                           in1=mask[:, which, :], scale=1.0, scalar=-3.4e38,
                                                           op0=ALU.add, op1=ALU.max,
                                                           accum_out=mx[:, u % 2, hd:hd + 1]).then_inc(max_done, 1)
                        dve.wait_ge(max_done, n * 8 + 2 * j + 2)
                        nc.vector.tensor_scalar(nmx[:, u % 2, 2 * j:2 * j + 2], mx[:, u % 2, 2 * j:2 * j + 2], -1.0,
                                                None, ALU.mult).then_inc(nmx_ready, 1)
                    return stage

                def p_out(j):
                    def stage(n, u):
                        dve.wait_ge(p_turned, n * 4 + j + 1)
                        if j >= 2:
                            dve.wait_ge(pv_done, n * 4 + j - 1)
                        else:
                            wait_reuse(dve, pv_done, n, 1, 4)
                        nc.vector.tensor_copy(pT[:, j % 2, :, :], bank[0][:, :].rearrange(
                            "p (j t) -> p j t", j=4)).then_inc(pT_even, 1)
                    return stage

                def o_out(n, u):
                    dve.wait_ge(p_ready, n * 8 + 8)
                    nc.vector.reciprocal(rsum[:, u % 2, :], sums[:, u % 2, :]).then_inc(rsum_ready, 1)
                    dve.wait_ge(rsum_ready, n + 1)
                    dve.wait_ge(pv_done, n * 4 + 4)
                    wait_reuse(dve, o_turned, n, 2)
                    nc.vector.tensor_tensor(o[:, u % 2, :].rearrange("p (h d) -> p h d", h=HL),
                                            ps_vo[:, :].rearrange("p (h d) -> p h d", h=HL),
                                            rsum[:, u % 2, :].unsqueeze(2).to_broadcast([P, HL, DL]),
                                            ALU.mult).then_inc(o_ready, 1)

                def residual(n, u):
                    here = inner[:, ds(at_inner(n, u), D)]
                    dve.wait_ge(wo_done, n + 1)
                    nc.vector.tensor_tensor(here, bank[1][:, 0:D], here, ALU.add).then_inc(inner_done, 1)

                pipeline(NT, 4, [(L_QK, scale_qk), (L_ATT, mask_max(0)), (L_ATT, mask_max(1)), (L_ATT, p_out(0)),
                                 (L_ATT, mask_max(2)), (L_PROJ, rotate), (L_ATT, mask_max(3)), (L_ATT, p_out(2)),
                                 (L_WO, residual), (L_ATT, o_out)], 4)(dve)

            @block.tensor
            def _(pe):
                pe.wait_ge(loaded, 80)
                pe.wait_ge(cleared, 3)

                def turn_h(n, u):
                    pe.wait_ge(h_ready, n + 1)
                    free(pe, 2, 0, n)
                    for k in range(KD):
                        last = nc.tensor.transpose(bank[2][:, k * P:(k + 1) * P], h[:, u % 2, k * P:(k + 1) * P],
                                                   ident[:, :])
                    last.then_inc(h_turned, 1)

                def project(i, done):
                    def stage(n, u):
                        if i == 2:
                            pe.wait_ge(hT_ready, n * 3 + 3)
                            if isinstance(n, int):
                                if n >= 3:
                                    pe.wait_ge(o_ready, min(n - 2, NT))
                            else:
                                pe.wait_ge(o_ready, n - 2)
                        else:
                            wait_reuse(pe, cos_done, n, 1, 2)
                            wait_reuse(pe, sin_done, n, 1, 2)
                            wait_reuse(pe, squared, n, 1, 2)
                        out = ps_vo[:, :] if i == 2 else ps_qk[:, i, :]
                        for k in range(KD):
                            last = nc.tensor.matmul(out, hT[:, u, k, 0:P], wqkv[:, k, i * IN:(i + 1) * IN],
                                                    start=(k == 0), stop=(k == KD - 1))
                        last.then_inc(done, 1)
                    return stage

                def turn_qk(i, b, done):
                    def stage(n, u):
                        pe.wait_ge(qk_ready, n + 1)
                        free(pe, b, 2, n)
                        for j in range(4):
                            last = nc.tensor.transpose(bank[b][:, j * P:(j + 1) * P],
                                                       qk[:, u % 2, i, j * P:(j + 1) * P], ident[:, :])
                        last.then_inc(done, 1)
                    return stage

                def scores(j):
                    def stage(n, u):
                        if j == 0:
                            pe.wait_ge(kT_ready, n * 2 + 2)
                            pe.wait_ge(qT_ready, n + 1)
                        if j >= 2:
                            pe.wait_ge(max_done, n * 8 + 2 * j - 2)
                        else:
                            wait_reuse(pe, max_done, n, 1, 8)
                        for e in range(2):
                            keys = kT[:, u % 2, 2 * j + e, :, :].rearrange("p s t -> p (s t)")
                            last = nc.tensor.matmul(ps_s[j % 2][:, e, :], qT[:, u % 2, j, :], keys,
                                                    start=True, stop=True)
                        last.then_inc(s_done, 1)
                    return stage

                def turn_p(j, b, i):
                    def stage(n, u):
                        pe.wait_ge(p_ready, n * 8 + 2 * j + 2)
                        free(pe, b, i, n)
                        for e in range(2):
                            for blk in range(2):
                                at = (2 * e + blk) * P
                                last = nc.tensor.transpose(bank[b][:, at:at + P],
                                                           pr[:, (2 * j + e) % 4, blk * P:(blk + 1) * P], ident[:, :])
                        last.then_inc(p_turned, 1)
                    return stage

                def weigh(j):
                    def stage(n, u):
                        if j == 0:
                            pe.wait_ge(v_ready, n + 1)
                            pe.wait_ge(v_copied, min(n + 3, NT) if isinstance(n, int) else n + 3)
                        pe.wait_ge(pT_odd if j % 2 else pT_even, n * 2 + j // 2 + 1)
                        for e in range(2):
                            hd = 2 * j + e
                            for slot in range(2):
                                vals = v[:, (u % 2) + 2 * slot, hd * DL:(hd + 1) * DL]
                                last = nc.tensor.matmul(ps_vo[:, hd * DL:(hd + 1) * DL], pT[:, j % 2, 2 * e + slot, :],
                                                        vals, start=(slot == 0), stop=(slot == 1))
                        last.then_inc(pv_done, 1)
                    return stage

                def turn_o(n, u):
                    pe.wait_ge(o_ready, n + 1)
                    free(pe, 2, 2, n)
                    for j in range(4):
                        last = nc.tensor.transpose(bank[2][:, j * P:(j + 1) * P], o[:, u % 2, j * P:(j + 1) * P],
                                                   ident[:, :])
                    last.then_inc(o_turned, 1)

                def times_wo(n, u):
                    pe.wait_ge(oT_ready, n + 1)
                    free(pe, 1, 1, n)
                    for j in range(4):
                        last = nc.tensor.matmul(bank[1][:, 0:D], oT[:, u % 2, j, :], wo[:, j, :],
                                                start=(j == 0), stop=(j == 3))
                    last.then_inc(wo_done, 1)

                pipeline(NT, 4, [
                    (L_ATT, scores(0)), (L_PROJ, project(2, v_done)), (L_ATT, scores(1)), (L_PROJ, project(0, q_done)),
                    (L_ATT, turn_p(0, 0, 0)), (L_ATT, scores(2)), (L_PROJ, project(1, k_done)), (L_ATT, weigh(0)),
                    (L_ATT, turn_p(1, 1, 0)), (L_ATT, scores(3)), (L_TURN, turn_h), (L_ATT, weigh(1)),
                    (L_ATT, turn_p(2, 0, 1)), (L_WO, times_wo), (L_ATT, weigh(2)), (L_ATT, turn_p(3, 2, 1)),
                    (L_QK, turn_qk(0, 0, q_turned)), (L_QK, turn_qk(1, 1, k_turned)), (L_ATT, weigh(3)),
                    (L_OUT, turn_o)], 4)(pe)

        S.close()


def gated_mlp(nc, inner, ident, consts, w, layer):
    MT = 6
    HID = 682
    LAST = HID - (MT - 1) * P
    tag = f"gm{Sems.phases}_"
    with ExitStack() as c:
        sb = lambda name, shape, dt=F32: c.enter_context(nc.sbuf_tensor(tag + name, shape, dt))
        ps = lambda name, n: c.enter_context(nc.psum_tensor(tag + "ps_" + name, [P, n, 512], F32))
        w1 = sb("w1", [P, KD, 2, MT * P])
        w2 = sb("w2", [P, MT, D])
        cols = sb("cols", [P, 2 * KD + 2 * MT])
        late = sb("late", [P, B * WT * P])
        parts = sb("parts", [P, 2, G, 12])
        ln = LnBuffers(sb, "mlp")
        z = sb("z", [P, 2, G, D])
        zT = sb("zT", [P, 2, KD, GT])
        gelu = sb("gelu", [P, 2, GT])
        u_ = sb("u", [P, 2, MT, GT])
        ps_t, ps_g, ps_a, ps_o = ps("t", KD), ps("g", 2), ps("a", 2), ps("o", 2)
        S = Sems(nc)
        loaded, shifted, ones_set = S("loaded"), [S("shifted0"), S("shifted1")], S("ones_set")
        s = LnSems(S)
        z_ready, z_turned, zT_ready = S("z_ready"), S("z_turned"), S("zT_ready")
        g_done, a_done, gelu_ready, u_ready = S("g_done"), S("a_done"), S("gelu_ready"), S("u_ready")
        out_done, inner_done = S("out_done"), S("inner_done")
        at = lambda n, j: ((n // 4) * SLOTS + 1 + (n % 4) * G + j) * D
        with nc.Block() as block:

            @block.sync
            def _(sp):
                tiles = inner[:, :].rearrange("p (b s d) -> p b s d", b=B, s=SLOTS)
                to = late[:, :].rearrange("p (b s d) -> p b s d", b=B, s=WT)
                for b in range(B):
                    sp.dma_start(to[1:P, b, :, :], tiles[0:P - 1, b, 1:, P:D]).then_inc(shifted[b], 16)
                    sp.dma_start(to[0:1, b, :, :], tiles[P - 1:P, b, 0:WT, P:D]).then_inc(shifted[b], 16)
                    if b == 0:
                        sp.dma_start(w1[:, :, :, :], w["w1"][layer]).then_inc(loaded, 16)
                        sp.dma_start(cols[:, :], w["mlp_cols"][layer]).then_inc(loaded, 16)
                        sp.dma_start(w2[:, :, :], w["w2"][layer]).then_inc(loaded, 16)

            @block.gpsimd
            def _(pool):
                nc.gpsimd.memset(u_[:, :, MT - 1, :], 1.0).then_inc(ones_set, 1)
                pipeline(NG, 2, [(0, lambda n, p: ln_scale(nc, pool, ln, s, consts, n, p))], NG)(pool)

            @block.vector
            def _(dve):
                dve.wait_ge(loaded, 48)
                dve.wait_ge(ones_set, 1)

                def stats(n, p):
                    dve.wait_ge(shifted[n // 4], 32)
                    for j in range(G):
                        for half, src in enumerate((inner[:, at(n, j):at(n, j) + P],
                                                    late[:, (n * G + j) * P:(n * G + j + 1) * P])):
                            nc.vector.bn_stats(parts[:, p, j, 6 * half:6 * half + 6], src).then_inc(s.parts, 1)
                    dve.wait_ge(s.parts, n * 2 * G + 2 * G)
                    for j in range(G):
                        nc.vector.bn_aggr(ln.mean_var[:, p, j, :], parts[:, p, j, :]).then_inc(s.mean_var, 1)

                def normalise(n, p):
                    wait_reuse(dve, z_turned, n, 2)
                    dve.wait_ge(s.rstd, n + 1)
                    for j in range(G):
                        for half, src in enumerate((inner[:, at(n, j):at(n, j) + P],
                                                    late[:, (n * G + j) * P:(n * G + j + 1) * P])):
                            nc.vector.tensor_scalar(z[:, p, j, half * P:half * P + P], src,
                                                    ln.mean_var[:, p, j, 0:1], ln.rstd[:, p, j:j + 1],
                                                    ALU.subtract, ALU.mult).then_inc(z_ready, 1)

                def gate(n, p):
                    wait_reuse(dve, out_done, n, 2, 2)
                    for m in range(MT):
                        rows = P if m < MT - 1 else LAST
                        dve.wait_ge(gelu_ready, n * MT + m + 1)
                        dve.wait_ge(a_done, n * MT + m + 1)
                        b_a = cols[0:rows, 2 * KD + m:2 * KD + m + 1]
                        nc.vector.scalar_tensor_tensor(u_[0:rows, p, m, :], ps_a[0:rows, m % 2, :], b_a,
                                                       gelu[0:rows, m % 2, :], ALU.add, ALU.mult).then_inc(u_ready, 1)

                def residual(n, p):
                    for j in range(2):
                        dve.wait_ge(out_done, n * 2 + j + 1)
                        here = inner[:, at(n, 2 * j):at(n, 2 * j) + 2 * D]
                        nc.vector.tensor_tensor(here, ps_o[:, j, :], here, ALU.add).then_inc(inner_done, 1)

                pipeline(NG, 2, [(3, residual), (1, normalise), (0, stats), (2, gate)], NG)(dve)

            @block.scalar
            def _(act):
                act.wait_ge(loaded, 48)

                def turned(n, p):
                    wait_reuse(act, a_done, n, 2, MT)
                    act.wait_ge(z_turned, n + 1)
                    for k in range(KD):
                        nc.scalar.activation(zT[:, p, k, :], ps_t[:, k, :], ACT.Identity, scale=cols[:, k:k + 1],
                                             bias=cols[:, KD + k:KD + k + 1]).then_inc(zT_ready, 1)

                def gelus(n, p):
                    for m in range(MT):
                        rows = P if m < MT - 1 else LAST
                        act.wait_ge(g_done, n * MT + m + 1)
                        if n * MT + m >= 2:
                            act.wait_ge(u_ready, n * MT + m - 1)
                        b_g = cols[0:rows, 2 * KD + MT + m:2 * KD + MT + m + 1]
                        nc.scalar.activation(gelu[0:rows, m % 2, :], ps_g[0:rows, m % 2, :], ACT.Gelu,
                                             bias=b_g).then_inc(gelu_ready, 1)

                pipeline(NG, 2, [(1, turned), (2, gelus)], NG)(act)

            @block.tensor
            def _(pe):
                pe.wait_ge(loaded, 48)

                def turn(n, p):
                    wait_reuse(pe, zT_ready, n, 1, KD)
                    pe.wait_ge(z_ready, (n + 1) * 2 * G)
                    turn_group(nc, ps_t, z, ident, p).then_inc(z_turned, 1)

                def hidden(n, p):
                    pe.wait_ge(zT_ready, n * KD + KD)
                    for m in range(MT):
                        rows = P if m < MT - 1 else LAST
                        for which, out, done, read in ((1, ps_g, g_done, gelu_ready), (0, ps_a, a_done, u_ready)):
                            if n * MT + m >= 2:
                                pe.wait_ge(read, n * MT + m - 1)
                            for k in range(KD):
                                last = nc.tensor.matmul(out[0:rows, m % 2, :], w1[:, k, which, m * P:m * P + rows],
                                                        zT[:, p, k, :], start=(k == 0), stop=(k == KD - 1))
                            last.then_inc(done, 1)

                def outwards(n, p):
                    pe.wait_ge(u_ready, n * MT + MT)
                    for j in range(G):
                        if j % 2 == 0:
                            wait_reuse(pe, inner_done, n, 1, 2)
                        for m in range(MT):
                            last = nc.tensor.matmul(ps_o[:, j // 2, (j % 2) * D:(j % 2 + 1) * D],
                                                    u_[:, p, m, j * P:(j + 1) * P], w2[:, m, :],
                                                    start=(m == 0), stop=(m == MT - 1))
                        if j % 2 == 1:
                            last.then_inc(out_done, 1)

                pipeline(NG, 2, [(3, outwards), (1, turn), (2, hidden)], NG)(pe)

        S.close()


HF, DF = 16, 16
NU = B * HF
ROWS_Q = (0, 0, 1, 1, 0, 2)
ROWS_K = (0, 1, 0, 1, 2, 0)
DEPTH_S = 16 * len(ROWS_Q)


def full_attention(nc, x, ident, consts, w):
    tag = f"fa{Sems.phases}_"
    q_parts = nc.dram_tensor(tag + "q_parts", [NU, 3, DF, T], BF16).ap()
    k_parts = nc.dram_tensor(tag + "k_parts", [NU, 3, DF, T], BF16).ap()
    with ExitStack() as c:
        v_all = c.enter_context(nc.sbuf_tensor(tag + "v_all", [P, NU * WT * DF], F32))
        attention_inputs(nc, x, ident, consts, w, q_parts, k_parts, v_all)
        o_all = c.enter_context(nc.sbuf_tensor(tag + "o_all", [P, NU * WT * DF], F32))
        attention_heads(nc, ident, q_parts, k_parts, v_all, o_all)
        attention_out(nc, x, ident, w, o_all)


def attention_inputs(nc, x, ident, consts, w, q_parts, k_parts, v_all):
    with ExitStack() as c:
        sb = lambda name, shape, dt=F32: c.enter_context(nc.sbuf_tensor("ai_" + name, shape, dt))
        ps = lambda name, n: c.enter_context(nc.psum_tensor("ai_ps_" + name, [P, n, 512], F32))
        wp = sb("wp", [P, KD, 3, D])
        ln = LnBuffers(sb, "ai")
        z = sb("z", [P, 2, G, D])
        zT = sb("zT", [P, 2, KD, GT])
        parts = sb("parts", [P, 4, 3, GT], BF16)
        rest = sb("rest", [P, 2, GT])
        ps_t, ps_q, ps_v = ps("t", KD), ps("q", 4), ps("v", 2)
        S = Sems(nc)
        loaded, s = S("loaded"), LnSems(S)
        z_ready, z_turned, zT_ready = S("z_ready"), S("z_turned"), S("zT_ready")
        qk_done, v_done, top_ready, rest_ready, mid_ready, low_ready = (
            S(y) for y in ("qk_done", "v_done", "top_ready", "rest_ready", "mid_ready", "low_ready"))
        v_ready = S("v_ready")
        stored = [S(f"stored{m}") for m in range(4)]
        with nc.Block() as block:

            @block.sync
            def _(sp):
                sp.dma_start(wp[:, :, :, :], w["proj"]).then_inc(loaded, 16)

                def store(n, p):
                    b, at = n // (NG // B), n % (NG // B) * GT
                    for m in range(4):
                        to = q_parts if m < 2 else k_parts
                        first = b * HF + (m % 2) * 8
                        sp.wait_ge(low_ready, n * 4 + m + 1)
                        for part in range(3):
                            sp.dma_start(to[first:first + 8, part, :, at:at + GT],
                                         parts[:, m, part, :]).then_inc(stored[m], 16)

                for n in range(NG):
                    store(n, n % 2)
                for m in range(4):
                    sp.wait_ge(stored[m], 48 * NG)

            @block.gpsimd
            def _(pool):
                pipeline(NG, 2, [(0, lambda n, p: ln_scale(nc, pool, ln, s, consts, n, p))], NG)(pool)

            @block.scalar
            def _(act):
                def turned(n, p):
                    wait_reuse(act, v_done, n, 2, 2)
                    act.wait_ge(z_turned, n + 1)
                    for k in range(KD):
                        nc.scalar.activation(zT[:, p, k, :], ps_t[:, k, :], ACT.Identity).then_inc(zT_ready, 1)

                def tops(n, p):
                    for m in range(4):
                        act.wait_ge(qk_done, n * 4 + m + 1)
                        wait_reuse(act, stored[m], n, 1, 48)
                        nc.scalar.activation(parts[:, m, 0, :], ps_q[:, m, :], ACT.Identity).then_inc(top_ready, 1)

                def v_out(n, p):
                    b, first = n // (NG // B), n % (NG // B) * G
                    to = v_all[:, :].rearrange("p (b h t d) -> p b t h d", b=B, h=HF, t=WT)
                    for j in range(G):
                        if j % 2 == 0:
                            act.wait_ge(v_done, n * 2 + j // 2 + 1)
                        nc.scalar.activation(to[:, b, first + j, :, :],
                                             ps_v[:, j // 2, (j % 2) * D:(j % 2 + 1) * D].rearrange(
                                                 "p (h d) -> p h d", h=HF), ACT.Identity).then_inc(v_ready, 1)

                pipeline(NG, 2, [(1, turned), (2, tops), (2, v_out)], NG)(act)

            @block.vector
            def _(dve):
                def normalise(n, p):
                    wait_reuse(dve, z_turned, n, 2)
                    ln_apply(nc, dve, ln, s, x, z, n, p, z_ready)

                def cut(n, p):
                    for m in range(4):
                        at = n * 4 + m
                        dve.wait_ge(top_ready, at + 1)
                        if at >= 2:
                            dve.wait_ge(low_ready, at - 1)
                        nc.vector.tensor_tensor(rest[:, m % 2, :], ps_q[:, m, :], parts[:, m, 0, :],
                                                ALU.subtract).then_inc(rest_ready, 1)
                        dve.wait_ge(rest_ready, at + 1)
                        nc.vector.tensor_copy(parts[:, m, 1, :], rest[:, m % 2, :]).then_inc(mid_ready, 1)
                        dve.wait_ge(mid_ready, at + 1)
                        nc.vector.tensor_tensor(parts[:, m, 2, :], rest[:, m % 2, :], parts[:, m, 1, :],
                                                ALU.subtract).then_inc(low_ready, 1)

                pipeline(NG, 2, [(1, normalise), (0, lambda n, p: ln_stats(nc, dve, ln, s, x, n, p)),
                                 (2, cut)], NG)(dve)

            @block.tensor
            def _(pe):
                pe.wait_ge(loaded, 16)

                def turn(n, p):
                    wait_reuse(pe, zT_ready, n, 1, KD)
                    pe.wait_ge(z_ready, n * G + G)
                    turn_group(nc, ps_t, z, ident, p).then_inc(z_turned, 1)

                def products(n, p):
                    pe.wait_ge(zT_ready, n * KD + KD)
                    for m in range(4):
                        if n:
                            pe.wait_ge(rest_ready, (n - 1) * 4 + m + 1)
                        for k in range(KD):
                            last = nc.tensor.matmul(ps_q[:, m, :], wp[:, k, m // 2, (m % 2) * P:(m % 2 + 1) * P],
                                                    zT[:, p, k, :], start=(k == 0), stop=(k == KD - 1))
                        last.then_inc(qk_done, 1)
                    for j in range(G):
                        if j % 2 == 0 and n:
                            pe.wait_ge(v_ready, (n - 1) * G + j + 2)
                        for k in range(KD):
                            last = nc.tensor.matmul(ps_v[:, j // 2, (j % 2) * D:(j % 2 + 1) * D],
                                                    zT[:, p, k, j * P:(j + 1) * P], wp[:, k, 2, :],
                                                    start=(k == 0), stop=(k == KD - 1))
                        if j % 2:
                            last.then_inc(v_done, 1)

                pipeline(NG, 2, [(1, turn), (2, products)], NG)(pe)

        S.close()


def attention_heads(nc, ident, q_parts, k_parts, v_all, o_all):
    CH = T // GT
    with ExitStack() as c:
        sb = lambda name, shape, dt=F32: c.enter_context(nc.sbuf_tensor("ah_" + name, shape, dt))
        q_st = sb("q_st", [P, 4, T], BF16)
        k_st = sb("k_st", [P, 4, T], BF16)
        va = sb("va", [P, 2, WT, 32])
        pm = sb("pm", [P, 4, 2 * GT])
        mpart = sb("mpart", [P, 2, WT, CH])
        mneg = sb("mneg", [P, 2, WT])
        mrest = sb("mrest", [P, 2, 2, WT])
        m3 = sb("m3", [P, WT, 32], BF16)
        m3T = sb("m3T", [P, WT, 32], BF16)
        num = sb("num", [P, GT])
        den = sb("den", [P, 2, WT])
        ps_m = [c.enter_context(nc.psum_tensor(f"ah_ps_m{i}", [P, GT], F32)) for i in range(3)]
        ps_s = [c.enter_context(nc.psum_tensor(f"ah_ps_s{i}", [P, 2, GT], F32)) for i in range(2)]
        ps_o = c.enter_context(nc.psum_tensor("ah_ps_o", [P, GT], F32))
        S = Sems(nc)
        q_in, k_in = [S(f"q_in{i}") for i in range(4)], [S(f"k_in{i}") for i in range(4)]
        cleared, va_ready, m_done, max_done, m_ready = (
            S(y) for y in ("cleared", "va_ready", "m_done", "max_done", "m_ready"))
        m_step, m3_ready, m3T_ready, m_placed = S("m_step"), S("m3_ready"), S("m3T_ready"), S("m_placed")
        s_done, p_ready, pv_done, pv_all, num_ready = (
            S(y) for y in ("s_done", "p_ready", "pv_done", "pv_all", "num_ready"))
        num_turned, den_step, o_done = S("num_turned"), S("den_step"), S("o_done")
        L_MAX, L_EXP, L_OUT = 0, 1, 2
        NM = WT * CH
        with nc.Block() as block:

            @block.sync
            def _(sp):
                sp.wait_ge(cleared, 4)

                def load(n, u):
                    wait_reuse(sp, s_done, n, 4, 2 * WT)
                    for i in range(len(ROWS_Q)):
                        rows = slice(DF * i, DF * i + DF)
                        for st, parts, which, arrived in ((q_st, q_parts, ROWS_Q[i], q_in), (k_st, k_parts, ROWS_K[i], k_in)):
                            src = parts[ds(n, 1), which, :, :].rearrange("a d t -> (a d) t")
                            sp.dma_start(st[rows, u, :], src).then_inc(arrived[u], 16)

                pipeline(NU, 4, [(0, load)], 4)(sp)

            @block.gpsimd
            def _(pool):
                for i, (area, value) in enumerate(((k_st[96:P, :, :], 1.0), (va[:, :, :, :], 1.0), (m3[:, :, :], 0.0),
                                                   (q_st[96:P, :, :], 0.0))):
                    if i:
                        pool.wait_ge(cleared, i)
                    nc.gpsimd.memset(area, value).then_inc(cleared, 1)
                pool.wait_ge(cleared, 4)

                def copy_v(n, u):
                    wait_apart(pool, (cleared, 4), (pv_all, n - 1))
                    nc.gpsimd.tensor_copy(va[:, u % 2, :, 0:DF], v_all[:, ds(n * (WT * DF), WT * DF)].rearrange(
                        "p (t d) -> p t d", t=WT)).then_inc(va_ready, 1)

                pipeline(NU, 4, [(0, copy_v)], 4)(pool)

            @block.scalar
            def _(act):
                def place_max(n, u):
                    act.wait_ge(m3T_ready, n + 1)
                    for a in range(4):
                        nc.scalar.activation(
                            q_st[96:99, u, :].rearrange("p (t a j) -> p t a j", t=WT, a=4)[:, :, a, :],
                            m3T[32 * a:32 * a + 3, :, :], ACT.Identity).then_inc(m_placed, 1)

                def exps(n, u):
                    for i in range(2 * WT):
                        act.wait_ge(s_done, n * (2 * WT) + i + 1)
                        if i >= 4:
                            act.wait_ge(pv_done, n * (WT - 1) + (i - 4) // 2 + 1)
                        else:
                            wait_reuse(act, pv_all, n, 1)
                        nc.scalar.activation(pm[:, i % 4, :], ps_s[i % 2][:, :, :].rearrange("p a t -> p (a t)"),
                                             ACT.Exp, scale=DF ** -0.5).then_inc(p_ready, 1)

                def numerators(n, u):
                    act.wait_ge(pv_all, n + 1)
                    wait_reuse(act, num_turned, n, 1)
                    nc.scalar.activation(num[:, :], ps_o[:, :], ACT.Identity).then_inc(num_ready, 1)

                pipeline(NU, 4, [(L_EXP, exps), (L_EXP, numerators), (L_MAX, place_max)], 4)(act)

            @block.vector
            def _(dve):
                dve.wait_ge(cleared, 4)

                def finish(n, u):
                    dve.wait_ge(num_turned, n + 1)
                    turned = ps_o[:, :].rearrange("p (j c r) -> p j c r", j=4, c=CH)
                    d = lambda i: den[:, i, :].rearrange("p (j c) -> p j c", j=4)
                    nc.vector.tensor_scalar(d(0), turned[:, :, :, DF], 1e-8, None, ALU.add).then_inc(den_step, 1)
                    dve.wait_ge(den_step, n * 2 + 1)
                    nc.vector.reciprocal(den[:, 1, :], den[:, 0, :]).then_inc(den_step, 1)
                    dve.wait_ge(den_step, n * 2 + 2)
                    to = o_all[:, ds(n * (WT * DF), WT * DF)].rearrange("p (c j d) -> p j c d", c=CH, j=4)
                    nc.vector.tensor_tensor(to, turned[:, :, :, 0:DF], d(1).unsqueeze(3).to_broadcast([P, 4, CH, DF]),
                                            ALU.mult).then_inc(o_done, 1)

                def maxima(first, last):
                    def stage(n, u):
                        for i in range(first, last):
                            dve.wait_ge(m_done, n * NM + i + 1)
                            nc.vector.reduce_max(mpart[:, u % 2, i // CH, i % CH:i % CH + 1], ps_m[i % 3][:, :],
                                                 AX_X).then_inc(max_done, 1)
                        if last < NM:
                            return
                        dve.wait_ge(max_done, n * NM + NM)
                        top, mid = mrest[:, u % 2, 0, :], mrest[:, u % 2, 1, :]
                        wide = lambda k: m3[:, :, k]
                        nc.vector.reduce_max(mrest[:, u % 2, 0, :], mpart[:, u % 2, :, :], AX_X).then_inc(m_step, 1)
                        dve.wait_ge(m_step, n * 5 + 1)
                        nc.vector.tensor_scalar(mneg[:, u % 2, :], top, -1.0, None, ALU.mult).then_inc(m_step, 1)
                        dve.wait_ge(m_step, n * 5 + 2)
                        nc.vector.tensor_copy(wide(0), mneg[:, u % 2, :]).then_inc(m_step, 1)
                        dve.wait_ge(m_step, n * 5 + 3)
                        nc.vector.tensor_tensor(mid, mneg[:, u % 2, :], wide(0), ALU.subtract).then_inc(m_step, 1)
                        dve.wait_ge(m_step, n * 5 + 4)
                        nc.vector.tensor_copy(wide(1), mid).then_inc(m_step, 1)
                        dve.wait_ge(m_step, n * 5 + 5)
                        nc.vector.tensor_tensor(wide(2), mid, wide(1), ALU.subtract).then_inc(m3_ready, 1)
                        dve.wait_ge(m3_ready, n + 1)
                        wait_reuse(dve, m_placed, n, 1, 4)
                        nc.vector.transpose(m3T[:, :, :].rearrange("p t j -> p (t j)"),
                                            m3[:, :, :].rearrange("p t j -> p (t j)")).then_inc(m3T_ready, 1)
                    return stage

                pipeline(NU, 4, [(L_MAX, maxima(0, 8)), (L_OUT, finish), (L_MAX, maxima(8, NM))], 4)(dve)

            @block.tensor
            def _(pe):
                pe.wait_ge(cleared, 4)

                def for_max(t, lo, hi):
                    def stage(n, u):
                        if t == 0 and lo == 0:
                            for arrived in (q_in, k_in):
                                pe.wait_ge(arrived[u], (n - u) * (16 * len(ROWS_Q) // 4) + 16 * len(ROWS_Q))
                        for ch in range(lo, hi):
                            i = t * CH + ch
                            if i >= 3:
                                pe.wait_ge(max_done, n * NM + i - 2)
                            else:
                                wait_reuse(pe, max_done, n, 1, NM)
                            nc.tensor.matmul(ps_m[i % 3][:, :], q_st[0:DEPTH_S, u, t * P:(t + 1) * P],
                                             k_st[0:DEPTH_S, u, ch * GT:(ch + 1) * GT], start=True,
                                             stop=True).then_inc(m_done, 1)
                    return stage

                def for_exp(t, half):
                    def stage(n, u):
                        i = 2 * t + half
                        if i == 0:
                            pe.wait_ge(m_placed, n * 4 + 4)
                        if i >= 2:
                            pe.wait_ge(p_ready, n * (2 * WT) + i - 1)
                        else:
                            wait_reuse(pe, p_ready, n, 1, 2 * WT)
                        for ch in range(2):
                            at = (2 * half + ch) * GT
                            last = nc.tensor.matmul(ps_s[i % 2][:, ch, :], k_st[0:DEPTH_S + 3, u, t * P:(t + 1) * P],
                                                    q_st[0:DEPTH_S + 3, u, at:at + GT], start=True, stop=True)
                        last.then_inc(s_done, 1)
                    return stage

                def weigh(t):
                    def stage(n, u):
                        if t == 0:
                            pe.wait_ge(va_ready, n + 1)
                            wait_reuse(pe, o_done, n, 1)
                        pe.wait_ge(p_ready, n * (2 * WT) + 2 * t + 2)
                        for ch in range(CH):
                            last = nc.tensor.matmul(ps_o[32 * ch:32 * ch + 32, :], va[:, u % 2, t, :],
                                                    pm[:, (2 * t + ch // 2) % 4, ch % 2 * GT:(ch % 2 + 1) * GT],
                                                    start=(t == 0), stop=(t == WT - 1))
                        last.then_inc(pv_done if t < WT - 1 else pv_all, 1)
                    return stage

                def turn_out(n, u):
                    pe.wait_ge(num_ready, n + 1)
                    for j in range(4):
                        last = nc.tensor.transpose(ps_o[:, j * P:(j + 1) * P], num[:, j * P:(j + 1) * P], ident[:, :])
                    last.then_inc(num_turned, 1)

                order = []
                for t in range(WT):
                    order += [(L_EXP, for_exp(t, 0)), (L_MAX, for_max(t, 0, 2)), (L_EXP, for_exp(t, 1)),
                              (L_MAX, for_max(t, 2, 4))]
                    if t == 0:
                        order.append((L_OUT, turn_out))
                    else:
                        order.append((L_EXP, weigh(t - 1)))
                order.append((L_EXP, weigh(WT - 1)))
                pipeline(NU, 4, order, 4)(pe)

        S.close()


def attention_out(nc, x, ident, w, o_all):
    with ExitStack() as c:
        sb = lambda name, shape, dt=F32: c.enter_context(nc.sbuf_tensor("ao_" + name, shape, dt))
        wo = sb("wo", [P, KD, D])
        bo = sb("bo", [P, D])
        o = sb("o", [P, 2, D])
        oT = sb("oT", [P, 2, KD, P])
        out = sb("out", [P, 2, D])
        ps_t = [c.enter_context(nc.psum_tensor(f"ao_ps_t{i}", [P, 512], F32)) for i in range(2)]
        ps_o = [c.enter_context(nc.psum_tensor(f"ao_ps_o{i}", [P, 512], F32)) for i in range(2)]
        S = Sems(nc)
        loaded, o_ready, o_turned, oT_ready, out_done, out_ready, x_done = (
            S(y) for y in ("loaded", "o_ready", "o_turned", "oT_ready", "out_done", "out_ready", "x_done"))
        with nc.Block() as block:

            @block.sync
            def _(sp):
                sp.dma_start(wo[:, :, :], w["wo"]).then_inc(loaded, 16)
                sp.dma_start(bo[:, :], w["bo"].to_broadcast([P, D])).then_inc(loaded, 16)

            @block.gpsimd
            def _(pool):
                pool.wait_ge(loaded, 32)

                for b in range(B):
                    def copy_o(t, u):
                        n = t + b * WT
                        wait_apart(pool, (loaded, 32), (o_turned, n - 1))
                        nc.gpsimd.tensor_copy(o[:, u, :].rearrange("p (h d) -> p h d", h=HF),
                                              tile_of_heads(o_all, b, t)).then_inc(o_ready, 1)
                    pipeline(WT, 2, [(0, copy_o)], 2)(pool)

            @block.tensor
            def _(pe):
                pe.wait_ge(loaded, 32)

                def turn(n, u):
                    wait_reuse(pe, oT_ready, n, 2)
                    pe.wait_ge(o_ready, n + 1)
                    for k in range(KD):
                        last = nc.tensor.transpose(ps_t[u][:, k * P:(k + 1) * P], o[:, u, k * P:(k + 1) * P], ident[:, :])
                    last.then_inc(o_turned, 1)

                def project(n, u):
                    wait_reuse(pe, out_ready, n, 2)
                    pe.wait_ge(oT_ready, n + 1)
                    for k in range(KD):
                        last = nc.tensor.matmul(ps_o[u][:, 0:D], oT[:, u, k, :], wo[:, k, :], start=(k == 0),
                                                stop=(k == KD - 1))
                    last.then_inc(out_done, 1)

                pipeline(NT, 2, [(1, project), (0, turn)])(pe)

            @block.scalar
            def _(act):
                def turned(n, u):
                    wait_reuse(act, out_done, n, 2)
                    act.wait_ge(o_turned, n + 1)
                    nc.scalar.activation(oT[:, u, :, :], ps_t[u][:, 0:D].rearrange("p (k t) -> p k t", k=KD),
                                         ACT.Identity).then_inc(oT_ready, 1)

                pipeline(NT, 2, [(0, turned)])(act)

            @block.vector
            def _(dve):
                dve.wait_ge(loaded, 32)

                def add(n, u):
                    xs = x[:, ds(n * D, D)]
                    dve.wait_ge(out_done, n + 1)
                    wait_reuse(dve, x_done, n, 2)
                    nc.vector.tensor_tensor(out[:, u, :], ps_o[u][:, 0:D], bo[:, :], ALU.add).then_inc(out_ready, 1)
                    dve.wait_ge(out_ready, n + 1)
                    nc.vector.tensor_tensor(xs, xs, out[:, u, :], ALU.add).then_inc(x_done, 1)

                pipeline(NT, 2, [(0, add)])(dve)

        S.close()


def tile_of_heads(o_all, b, t):
    by_head = o_all[:, b * (HF * WT * DF):(b + 1) * (HF * WT * DF)].rearrange("p (h q) -> p h q", h=HF)
    return by_head[:, :, ds(t * DF, DF)]


def build(nc, ins, out, phases):
    Sems.phases = 0
    with ExitStack() as c:
        x = c.enter_context(nc.sbuf_tensor("x_tiles", [P, NT * D], F32))
        ident = c.enter_context(nc.sbuf_tensor("identity", [P, P], F32))
        consts = c.enter_context(nc.sbuf_tensor("consts", [P, 2, 16], F32))
        rows = lambda dram: dram.rearrange("b (n p) d -> p (b n) d", p=P)
        S = Sems(nc)
        x_in = S("x_in")
        with nc.Block() as block:

            @block.sync
            def _(sp):
                sp.dma_start(x[:, :].rearrange("p (n d) -> p n d", d=D), rows(ins["x"])).then_inc(x_in, 16)
                sp.dma_start(ident[:, :], ins["ident"]).then_inc(x_in, 16)
                sp.wait_ge(x_in, 32)

            @block.gpsimd
            def _(pool):
                nc.gpsimd.memset(consts[:, 0, :], -0.5)
                nc.gpsimd.memset(consts[:, 1, :], EPS)

        S.close()
        for phase in phases:
            phase(nc, x, ident, consts, ins)
        S = Sems(nc)
        stored = S("stored")
        with nc.Block() as block:

            @block.sync
            def _(sp):
                sp.dma_start(rows(out), x[:, :].rearrange("p (n d) -> p n d", d=D)).then_inc(stored, 16)
                sp.wait_ge(stored, 16)
        S.close()


def ffn0(nc, x, ident, consts, ins):
    token_wise_kan(nc, x, ident, {k[2:]: v for k, v in ins.items() if k.startswith("k_")}, consts)


def memory(nc, x, ident, consts, ins):
    decay_memory(nc, x, ident, consts, {k[2:]: v for k, v in ins.items() if k.startswith("m_")})


def local(nc, x, ident, consts, ins):
    local_transformer(nc, x, ident, consts, {k[2:]: v for k, v in ins.items() if k.startswith("l_")})


def full(nc, x, ident, consts, ins):
    full_attention(nc, x, ident, consts, {k[2:]: v for k, v in ins.items() if k.startswith("f_")})


def by_block(w, k=P):
    return np.ascontiguousarray(w.reshape(-1, k, w.shape[-1]).transpose(1, 0, 2))


def kan_arrays(Win, bin_, W1, b1, W2, b2, Wout, bout):
    m = np.arange(64)
    place = 32 * (m // 8 % 4) + 8 * (m // 32) + m % 8
    pairs = lambda a: np.ascontiguousarray(a.reshape(8, 128).T)
    g_bias = np.zeros((P, 1), np.float32)
    g_bias[place, 0] = b2
    g_bias[16, 0] = 1.0
    wout = np.zeros((P, D), np.float32)
    wout[place] = Wout
    wout[16] = bout
    cols = np.concatenate([np.concatenate([bin_, bin_])[:, None], g_bias, pairs(W1), pairs(b1), pairs(W2)], 1)
    row, col = np.arange(P)[:, None, None], np.arange(P)[None, None, :]
    j = np.arange(8)[None, :, None]
    sel = (row % 64 == 8 * j + col // 16).astype(np.float32)
    w2_mask = (np.arange(32)[None, None, :] == 8 * (j // 4) + row // 16).astype(np.float32)
    return {"k_win": by_block(Win), "k_cols": cols, "k_sel": sel, "k_w2_mask": w2_mask, "k_wout": wout}


def memory_arrays(q_w, k_w, v_w, Wq, Wk, g_w, g_b, base_decay_logits, out_w, out_b, ln_g, ln_b):
    proj = np.stack([by_block(a.T) for a in (q_w, k_w, v_w, g_w)], 2)
    rank = np.zeros((P, 8, P), np.float32)
    for m, (w, hf) in enumerate(((Wq, 0), (Wq, 1), (Wk, 0), (Wk, 1))):
        for h in range(8):
            at = slice(16 * h, 16 * h + 16)
            rank[at, m, at] = w[8 * hf + h].T
            rank[at, m + 4, at] = w[8 * hf + h].T[np.arange(16) ^ 1]
    halves = lambda a: np.ascontiguousarray(a.reshape(2, P).T)
    cols = np.concatenate([halves(g_b), np.repeat(halves(base_decay_logits.reshape(-1)), B, 1)], 1)
    row, col, d = np.arange(P)[:, None, None], np.arange(P)[None, None, :], np.arange(16)[None, :, None]
    spread = ((row // 16 == col // 16) & (row % 16 == d)).astype(np.float32)
    sum_r = (np.arange(32)[None, None, :] == 8 * np.arange(4)[None, :, None] + row // 16).astype(np.float32)
    y_row = np.arange(P)
    feature = 16 * (y_row % 8) + 4 * (y_row % 32 // 8) + y_row // 32
    w_out = np.stack([np.ascontiguousarray(out_w.T[P * hf + feature]) for hf in range(2)], 1)
    return {"m_proj": proj, "m_rank": rank, "m_cols": cols, "m_rope": rope_table(), "m_spread": spread,
            "m_sum_r": sum_r, "m_out_w": w_out, "m_out_b": out_b[None], "m_ln_g": ln_g[None], "m_ln_b": ln_b[None]}


def rope_table():
    f = np.float32
    inv = f(1.0) / f(10000.0) ** (np.arange(8, dtype=f) / f(8))
    angle = (np.arange(T, dtype=f)[:, None] * inv[None, :]).astype(f)
    d = np.arange(P) % 16
    cos, sin = np.cos(angle).T[d // 2], np.sin(angle).T[d // 2]
    return np.ascontiguousarray(np.stack([cos, np.where(d % 2, -1, 1)[:, None] * sin], 1).astype(f))


def local_arrays(wqkv, q_scale, k_scale, wo, ln_g, ln_b, w1, b1, w2, b2):
    turn = (np.arange(64) + 32) % 64
    scales = np.stack([np.stack([np.concatenate([q, k]), np.concatenate([q[turn], k[turn]])])[None]
                       for q, k in zip(q_scale, k_scale)])
    hid = w2.shape[1]
    w1p = np.zeros((2, P, KD, 2, 6 * P), np.float32)
    for i in range(2):
        w1p[i, :, :, 0, :hid] = by_block(w1[i][:, :hid])
        w1p[i, :, :, 1, :hid] = by_block(w1[i][:, hid:])
    w2p = np.zeros((2, 6 * P, D), np.float32)
    w2p[:, :hid] = w2
    w2p[:, hid] = b2
    cols = np.zeros((2, P, 4 + 12), np.float32)
    cols[:, :, 0:2] = ln_g.reshape(2, 2, P).transpose(0, 2, 1)
    cols[:, :, 2:4] = ln_b.reshape(2, 2, P).transpose(0, 2, 1)
    b1p = np.zeros((2, 2, 6 * P), np.float32)
    b1p[:, :, :hid] = b1.reshape(2, 2, hid)
    cols[:, :, 4:] = b1p.reshape(2, 12, P).transpose(0, 2, 1)
    blocks = lambda a: np.stack([by_block(v) for v in a])
    return {"l_wqkv": blocks(wqkv), "l_scales": scales, "l_wo": blocks(wo), "l_w1": w1p, "l_w2": blocks(w2p),
            "l_mlp_cols": cols, "l_table": rotary_table(), "l_mask": window_mask()}


def rotary_table():
    f = np.float32
    half = np.arange(0, 64, 2, dtype=f)
    inv = f(1.0) / f(10000.0) ** (half / f(64))
    t = np.arange(T, dtype=f)
    angle = t[:, None] * inv[None, :]
    angle = np.concatenate([angle, angle], 1)
    base = (half + f(0.4 * 64)) / f(1.4 * 64)
    power = (t - f(T // 2)) / f(64.0)
    scale = base[None, :] ** power[:, None]
    scale = np.concatenate([scale, scale], 1)
    sign = np.where(np.arange(64) < 32, -1, 1).astype(f)
    cos, sin = np.cos(angle), np.sin(angle) * sign
    table = np.stack([np.stack([f(8) * cos * scale, cos / scale], 1), np.stack([f(8) * sin * scale, sin / scale], 1)], 1)
    table = table.reshape(WT, P, 2, 2 * 64).transpose(1, 0, 2, 3)
    return np.ascontiguousarray(table.astype(f))


def window_mask():
    i, j = np.arange(P)[:, None], np.arange(P)[None, :]
    far = np.float32(-3e38)
    own, before = np.where(j <= i, 0, far), np.where(j >= i, 0, far)
    none = np.full((P, P), far)
    return np.stack([np.concatenate(x, 1) for x in ((own, before), (before, own), (own, none))], 1).astype(np.float32)


def full_arrays(Wq, Wk, Wv, Wo, bo):
    return {"f_proj": np.stack([by_block(a.T) for a in (Wq, Wk, Wv)], 2), "f_wo": by_block(Wo.T), "f_bo": bo[None]}


def arrays_of(i):
    pick = lambda prefix, names: [i[prefix + n] for n in names.split()]
    arrays = {"x": i["L0_attn_x"], "ident": np.eye(P, dtype=np.float32)}
    arrays.update(kan_arrays(*pick("L0_ffn_", "Win bin_ W1 b1 W2 b2 Wout bout")))
    arrays.update(memory_arrays(*pick("L0_attn_", "q_w k_w v_w Wq Wk g_w g_b base_decay_logits out_w out_b ln_g ln_b")))
    arrays.update(local_arrays(*pick("L1_ffn_", "wqkv q_scale k_scale wo ln_g ln_b w1 b1 w2 b2")))
    arrays.update(full_arrays(*pick("L1_attn_", "Wq Wk Wv Wo bo")))
    return arrays


def kernel(**inputs):
    import concourse.bacc as bacc
    from concourse.bass_utils import run_bass_kernel_spmd

    nc = bacc.Bacc("TRN2", target_bir_lowering=False, num_devices=1)
    arrays, ins = {}, {}
    for name, a in arrays_of({name: np.asarray(a) for name, a in inputs.items()}).items():
        a = np.ascontiguousarray(a)
        arrays[f"in_{name}_dram"] = a
        ins[name] = nc.dram_tensor(f"in_{name}_dram", a.shape, mybir.dt.from_np(a.dtype), kind="ExternalInput").ap()
    out = nc.dram_tensor("out_0_dram", (B, T, D), F32, kind="ExternalOutput").ap()
    build(nc, ins, out, [ffn0, memory, ffn0, local, full, local])
    r = run_bass_kernel_spmd(nc, [arrays], core_ids=[0])
    return r.results[0]["out_0_dram"]
```

```python
from contextlib import ExitStack

import numpy as np

import concourse.bass as bass
from concourse import mybir

ACT = mybir.ActivationFunctionType
ALU = mybir.AluOpType
AX_X = mybir.AxisListType.X
F32 = mybir.dt.float32
BF16 = mybir.dt.bfloat16
F32R = mybir.dt.float32r

P = 128
B, T, D = 2, 2048, 256
NT = B * T // P
WT = T // P
KD = D // P
G = 4
GT = G * P
NG = NT // G
EPS = 1e-5


def ds(start, size):
    return bass.ds(start, size)


def pipeline(units, unroll, stages, depth=2):

    def program(eng):
        last_lag = max(lag for lag, _ in stages)
        first = -(-(last_lag + depth) // unroll) * unroll
        first = min(first, units)
        end = max(first, units // unroll * unroll)

        def peeled(n):
            for lag, stage in stages:
                if 0 <= n - lag < units:
                    stage(n - lag, (n - lag) % unroll)

        for n in range(first):
            peeled(n)
        if end > first:
            with eng.Fori(first // unroll, end // unroll) as i:
                for u in range(unroll):
                    for lag, stage in stages:
                        stage(i * unroll + (u - lag), (u - lag) % unroll)
        for n in range(end, units + last_lag):
            peeled(n)

    return program


def after_first(n):
    return not isinstance(n, int) or n > 0


def wait_reuse(eng, sem, unit, depth, per=1):
    if isinstance(unit, int) and unit < depth:
        return
    eng.wait_ge(sem, (unit - (depth - 1)) * per)


def wait_apart(eng, settled, *waits):
    if any(not isinstance(count, int) for _, count in waits):
        waits = [(sem, count if isinstance(count, int) else eng.to_reg(count)) for sem, count in waits]
        eng.wait_ge(*settled)
    for sem, count in waits:
        if not isinstance(count, int) or count > 0:
            eng.wait_ge(sem, count)


class Sems:

    phases = 0

    def __init__(self, nc):
        self.nc, self.made = nc, []
        Sems.phases += 1

    def __call__(self, name):
        s = self.nc.alloc_semaphore(f"{name}_{Sems.phases}")
        self.made.append(s)
        return s

    def close(self):
        self.nc.clear_and_free_semaphores(self.made)
        self.nc.all_engine_barrier()


class LnBuffers:

    def __init__(self, sb, name):
        self.parts = sb(f"{name}_ln_parts", [P, 2, G, 6])
        self.mean_var = sb(f"{name}_ln_mv", [P, 2, G, 2])
        self.var_eps = sb(f"{name}_ln_ve", [P, 2, G])
        self.rstd = sb(f"{name}_ln_rstd", [P, 2, G])


class LnSems:
    def __init__(self, S, name="ln"):
        self.parts, self.mean_var, self.var_eps, self.rstd = (
            S(f"{name}_{x}") for x in ("parts", "mean_var", "var_eps", "rstd"))


def ln_stats(nc, dve, b, s, x, n, p):
    for j in range(G):
        nc.vector.bn_stats(b.parts[:, p, j, :], x[:, ds(n * (G * D) + j * D, D)]).then_inc(s.parts, 1)
    wait_apart(dve, (s.parts, G), (s.parts, n * G + G))
    for j in range(G):
        nc.vector.bn_aggr(b.mean_var[:, p, j, :], b.parts[:, p, j, :]).then_inc(s.mean_var, 1)


def ln_scale(nc, pool, b, s, consts, n, p):
    pool.wait_ge(s.mean_var, n * G + G)
    nc.gpsimd.tensor_tensor(b.var_eps[:, p, :], b.mean_var[:, p, :, 1], consts[:, 1, 0:G], ALU.add).then_inc(s.var_eps, 1)
    pool.wait_ge(s.var_eps, n + 1)
    nc.gpsimd.tensor_tensor(b.rstd[:, p, :], b.var_eps[:, p, :], consts[:, 0, 0:G], ALU.pow).then_inc(s.rstd, 1)


def ln_apply(nc, dve, b, s, x, z, n, p, z_ready):
    dve.wait_ge(s.rstd, n + 1)
    for j in range(G):
        nc.vector.tensor_scalar(z[:, p, j, :], x[:, ds(n * (G * D) + j * D, D)], b.mean_var[:, p, j, 0:1],
                                b.rstd[:, p, j:j + 1], ALU.subtract, ALU.mult).then_inc(z_ready, 1)


def token_wise_kan(nc, x, ident, w, consts, arrived=None):
    NF = 64
    MT = 8
    with ExitStack() as c:
        sb = lambda name, shape, dt=F32: c.enter_context(nc.sbuf_tensor(f"ff{Sems.phases}_{name}", shape, dt))
        ps = lambda name, n: c.enter_context(nc.psum_tensor(f"ff{Sems.phases}_{name}", [P, n, 512], F32))
        win = sb("kan_win", [P, KD, P])
        wout = sb("kan_wout", [P, D])
        cols = sb("kan_cols", [P, 2 * MT + 2 + MT])
        b_in, g_bias = cols[:, 0:1], cols[:, 1:2]
        w1c, b1c, w2c = (cols[:, 2 + MT * i:2 + MT * (i + 1)] for i in range(3))
        w2m = sb("kan_w2m", [P, MT, 32])
        w2b = sb("kan_w2b", [P, MT, 32])
        sel_f = sb("kan_self", [P, MT, P])
        sel = sb("kan_sel", [P, MT, P], BF16)
        ln = LnBuffers(sb, "k")
        z = sb("kan_z", [P, 2, G, D])
        zT = sb("kan_zT", [P, 2, KD, GT])
        s32 = sb("kan_s32", [P, 2, GT])
        s_rest = sb("kan_srest", [P, 2, GT])
        s_top = sb("kan_stop", [P, 2, GT], BF16)
        s_mid = sb("kan_smid", [P, 2, GT], BF16)
        s_low = sb("kan_slow", [P, 2, GT], BF16)
        h = sb("kan_h", [P, MT, GT])
        g = sb("kan_g", [P, 2, GT])
        ps_t, ps_s, ps_b, ps_g, ps_o = ps("kan_pt", KD), ps("kan_ps", 1), ps("kan_pb", 2), ps("kan_pg", 1), ps("kan_po", 2)

        S = Sems(nc)
        loaded, sel_ready, w2_built = S("loaded"), S("sel_ready"), S("w2_built")
        stats = LnSems(S)
        z_ready, z_turned, zT_ready = S("z_ready"), S("z_turned"), S("zT_ready")
        s_done, s_ready, split_a, split_ready = S("s_done"), S("s_ready"), S("split_a"), S("split_ready")
        spread_done, relu_done, g_halves, g_ready = S("spread_done"), S("relu_done"), S("g_done"), S("g_ready")
        out_done, x_done = S("out_done"), S("x_done")
        with nc.Block() as block:

            @block.sync
            def _(sp):
                sp.dma_start(win[:, :, 0:NF], w["win"]).then_inc(loaded, 16)
                sp.dma_start(win[:, :, NF:P], w["win"]).then_inc(loaded, 16)
                sp.dma_start(cols[:, :], w["cols"]).then_inc(loaded, 16)
                sp.dma_start(sel_f[:, :, :], w["sel"]).then_inc(loaded, 16)
                sp.dma_start(w2m[:, :, :], w["w2_mask"]).then_inc(loaded, 16)
                sp.dma_start(wout[:, :], w["wout"]).then_inc(loaded, 16)

            @block.gpsimd
            def _(pool):
                pool.wait_ge(loaded, 96)
                nc.gpsimd.tensor_copy(sel[:, :, :], sel_f[:, :, :]).then_inc(sel_ready, 1)
                pipeline(NG, 2, [(0, lambda n, p: ln_scale(nc, pool, ln, stats, consts, n, p))])(pool)

            @block.vector
            def _(dve):
                dve.wait_ge(loaded, 96)
                for j in range(MT):
                    nc.vector.tensor_scalar(w2b[:, j, :], w2m[:, j, :], w2c[:, j:j + 1], None,
                                            ALU.mult).then_inc(w2_built, 1)

                def normalise(n, p):
                    wait_reuse(dve, z_turned, n, 2)
                    ln_apply(nc, dve, ln, stats, x, z, n, p, z_ready)

                def split(n, p):
                    dve.wait_ge(s_ready, n + 1)
                    wait_reuse(dve, spread_done, n, 2, MT)
                    nc.vector.tensor_copy(s_top[:, p, :], s32[:, p, :]).then_inc(split_a, 1)
                    dve.wait_ge(split_a, n * 3 + 1)
                    nc.vector.tensor_tensor(s_rest[:, p, :], s32[:, p, :], s_top[:, p, :],
                                            ALU.subtract).then_inc(split_a, 1)
                    dve.wait_ge(split_a, n * 3 + 2)
                    nc.vector.tensor_copy(s_mid[:, p, :], s_rest[:, p, :]).then_inc(split_a, 1)
                    dve.wait_ge(split_a, n * 3 + 3)
                    nc.vector.tensor_copy(s_top[NF:P, p, :], s_mid[NF:P, p, :]).then_inc(split_ready, 1)
                    nc.vector.tensor_tensor(s_low[0:NF, p, :], s_rest[0:NF, p, :], s_mid[0:NF, p, :],
                                            ALU.subtract).then_inc(split_ready, 1)

                def g_out(n, p):
                    dve.wait_ge(g_halves, n * 2 + 2)
                    wait_reuse(dve, out_done, n, 2, 2)
                    nc.vector.tensor_scalar(g[:, p, :], ps_g[:, 0, :], g_bias, None, ALU.add).then_inc(g_ready, 1)

                def residual(n, p):
                    for j in range(2):
                        dve.wait_ge(out_done, n * 2 + j + 1)
                        xs = x[:, ds(n * (G * D) + j * 2 * D, 2 * D)]
                        nc.vector.scalar_tensor_tensor(xs, ps_o[:, j, :], 0.5, xs, ALU.mult,
                                                       ALU.add).then_inc(x_done, 1)

                def statistics(n, p):
                    if arrived:
                        dve.wait_ge(arrived[n], 16)
                    ln_stats(nc, dve, ln, stats, x, n, p)

                pipeline(NG, 2, [(5, g_out), (1, normalise), (0, statistics), (3, split), (5, residual)],
                         NG if arrived else 2)(dve)

            @block.scalar
            def _(act):
                act.wait_ge(loaded, 96)

                def turned(n, p):
                    wait_reuse(act, s_done, n, 2)
                    act.wait_ge(z_turned, n + 1)
                    for k in range(KD):
                        nc.scalar.activation(zT[:, p, k, :], ps_t[:, k, :], ACT.Identity).then_inc(zT_ready, 1)

                def s_out(n, p):
                    act.wait_ge(s_done, n + 1)
                    wait_reuse(act, split_ready, n, 2, 2)
                    nc.scalar.activation(s32[:, p, :], ps_s[:, 0, :], ACT.Identity, bias=b_in).then_inc(s_ready, 1)

                def relus(first, last):
                    def stage(n, p):
                        for j in range(first, last):
                            act.wait_ge(spread_done, n * MT + j + 1)
                            if after_first(n):
                                act.wait_ge(g_halves, (n - 1) * 2 + j // 4 + 1)
                            nc.scalar.activation(h[:, j, :], ps_b[:, j % 2, :], ACT.Relu, bias=b1c[:, j:j + 1],
                                                 scale=w1c[:, j:j + 1]).then_inc(relu_done, 1)
                    return stage

                pipeline(NG, 2, [(4, relus(0, 2)), (2, turned), (4, relus(2, 4)), (3, s_out), (4, relus(4, 8))])(act)

            @block.tensor
            def _(pe):
                pe.wait_ge(loaded, 96)
                if arrived:
                    pe.wait_ge(arrived[NG], 16)
                pe.wait_ge(sel_ready, 1)
                pe.wait_ge(w2_built, MT)

                def turn(n, p):
                    wait_reuse(pe, zT_ready, n, 1, KD)
                    pe.wait_ge(z_ready, n * G + G)
                    for j in range(G):
                        for k in range(KD):
                            last = nc.tensor.transpose(ps_t[:, k, j * P:(j + 1) * P],
                                                       z[:, p, j, k * P:(k + 1) * P], ident[:, :])
                    last.then_inc(z_turned, 1)

                def project(n, p):
                    wait_reuse(pe, s_ready, n, 1)
                    pe.wait_ge(zT_ready, n * KD + KD)
                    for k in range(KD):
                        last = nc.tensor.matmul(ps_s[:, 0, :], win[:, k, :], zT[:, p, k, :],
                                                start=(k == 0), stop=(k == KD - 1))
                    last.then_inc(s_done, 1)

                def spread(*js):
                    def stage(n, p):
                        for j in js:
                            if j == 0:
                                pe.wait_ge(split_ready, n * 2 + 2)
                            if j >= 2:
                                pe.wait_ge(relu_done, n * MT + j - 1)
                            else:
                                wait_reuse(pe, relu_done, n, 1, MT)
                            nc.tensor.matmul(ps_b[:, j % 2, :], sel[:, j, :], s_top[:, p, :], start=True, stop=False)
                            nc.tensor.matmul(ps_b[:, j % 2, :], sel[0:NF, j, :], s_low[0:NF, p, :],
                                             start=False, stop=True).then_inc(spread_done, 1)
                    return stage

                def over_h(half):
                    def stage(n, p):
                        if half == 0:
                            wait_reuse(pe, g_ready, n, 1)
                        pe.wait_ge(relu_done, n * MT + half * 4 + 4)
                        for q in range(4):
                            j = half * 4 + q
                            last = nc.tensor.matmul(ps_g[32 * q:32 * q + 32, 0, :], w2b[:, j, :], h[:, j, :],
                                                    start=(half == 0), stop=(half == 1))
                        last.then_inc(g_halves, 1)
                    return stage

                def outwards(n, p):
                    pe.wait_ge(g_ready, n + 1)
                    for j in range(G):
                        if j % 2 == 0:
                            wait_reuse(pe, x_done, n, 1, 2)
                        last = nc.tensor.matmul(ps_o[:, j // 2, (j % 2) * D:(j % 2 + 1) * D],
                                                g[:, p, j * P:(j + 1) * P], wout[:, :], start=True, stop=True)
                        if j % 2 == 1:
                            last.then_inc(out_done, 1)

                pipeline(NG, 2, [(4, spread(0, 1)), (2, turn), (4, spread(2, 3)), (3, project), (4, spread(4, 5)),
                                 (4, over_h(0)), (4, spread(6, 7)), (5, outwards), (4, over_h(1))])(pe)

        S.close()


def decay_memory(nc, x, ident, consts, w):
    DH = 16
    with ExitStack() as c:
        sb = lambda name, shape, dt=F32: c.enter_context(nc.sbuf_tensor("mem_" + name, shape, dt))
        q_r = sb("q_r", [P, 2 * B * T])
        k_g = sb("k_g", [P, 2 * B * T])
        v_p = [sb(f"v{i}", [P, 2 * B * T], BF16) for i in range(3)]
        decay = sb("decay", [P, 2 * B])

        with ExitStack() as c2:
            sb2 = lambda name, shape, dt=F32: c2.enter_context(nc.sbuf_tensor("mem_" + name, shape, dt))
            ps = lambda name, n: c2.enter_context(nc.psum_tensor("mem_" + name, [P, n, 512], F32))
            wp = sb2("wp", [P, KD, 4, D])
            rank = sb2("rank", [P, 8, P])
            cols = sb2("cols", [P, 2 + 2 * B])
            rope = sb2("rope", [P, 2, 2, GT])
            ln = LnBuffers(sb2, "mem")
            z = sb2("z", [P, 2, G, D])
            zT = sb2("zT", [P, 2, KD, GT])
            qc = sb2("qc", [P, 4, 2, GT])
            gate = sb2("gate", [P, 2, GT])
            v32 = sb2("v32", [P, 2, GT])
            v_rest = sb2("v_rest", [P, GT])
            ps_t, ps_q, ps_r, ps_v, = ps("pt", KD), ps("pq", 2), ps("pr", 2), ps("pv", 2)
            S = Sems(nc)
            loaded, rope_in, decay_a = S("loaded"), [S("rope_in0"), S("rope_in1")], S("decay_a")
            stats = LnSems(S)
            z_ready, z_turned, zT_ready = S("z_ready"), S("z_turned"), S("zT_ready")
            qk_done, roped, rank_done, rank_out = S("qk_done"), S("roped"), S("rank_done"), S("rank_out")
            gv_done, gate_ready, v_copied, v_split = S("gv_done"), S("gate_ready"), S("v_copied"), S("v_split")
            with nc.Block() as block:

                @block.sync
                def _(sp):
                    sp.dma_start(wp[:, :, :, :], w["proj"]).then_inc(loaded, 16)
                    sp.dma_start(rank[:, :, :], w["rank"]).then_inc(loaded, 16)
                    sp.dma_start(cols[:, :], w["cols"]).then_inc(loaded, 16)

                    def load_rope(n, p):
                        wait_reuse(sp, roped, n, 2, 8)
                        at = n % (NG // B)
                        sp.dma_start(rope[:, p, :, :], w["rope"][:, :, ds(at * GT, GT)]).then_inc(rope_in[p], 16)

                    for n in range(NG):
                        load_rope(n, n % 2)

                @block.gpsimd
                def _(pool):
                    pipeline(NG, 2, [(0, lambda n, p: ln_scale(nc, pool, ln, stats, consts, n, p))])(pool)

                @block.scalar
                def _(act):
                    act.wait_ge(loaded, 48)
                    nc.scalar.activation(decay[:, :], cols[:, 2:2 + 2 * B], ACT.Sigmoid).then_inc(decay_a, 1)

                    def turned(n, p):
                        wait_reuse(act, gv_done, n, 2, 4)
                        act.wait_ge(z_turned, n + 1)
                        for k in range(KD):
                            nc.scalar.activation(zT[:, p, k, :], ps_t[:, k, :], ACT.Identity).then_inc(zT_ready, 1)

                    def gates(n, p):
                        for hf in range(2):
                            act.wait_ge(gv_done, n * 4 + hf + 1)
                            wait_reuse(act, rank_out, n, 1, 4)
                            nc.scalar.activation(gate[:, hf, :], ps_v[:, hf, :], ACT.Sigmoid,
                                                 bias=cols[:, hf:hf + 1]).then_inc(gate_ready, 1)
                        for hf in range(2):
                            act.wait_ge(gv_done, n * 4 + hf + 3)
                            wait_reuse(act, v_split, n, 1, 10)
                            nc.scalar.activation(v32[:, hf, :], ps_v[:, hf, :], ACT.Identity).then_inc(v_copied, 1)

                    pipeline(NG, 2, [(2, turned), (3, gates)])(act)

                @block.vector
                def _(dve):
                    dve.wait_ge(loaded, 48)

                    def normalise(n, p):
                        wait_reuse(dve, z_turned, n, 2)
                        ln_apply(nc, dve, ln, stats, x, z, n, p, z_ready)

                    def turn_qk(m):
                        def stage(n, p):
                            dve.wait_ge(rope_in[p], (n - p) * 8 + 16)
                            dve.wait_ge(qk_done, n * 4 + m + 1)
                            if after_first(n):
                                dve.wait_ge(rank_done, (n - 1) * 4 + m + 1)
                            for cs in range(2):
                                nc.vector.tensor_tensor(qc[:, m, cs, :], ps_q[:, m % 2, :], rope[:, p, cs, :],
                                                        ALU.mult).then_inc(roped, 1)
                        return stage

                    def ranks(m):
                        def stage(n, p):
                            hf = m % 2
                            wait_apart(dve, (loaded, 48), (rank_done, n * 4 + m + 1))
                            if m < 2:
                                nc.vector.tensor_copy(q_r[:, ds(n * GT + hf * B * T, GT)],
                                                      ps_r[:, m % 2, :]).then_inc(rank_out, 1)
                            else:
                                dve.wait_ge(gate_ready, n * 2 + 2)
                                nc.vector.scalar_tensor_tensor(k_g[:, ds(n * GT + hf * B * T, GT)], ps_r[:, m % 2, :],
                                                               DH ** -0.5, gate[:, hf, :], ALU.mult,
                                                               ALU.mult).then_inc(rank_out, 1)
                        return stage

                    def split_v(n, p):
                        for hf in range(2):
                            tok = lambda i: v_p[i][:, ds(n * GT + hf * B * T, GT)]
                            base = n * 10 + hf * 5
                            wait_apart(dve, (loaded, 48), (v_copied, n * 2 + hf + 1))
                            nc.vector.tensor_copy(tok(0), v32[:, hf, :]).then_inc(v_split, 1)
                            dve.wait_ge(v_split, base + 1)
                            nc.vector.tensor_tensor(v_rest[:, :], v32[:, hf, :], tok(0), ALU.subtract).then_inc(v_split, 1)
                            wait_apart(dve, (loaded, 48), (v_split, base + 2))
                            nc.vector.tensor_copy(tok(1), v_rest[:, :]).then_inc(v_split, 1)
                            dve.wait_ge(v_split, base + 3)
                            nc.vector.tensor_tensor(tok(2), v_rest[:, :], tok(1), ALU.subtract).then_inc(v_split, 2)

                    pipeline(NG, 2, [(4, ranks(0)), (3, turn_qk(0)), (4, ranks(1)), (3, turn_qk(1)), (4, split_v),
                                     (4, ranks(2)), (3, turn_qk(2)), (4, ranks(3)), (3, turn_qk(3)),
                                     (1, normalise), (0, lambda n, p: ln_stats(nc, dve, ln, stats, x, n, p))])(dve)

                @block.tensor
                def _(pe):
                    pe.wait_ge(loaded, 48)

                    def turn(n, p):
                        wait_reuse(pe, zT_ready, n, 1, KD)
                        pe.wait_ge(z_ready, n * G + G)
                        turn_group(nc, ps_t, z, ident, p).then_inc(z_turned, 1)

                    def proj(out, which, hf, p):
                        for k in range(KD):
                            last = nc.tensor.matmul(out, wp[:, k, which, hf * P:(hf + 1) * P], zT[:, p, k, :],
                                                    start=(k == 0), stop=(k == KD - 1))
                        return last

                    def qk(m):
                        def stage(n, p):
                            pe.wait_ge(zT_ready, n * KD + KD)
                            if m >= 2:
                                pe.wait_ge(roped, n * 8 + 2 * (m - 1))
                            else:
                                wait_reuse(pe, roped, n, 1, 8)
                            proj(ps_q[:, m % 2, :], m // 2, m % 2, p).then_inc(qk_done, 1)
                        return stage

                    def gate_or_v(i):
                        def stage(n, p):
                            if i < 2:
                                wait_reuse(pe, v_copied, n, 1, 2)
                            else:
                                pe.wait_ge(gate_ready, n * 2 + i - 1)
                            proj(ps_v[:, i % 2, :], 3 if i < 2 else 2, i % 2, p).then_inc(gv_done, 1)
                        return stage

                    def to_ranks(m):
                        def stage(n, p):
                            pe.wait_ge(roped, n * 8 + 2 * (m + 1))
                            if m >= 2:
                                pe.wait_ge(rank_out, n * 4 + m - 1)
                            else:
                                wait_reuse(pe, rank_out, n, 1, 4)
                            for cs in range(2):
                                last = nc.tensor.matmul(ps_r[:, m % 2, :], rank[:, m + 4 * cs, :], qc[:, m, cs, :],
                                                        start=(cs == 0), stop=(cs == 1))
                            last.then_inc(rank_done, 1)
                        return stage

                    order = []
                    for m in range(4):
                        order += [(4, to_ranks(m)), (3, qk(m))]
                        if m == 1:
                            order.append((2, turn))
                    pipeline(NG, 2, order + [(3, gate_or_v(i)) for i in range(4)])(pe)

            S.close()
        memory_scan(nc, q_r, k_g, v_p, decay, w)
        memory_out(nc, x, ident, consts, k_g, w)


def turn_group(nc, ps_t, z, ident, p):
    for j in range(G):
        for k in range(KD):
            last = nc.tensor.transpose(ps_t[:, k, j * P:(j + 1) * P], z[:, p, j, k * P:(k + 1) * P], ident[:, :])
    return last


def memory_scan(nc, q_r, k_g, v_p, decay, w):
    NC = T // GT
    UN = 4 * NC
    with ExitStack() as c:
        sb = lambda name, shape, dt=F32: c.enter_context(nc.sbuf_tensor("scan_" + name, shape, dt))
        ps = lambda name, n: c.enter_context(nc.psum_tensor("scan_" + name, [P, n, 512], F32))
        sel_f = sb("self", [P, 16, P])
        sel = sb("sel", [P, 16, P], BF16)
        red = sb("red", [P, 4, 32])
        kv = sb("kv", [P, 4, GT])
        mem = sb("mem", [P, 8, GT])
        qm = sb("qm", [P, 8, GT])
        ps_v, ps_y = ps("pv", 4), ps("py", NC)
        S = Sems(nc)
        loaded, sel_ready, spread, kv_done, scanned, qm_done, summed, y_done = (
            S(x) for x in ("loaded", "sel_ready", "spread", "kv_done", "scanned", "qm_done", "summed", "y_done"))
        sel_in = [S(f"sel_in{dg}") for dg in range(4)]
        with nc.Block() as block:

            @block.sync
            def _(sp):
                for dg in range(4):
                    some = slice(4 * dg, 4 * dg + 4)
                    sp.dma_start(sel_f[:, some, :], w["spread"][:, some, :]).then_inc(sel_in[dg], 16)
                    if dg == 0:
                        sp.dma_start(red[:, :, :], w["sum_r"]).then_inc(loaded, 16)

            @block.scalar
            def _(act):
                for dg in range(4):
                    some = slice(4 * dg, 4 * dg + 4)
                    act.wait_ge(sel_in[dg], 16)
                    nc.scalar.activation(sel[:, some, :], sel_f[:, some, :], ACT.Identity).then_inc(sel_ready, 1)

                def sequences(i):
                    for cc in range(NC):
                        act.wait_ge(summed, i * UN + UN - NC + cc + 1)
                        nc.scalar.activation(k_g[:, ds(i * T + cc * GT, GT)], ps_y[:, cc, :],
                                             ACT.Identity).then_inc(y_done, 1)

                over_sequences(act, sequences)

            @block.gpsimd
            def _(pool):
                pool.wait_ge(loaded, 16)

                def sequences(i):
                    for u in range(4 * UN):
                        cc = u // 4 % NC
                        if u >= 8 or after_first(i):
                            pool.wait_ge(summed, i * UN + u // 4 - 1)
                        wait_apart(pool, (loaded, 16), (scanned, i * (4 * UN) + u + 1))
                        nc.gpsimd.tensor_tensor(qm[:, u % 8, :], mem[:, u % 8, :], q_r[:, ds(i * T + cc * GT, GT)],
                                                ALU.mult).then_inc(qm_done, 1)

                over_sequences(pool, sequences)

            @block.vector
            def _(dve):
                def sequences(i):
                    def times_v(u):
                        dve.wait_ge(spread, i * (4 * UN) + u + 1)
                        nc.vector.tensor_tensor(kv[:, u % 4, :], ps_v[:, u % 4, :],
                                                k_g[:, ds(i * T + u // 4 % NC * GT, GT)], ALU.mult).then_inc(kv_done, 1)

                    def scan(u):
                        dve.wait_ge(kv_done, i * (4 * UN) + u + 1)
                        if u >= 8 or after_first(i):
                            dve.wait_ge(qm_done, i * (4 * UN) + u - 7)
                        start = 0.0
                        if u // 4 % NC:
                            dve.wait_ge(scanned, i * (4 * UN) + u - 3)
                            start = mem[:, (u - 4) % 8, GT - 1:GT]
                        nc.vector.tensor_tensor_scan(mem[:, u % 8, :], decay[:, ds(i, 1)].to_broadcast([P, GT]),
                                                     kv[:, u % 4, :], start, ALU.mult, ALU.add).then_inc(scanned, 1)

                    times_v(0)
                    for u in range(4 * UN):
                        if u + 1 < 4 * UN:
                            times_v(u + 1)
                        scan(u)

                over_sequences(dve, sequences)

            @block.tensor
            def _(pe):
                pe.wait_ge(loaded, 16)

                def sequences(i):
                    def spread_v(u):
                        cc, d = u // 4 % NC, u // UN * 4 + u % 4
                        if u % UN == 0 and not after_first(i):
                            pe.wait_ge(sel_ready, u // UN + 1)
                        if u >= 4 or after_first(i):
                            pe.wait_ge(kv_done, i * (4 * UN) + u - 3)
                        for part in range(3):
                            last = nc.tensor.matmul(ps_v[:, u % 4, :], sel[:, d, :],
                                                    v_p[part][:, ds(i * T + cc * GT, GT)],
                                                    start=(part == 0), stop=(part == 2))
                        last.then_inc(spread, 1)

                    def sum_r(n, i=i):
                        cc, dg = n % NC, n // NC
                        pe.wait_ge(qm_done, i * (4 * UN) + n * 4 + 4)
                        if n < NC and after_first(i):
                            pe.wait_ge(y_done, (i - 1) * NC + n + 1)
                        for dd in range(4):
                            last = nc.tensor.matmul(ps_y[32 * dd:32 * dd + 32, cc, :], red[:, dg, :],
                                                    qm[:, (n * 4 + dd) % 8, :], start=(dg == 0), stop=(dg == 3))
                        last.then_inc(summed, 1)

                    for u in range(4 * UN):
                        spread_v(u)
                        if u % 4 == 3 and u >= 7:
                            sum_r(u // 4 - 1)
                        elif u == 3 and after_first(i):
                            sum_r(UN - 1, i - 1)
                    return sum_r

                over_sequences(pe, sequences)(UN - 1, 2 * B - 1)

        S.close()


def over_sequences(eng, body):
    body(0)
    with eng.Fori(1, 2 * B) as i:
        rest = body(i)
    return rest


def memory_out(nc, x, ident, consts, y, w):
    with ExitStack() as c:
        sb = lambda name, shape, dt=F32: c.enter_context(nc.sbuf_tensor("mo_" + name, shape, dt))
        w_out = sb("w_out", [P, 2, D])
        bc = sb("bc", [P, 3, D])
        y2 = sb("y2", [P, 2, 2, P])
        ln1, ln2 = TileLn(sb, "mo1"), TileLn(sb, "mo2")
        xb = sb("xb", [P, 2, D])
        zb = sb("zb", [P, 2, D])
        hres = sb("hres", [P, 2, D])
        ones_row = sb("ones_row", [P, P])
        t2 = sb("t2", [P, 2, D])
        ps_o = [c.enter_context(nc.psum_tensor(f"mo_po{i}", [P, 512], F32)) for i in range(2)]
        S = Sems(nc)
        loaded, y_copied, out_done, z_done, xb_done, h_done, d1, ones_set, x_done = (
            S(s) for s in ("loaded", "y_copied", "out_done", "z_done", "xb_done", "h_done", "d1", "ones_set", "x_done"))
        s1, s2 = LnSems(S, "ln1"), LnSems(S, "ln2")
        with nc.Block() as block:

            @block.sync
            def _(sp):
                sp.dma_start(w_out[:, :, :], w["out_w"]).then_inc(loaded, 16)
                for i, name in enumerate(("out_b", "ln_g", "ln_b")):
                    sp.dma_start(bc[:, i, :], w[name].to_broadcast([P, D])).then_inc(loaded, 16)

            @block.gpsimd
            def _(pool):
                nc.gpsimd.memset(ones_row[:, :], 0.0).then_inc(ones_set, 1)
                pool.wait_ge(ones_set, 1)
                nc.gpsimd.memset(ones_row[0:1, :], 1.0).then_inc(ones_set, 1)
                pool.wait_ge(loaded, 64)

                def add_bias(n, p):
                    wait_apart(pool, (loaded, 64), (x_done, n - 1))
                    nc.gpsimd.tensor_tensor(xb[:, p, :], x[:, ds(n * D, D)], bc[:, 2, :], ALU.add).then_inc(xb_done, 1)

                pipeline(NT, 2, [(0, lambda n, p: tile_scale(nc, pool, ln1, s1, consts, n, p)),
                                 (1, add_bias), (2, lambda n, p: tile_scale(nc, pool, ln2, s2, consts, n, p))])(pool)

            @block.scalar
            def _(act):
                def copy_y(n, p):
                    wait_reuse(act, out_done, n, 2)
                    for hf in range(2):
                        nc.scalar.activation(y2[:, p, hf, :], y[:, ds(n * P + hf * B * T, P)],
                                             ACT.Identity).then_inc(y_copied, 1)

                pipeline(NT, 2, [(0, copy_y)])(act)

            @block.tensor
            def _(pe):
                pe.wait_ge(loaded, 64)
                pe.wait_ge(ones_set, 2)

                def out(n, p):
                    pe.wait_ge(y_copied, n * 2 + 2)
                    wait_reuse(pe, h_done, n, 2)
                    for hf in range(2):
                        nc.tensor.matmul(ps_o[p][:, 0:D], y2[:, p, hf, :], w_out[:, hf, :],
                                                start=(hf == 0), stop=False)
                    nc.tensor.matmul(ps_o[p][:, 0:D], ones_row[:, :], bc[:, 0, :], start=False,
                                     stop=True).then_inc(out_done, 1)

                pipeline(NT, 2, [(0, out)])(pe)

            @block.vector
            def _(dve):
                dve.wait_ge(loaded, 64)

                def stats1(n, p):
                    nc.vector.bn_stats(ln1.parts[:, p, :], x[:, ds(n * D, D)]).then_inc(s1.parts, 1)

                def gather1(n, p):
                    tile_aggregate(nc, dve, ln1, s1, n, p)

                def normalise(n, p):
                    dve.wait_ge(s1.rstd, n + 1)
                    wait_reuse(dve, h_done, n, 2)
                    nc.vector.tensor_scalar(zb[:, p, :], x[:, ds(n * D, D)], ln1.mean_var[:, p, 0:1],
                                            ln1.rstd[:, p:p + 1], ALU.subtract, ALU.mult).then_inc(z_done, 1)

                def add_out(n, p):
                    dve.wait_ge(z_done, n + 1)
                    dve.wait_ge(out_done, n + 1)
                    wait_reuse(dve, d1, n, 2)
                    nc.vector.tensor_tensor(hres[:, p, :], ps_o[p][:, 0:D], zb[:, p, :], ALU.add).then_inc(h_done, 1)

                def stats2(n, p):
                    dve.wait_ge(h_done, n + 1)
                    nc.vector.bn_stats(ln2.parts[:, p, :], hres[:, p, :]).then_inc(s2.parts, 1)

                def gather2(n, p):
                    tile_aggregate(nc, dve, ln2, s2, n, p)

                def scale(n, p):
                    dve.wait_ge(s2.rstd, n + 1)
                    nc.vector.scalar_tensor_tensor(t2[:, p, :], hres[:, p, :], ln2.mean_var[:, p, 0:1], bc[:, 1, :],
                                                   ALU.subtract, ALU.mult).then_inc(d1, 1)

                def add_ln(n, p):
                    dve.wait_ge(d1, n + 1)
                    dve.wait_ge(xb_done, n + 1)
                    nc.vector.scalar_tensor_tensor(x[:, ds(n * D, D)], t2[:, p, :], ln2.rstd[:, p:p + 1], xb[:, p, :],
                                                   ALU.mult, ALU.add).then_inc(x_done, 1)

                pipeline(NT, 2, [(2, add_out), (0, stats1), (2, stats2), (0, gather1), (3, scale), (1, normalise),
                                 (2, gather2), (3, add_ln)])(dve)

        S.close()


class TileLn:

    def __init__(self, sb, name):
        self.parts = sb(f"{name}_parts", [P, 2, 6])
        self.mean_var = sb(f"{name}_mv", [P, 2, 2])
        self.var_eps = sb(f"{name}_ve", [P, 2])
        self.rstd = sb(f"{name}_rstd", [P, 2])


def tile_aggregate(nc, dve, b, s, n, p):
    wait_apart(dve, (s.parts, 1), (s.parts, n + 1))
    nc.vector.bn_aggr(b.mean_var[:, p, :], b.parts[:, p, :]).then_inc(s.mean_var, 1)


def tile_scale(nc, pool, b, s, consts, n, p):
    pool.wait_ge(s.mean_var, n + 1)
    nc.gpsimd.tensor_tensor(b.var_eps[:, p:p + 1], b.mean_var[:, p, 1:2], consts[:, 1, 0:1],
                            ALU.add).then_inc(s.var_eps, 1)
    pool.wait_ge(s.var_eps, n + 1)
    nc.gpsimd.tensor_tensor(b.rstd[:, p:p + 1], b.var_eps[:, p:p + 1], consts[:, 0, 0:1],
                            ALU.pow).then_inc(s.rstd, 1)


HL, DL = 8, 64
SLOTS = WT + 1


def at_inner(n, u):
    return n * (D // 2) + (u % 2) * (SLOTS * D - D // 2) + D


def local_transformer(nc, x, ident, consts, w, store=None):
    with ExitStack() as c:
        inner = c.enter_context(nc.sbuf_tensor(f"inner_{Sems.phases}", [P, B * SLOTS * D], F32))
        enter_inner(nc, x, inner, consts)
        for layer in range(2):
            window_attention(nc, inner, ident, consts, w, layer)
            gated_mlp(nc, inner, ident, consts, w, layer)
        S = Sems(nc)
        added, stored = S("added"), S("stored")
        with nc.Block() as block:

            @block.sync
            def _(sp):
                if store is not None:
                    for n in range(NG):
                        sp.wait_ge(added, n + 1)
                        sp.dma_start(store[:, n * G:(n + 1) * G, :], x[:, n * G * D:(n + 1) * G * D].rearrange(
                            "p (n d) -> p n d", d=D)).then_inc(stored, 16)
                    sp.wait_ge(stored, 16 * NG)

            @block.vector
            def _(dve):
                for b in range(B):
                    for q in range(4):
                        xs = x[:, (b * 4 + q) * G * D:(b * 4 + q + 1) * G * D]
                        at = (b * SLOTS + 1 + q * G) * D
                        nc.vector.scalar_tensor_tensor(xs, inner[:, at:at + G * D], 0.5, xs, ALU.mult,
                                                       ALU.add).then_inc(added, 1)

        S.close()


def enter_inner(nc, x, inner, consts):
    with ExitStack() as c:
        ln = LnBuffers(lambda name, shape: c.enter_context(nc.sbuf_tensor(name, shape, F32)), f"in{Sems.phases}")
        minus_mean = c.enter_context(nc.sbuf_tensor(f"in{Sems.phases}_minus_mean", [P, 2, G], F32))
        shift = c.enter_context(nc.sbuf_tensor(f"in{Sems.phases}_shift", [P, NG, G], F32))
        S = Sems(nc)
        s = LnSems(S)
        neg_done, shift_ready, z_done = S("neg_done"), S("shift_ready"), S("z_done")
        with nc.Block() as block:

            @block.gpsimd
            def _(pool):
                for b in range(B):
                    nc.gpsimd.memset(inner[:, b * SLOTS * D:(b * SLOTS + 1) * D], 0.0)

                def scale(n, p):
                    wait_reuse(pool, z_done, n, 2, G)
                    ln_scale(nc, pool, ln, s, consts, n, p)
                    nc.gpsimd.tensor_tensor(minus_mean[:, p, :], ln.mean_var[:, p, :, 0], consts[:, 2, 0:G],
                                            ALU.mult).then_inc(neg_done, 1)
                    pool.wait_ge(s.rstd, n + 1)
                    pool.wait_ge(neg_done, n + 1)
                    nc.gpsimd.tensor_tensor(shift[:, n, :], minus_mean[:, p, :], ln.rstd[:, p, :],
                                            ALU.mult).then_inc(shift_ready, 1)

                for n in range(NG):
                    scale(n, n % 2)

            @block.scalar
            def _(act):
                for n in range(NG):
                    act.wait_ge(shift_ready, n + 1)
                    for j in range(G):
                        at = (n * G + j + 1 + n // (NG // B)) * D
                        nc.scalar.activation(inner[:, at:at + D], x[:, (n * G + j) * D:(n * G + j + 1) * D], ACT.Identity,
                                             scale=ln.rstd[:, n % 2, j:j + 1], bias=shift[:, n, j:j + 1]).then_inc(z_done, 1)

            @block.vector
            def _(dve):
                for n in range(NG):
                    wait_reuse(dve, shift_ready, n, 2)
                    ln_stats(nc, dve, ln, s, x, n, n % 2)

        S.close()


def bank_free(pe, users, i, unit, units):
    for back in range(1, len(users) + 1):
        k = (i - back) % len(users)
        sem, per, nth, lag = users[k]
        other = unit + (users[i][3] - lag) - (1 if back > i else 0)
        if isinstance(unit, int):
            other = min(other, units - 1)
            if other >= 0:
                pe.wait_ge(sem, other * per + nth)
        else:
            pe.wait_ge(sem, other * per + nth)
            return


def window_attention(nc, inner, ident, consts, w, layer):
    L_TURN, L_PROJ, L_QK, L_ATT, L_OUT, L_WO = 0, 1, 2, 3, 4, 5
    tag = f"wa{Sems.phases}_"
    IN = HL * DL
    with ExitStack() as c:
        sb = lambda name, shape, dt=F32: c.enter_context(nc.sbuf_tensor(tag + name, shape, dt))
        wqkv = [sb(f"wqkv_{part}", [P, KD * 3 * IN], F32R) for part in ("high", "low")]
        wo = [sb(f"wo_{part}", [P, 4 * D], F32R) for part in ("high", "low")]
        table = sb("table", [P, WT, 2, 2 * DL])
        scales = sb("scales", [P, 2, 2 * DL])
        mask = sb("mask", [P, 3, 2 * P])
        h = sb("h", [P, 2, D])
        hT = [sb(f"hT_{part}", [P, 4, KD, P + 4], F32R) for part in ("high", "low")]
        squares = sb("squares", [P, 2, IN])
        ss = sb("ss", [P, 2, 16])
        ssm = sb("ssm", [P, 2, 16])
        rn = sb("rn", [P, 2, 16])
        by_cos = sb("by_cos", [P, 2, IN])
        by_sin = sb("by_sin", [P, 2, IN])
        turned = sb("turned", [P, 2, IN])
        qk = sb("qk", [P, 2, 2, IN])
        v_new = sb("v_new", [P, 2, IN])
        v = sb("v", [P, 4, IN])
        qT = sb("qT", [P, 2, 4, P])
        kT = sb("kT", [P, 2, HL, 2, P])
        sm = sb("sm", [P, 4, 2 * P])
        mx = sb("mx", [P, 2, HL])
        nmx = sb("nmx", [P, 2, HL])
        sums = sb("sums", [P, 2, HL])
        rsum = sb("rsum", [P, 2, HL])
        pr = sb("pr", [P, 4, 2 * P])
        pT = sb("pT", [P, 2, 4, P])
        o = sb("o", [P, 2, IN])
        oT = [sb("oT_high", [P, 2, 4, P], F32R), sb("oT_low", [P, 1, 4, P], F32R)]
        bank = [c.enter_context(nc.psum_tensor(f"{tag}bank{i}", [P, 512], F32)) for i in range(3)]
        ps_qk = c.enter_context(nc.psum_tensor(f"{tag}ps_qk", [P, 2, 512], F32))
        ps_vo = c.enter_context(nc.psum_tensor(f"{tag}ps_vo", [P, 512], F32))
        ps_s = [c.enter_context(nc.psum_tensor(f"{tag}ps_s{i}", [P, 2, 256], F32)) for i in range(2)]

        S = Sems(nc)
        loaded, cleared, table_done = S("loaded"), S("cleared"), S("table_done")
        w_in, w_high, w_low = [S(f"w_in{i}") for i in range(4)], S("w_high"), S("w_low")
        hT_low, oT_low = S("hT_low"), S("oT_low")
        arrive = [a[:, :, :].rearrange("p i d -> p (i d)") for a in (by_cos, by_sin, turned, squares)]
        cuts = [[wqkv[i][:, 2 * IN * m:2 * IN * (m + 1)] for m in range(3)] + [wo[i][:, :]] for i in range(2)]
        h_ready, h_turned, hT_ready = S("h_ready"), S("h_turned"), S("hT_ready")
        q_done, k_done, v_done, v_copied, v_ready = S("q_done"), S("k_done"), S("v_done"), S("v_copied"), S("v_ready")
        squared, ss_done, ss_max, rn_ready = S("squared"), S("ss_done"), S("ss_max"), S("rn_ready")
        cos_done, sin_done, sum_done, qk_ready = S("cos_done"), S("sin_done"), S("sum_done"), S("qk_ready")
        q_turned, k_turned, qT_ready, kT_ready = S("q_turned"), S("k_turned"), S("qT_ready"), S("kT_ready")
        s_done, max_done, nmx_ready, p_ready = S("s_done"), S("max_done"), S("nmx_ready"), S("p_ready")
        p_turned, pT_even, pT_odd, pv_done = S("p_turned"), S("pT_even"), S("pT_odd"), S("pv_done")
        rsum_ready, o_ready, o_turned, oT_ready = S("rsum_ready"), S("o_ready"), S("o_turned"), S("oT_ready")
        wo_done, inner_done = S("wo_done"), S("inner_done")
        T = [(pT_even, 2, 1, L_ATT), (pT_odd, 2, 1, L_ATT), (pT_even, 2, 2, L_ATT), (pT_odd, 2, 2, L_ATT)]
        users = [[T[0], T[2], (qT_ready, 1, 1, L_QK)], [T[1], (inner_done, 1, 1, L_WO), (kT_ready, 2, 2, L_QK)],
                 [(hT_low, 2, 2, L_TURN), T[3], (oT_low, 1, 1, L_OUT)]]
        free = lambda pe, b, i, n: bank_free(pe, users[b], i, n, NT)

        with nc.Block() as block:

            @block.sync
            def _(sp):
                flat_w = w["wqkv"][layer].rearrange("p k n -> p (k n)")
                for m in range(4):
                    src = w["wo"][layer].rearrange("p j d -> p (j d)") if m == 3 else flat_w[:, 2 * IN * m:2 * IN * (m + 1)]
                    sp.dma_start(arrive[m], src).then_inc(w_in[m], 16)
                for dst, src in ((table[:, :, :, :], w["table"]), (mask[:, :, :], w["mask"]),
                                 (scales[:, :, :], w["scales"][layer].to_broadcast([P, 2, 2 * DL]))):
                    sp.dma_start(dst, src).then_inc(loaded, 16)

            @block.gpsimd
            def _(pool):
                for part in hT:
                    nc.gpsimd.memset(part[:, :, :, :].bitcast(F32), 0.0).then_inc(cleared, 1)
                nc.gpsimd.memset(kT[:, :, :, :, :], 0.0).then_inc(cleared, 1)
                nc.gpsimd.memset(v[:, :, :], 0.0).then_inc(cleared, 1)
                pool.wait_ge(cleared, 4)

                def copy_h(n, u):
                    wait_reuse(pool, h_turned, n, 2)
                    nc.gpsimd.tensor_copy(h[:, u % 2, :], inner[:, ds(at_inner(n, u), D)]).then_inc(h_ready, 1)

                def norms(n, u):
                    wait_apart(pool, (cleared, 4), (ss_done, n + 1), (qk_ready, n - 1))
                    nc.gpsimd.tensor_scalar(ssm[:, u % 2, :], ss[:, u % 2, :], 1e-24, None,
                                            ALU.max).then_inc(ss_max, 1)
                    pool.wait_ge(ss_max, n + 1)
                    nc.gpsimd.tensor_tensor(rn[:, u % 2, :], ssm[:, u % 2, :], consts[:, 0, :],
                                            ALU.pow).then_inc(rn_ready, 1)

                def add_turned(n, u):
                    pool.wait_ge(sin_done, n * 2 + 2)
                    wait_reuse(pool, qk_ready, n, 1)
                    nc.gpsimd.tensor_tensor(turned[:, :, :], by_cos[:, :, :], by_sin[:, :, :],
                                            ALU.add).then_inc(sum_done, 1)

                def place_v(n, u):
                    wait_apart(pool, (cleared, 4), (v_copied, n + 1), (pv_done, (n - 1) * 4))
                    nc.gpsimd.tensor_copy(v[:, u, :], v_new[:, u % 2, :]).then_inc(v_ready, 1)

                pipeline(NT, 4, [(L_TURN, copy_h), (L_QK, place_v), (L_PROJ, norms), (L_PROJ, add_turned)], 4)(pool)

            @block.scalar
            def _(act):
                for m in range(4):
                    act.wait_ge(w_in[m], 16)
                    nc.scalar.activation(cuts[0][m], arrive[m], ACT.Identity).then_inc(w_high, 1)
                act.wait_ge(cleared, 4)

                def turned_h(n, u):
                    wait_reuse(act, k_done, n, 2)
                    act.wait_ge(h_turned, n + 1)
                    nc.scalar.activation(hT[0][:, u, :, 1:P + 1], bank[2][:, 0:D].rearrange("p (k t) -> p k t", k=KD),
                                         ACT.Identity).then_inc(hT_ready, 1)
                    nc.scalar.activation(hT[0][:, (u + 2) % 4, 1, 0:1], bank[2][:, 2 * P - 1:2 * P],
                                         ACT.Identity).then_inc(hT_ready, 1)

                def copy_v(n, u):
                    act.wait_ge(v_done, n + 1)
                    wait_reuse(act, v_ready, n, 2)
                    nc.scalar.activation(v_new[:, u % 2, :], ps_vo[:, :], ACT.Identity).then_inc(v_copied, 1)

                def square(i, done):
                    def stage(n, u):
                        if isinstance(n, int) and n == 0:
                            act.wait_ge(w_low, 4)
                        wait_reuse(act, ss_done, n, 1)
                        act.wait_ge(done, n + 1)
                        nc.scalar.activation(squares[:, i, :], ps_qk[:, i, :], ACT.Square).then_inc(squared, 1)
                    return stage

                def turned_qk(n, u):
                    act.wait_ge(q_turned, n + 1)
                    wait_reuse(act, s_done, n, 2, 4)
                    nc.scalar.activation(qT[:, u % 2, :, :], bank[0][:, :].rearrange("p (j t) -> p j t", j=4),
                                         ACT.Identity).then_inc(qT_ready, 1)
                    act.wait_ge(k_turned, n + 1)
                    for e in range(2):
                        rows = slice(64 * e, 64 * e + 64)
                        nc.scalar.activation(kT[rows, u % 2, e:HL:2, u // 2, :],
                                             bank[1][rows, :].rearrange("p (j t) -> p j t", j=4),
                                             ACT.Identity).then_inc(kT_ready, 1)

                def exp_of(j):
                    def stage(n, u):
                        act.wait_ge(nmx_ready, n * 4 + j + 1)
                        if j >= 2:
                            act.wait_ge(p_turned, n * 4 + j - 1)
                        else:
                            wait_reuse(act, p_turned, n, 1, 4)
                        for e in range(2):
                            hd = 2 * j + e
                            nc.scalar.activation(pr[:, hd % 4, :], sm[:, hd % 4, :], ACT.Exp,
                                                 bias=nmx[:, u % 2, hd:hd + 1],
                                                 accum_out=sums[:, u % 2, hd:hd + 1]).then_inc(p_ready, 1)
                    return stage

                def p_out(j):
                    def stage(n, u):
                        act.wait_ge(p_turned, n * 4 + j + 1)
                        if j >= 2:
                            act.wait_ge(pv_done, n * 4 + j - 1)
                        else:
                            wait_reuse(act, pv_done, n, 1, 4)
                        nc.scalar.activation(pT[:, j % 2, :, :], bank[(0, 1, 0, 2)[j]][:, :].rearrange(
                            "p (j t) -> p j t", j=4), ACT.Identity).then_inc(pT_odd if j % 2 else pT_even, 1)
                    return stage

                def turned_o(n, u):
                    act.wait_ge(o_turned, n + 1)
                    wait_reuse(act, wo_done, n, 2)
                    nc.scalar.activation(oT[0][:, u % 2, :, :], bank[2][:, :].rearrange("p (j t) -> p j t", j=4),
                                         ACT.Identity).then_inc(oT_ready, 1)

                pipeline(NT, 4, [(L_ATT, exp_of(0)), (L_PROJ, square(0, q_done)), (L_ATT, exp_of(1)), (L_PROJ, copy_v),
                                 (L_ATT, exp_of(2)), (L_PROJ, square(1, k_done)), (L_ATT, p_out(1)),
                                 (L_TURN, turned_h), (L_ATT, p_out(2)), (L_ATT, exp_of(3)), (L_ATT, p_out(3)), (L_QK, turned_qk),
                                 (L_OUT, turned_o)], 4)(act)

            @block.vector
            def _(dve):
                for m in range(4):
                    dve.wait_ge(w_high, m + 1)
                    nc.vector.tensor_tensor(cuts[1][m], arrive[m], cuts[0][m], ALU.subtract).then_inc(w_low, 1)
                dve.wait_ge(w_low, 4)
                flat = table[:, :, :, :].rearrange("p w c d -> p (w c d)")

                def h_low(n, u):
                    dve.wait_ge(hT_ready, n * 2 + 2)
                    nc.vector.tensor_tensor(hT[1][:, u, :, 1:P + 1], bank[2][:, 0:D].rearrange("p (k t) -> p k t", k=KD),
                                            hT[0][:, u, :, 1:P + 1], ALU.subtract).then_inc(hT_low, 1)
                    nc.vector.tensor_tensor(hT[1][:, (u + 2) % 4, 1, 0:1], bank[2][:, 2 * P - 1:2 * P],
                                            hT[0][:, (u + 2) % 4, 1, 0:1], ALU.subtract).then_inc(hT_low, 1)

                def o_low(n, u):
                    dve.wait_ge(oT_ready, n + 1)
                    wait_reuse(dve, wo_done, n, 1)
                    nc.vector.tensor_tensor(oT[1][:, 0, :, :], bank[2][:, :].rearrange("p (j t) -> p j t", j=4),
                                            oT[0][:, u % 2, :, :], ALU.subtract).then_inc(oT_low, 1)

                def scale_table(n, u):
                    if isinstance(n, int) and n == 0:
                        dve.wait_ge(loaded, 48)
                        by_window = table[:, :, :, :].rearrange("p w c d -> p w (c d)")
                        nc.vector.tensor_tensor(
                            by_window, by_window,
                            scales[:, :, :].rearrange("p c d -> p (c d)").unsqueeze(1).to_broadcast([P, WT, 4 * DL]),
                            ALU.mult).then_inc(table_done, 1)
                        dve.wait_ge(table_done, 1)

                def rotate(i):
                    def stage(n, u):
                        row = n * (2 * DL) - (u % 2) * (2 * DL)
                        heads = lambda a: a.rearrange("p (h d) -> p h d", h=HL)
                        halves = lambda a: a.rearrange("p (h e d) -> p h e d", h=HL, e=2)
                        wait_reuse(dve, sum_done, n, 1)
                        dve.wait_ge(squared, n * 2 + i + 1)
                        cos = flat[:, ds(row + i * DL, DL)].unsqueeze(1).to_broadcast([P, HL, DL])
                        nc.vector.tensor_tensor(heads(by_cos[:, i, :]), heads(ps_qk[:, i, :]), cos,
                                                ALU.mult).then_inc(cos_done, 1)
                        sin = flat[:, ds(row + 2 * DL + i * DL, DL)].rearrange("p (e d) -> p e d", e=2)
                        for e in range(2):
                            op = nc.vector.tensor_tensor(
                                halves(by_sin[:, i, :])[:, :, e, :], halves(ps_qk[:, i, :])[:, :, 1 - e, :],
                                sin[:, e, :].unsqueeze(1).to_broadcast([P, HL, DL // 2]), ALU.mult)
                        op.then_inc(sin_done, 1)
                    return stage

                def sum_squares(n, u):
                    dve.wait_ge(squared, n * 2 + 2)
                    wait_reuse(dve, ss_max, n, 2)
                    nc.vector.reduce_sum(ss[:, u % 2, :], squares[:, :, :].rearrange("p i (h d) -> p (i h) d", h=HL),
                                         AX_X).then_inc(ss_done, 1)

                def scale_qk(n, u):
                    dve.wait_ge(rn_ready, n + 1)
                    dve.wait_ge(sum_done, n + 1)
                    wait_reuse(dve, k_turned, n, 2)
                    nc.vector.tensor_tensor(
                        qk[:, u % 2, :, :].rearrange("p i (h d) -> p (i h) d", h=HL),
                        turned[:, :, :].rearrange("p i (h d) -> p (i h) d", h=HL),
                        rn[:, u % 2, :].unsqueeze(2).to_broadcast([P, 2 * HL, DL]), ALU.mult).then_inc(qk_ready, 1)

                def mask_max(j):
                    def stage(n, u):
                        which = 2 if isinstance(n, int) and n < B else u // 2
                        wait_apart(dve, (loaded, 48), (s_done, n * 4 + j + 1),
                                   (p_ready, n * 8 + (2 * j - 2 if j >= 2 else 0)))
                        for e in range(2):
                            hd = 2 * j + e
                            nc.vector.tensor_tensor_reduce(out=sm[:, hd % 4, :], in0=ps_s[j % 2][:, e, :],
                                                           in1=mask[:, which, :], scale=1.0, scalar=-3.4e38,
                                                           op0=ALU.add, op1=ALU.max,
                                                           accum_out=mx[:, u % 2, hd:hd + 1]).then_inc(max_done, 1)
                        dve.wait_ge(max_done, n * 8 + 2 * j + 2)
                        nc.vector.tensor_scalar(nmx[:, u % 2, 2 * j:2 * j + 2], mx[:, u % 2, 2 * j:2 * j + 2], -1.0,
                                                None, ALU.mult).then_inc(nmx_ready, 1)
                    return stage

                def p_out(n, u):
                    dve.wait_ge(p_turned, n * 4 + 1)
                    wait_reuse(dve, pv_done, n, 1, 4)
                    nc.vector.tensor_copy(pT[:, 0, :, :], bank[0][:, :].rearrange("p (j t) -> p j t",
                                                                                 j=4)).then_inc(pT_even, 1)

                def o_out(n, u):
                    dve.wait_ge(p_ready, n * 8 + 8)
                    nc.vector.reciprocal(rsum[:, u % 2, :], sums[:, u % 2, :]).then_inc(rsum_ready, 1)
                    dve.wait_ge(rsum_ready, n + 1)
                    dve.wait_ge(pv_done, n * 4 + 4)
                    wait_reuse(dve, o_turned, n, 2)
                    nc.vector.tensor_tensor(o[:, u % 2, :].rearrange("p (h d) -> p h d", h=HL),
                                            ps_vo[:, :].rearrange("p (h d) -> p h d", h=HL),
                                            rsum[:, u % 2, :].unsqueeze(2).to_broadcast([P, HL, DL]),
                                            ALU.mult).then_inc(o_ready, 1)

                def residual(n, u):
                    here = inner[:, ds(at_inner(n, u), D)]
                    dve.wait_ge(wo_done, n + 1)
                    nc.vector.tensor_tensor(here, bank[1][:, 0:D], here, ALU.add).then_inc(inner_done, 1)

                pipeline(NT, 4, [(L_ATT, mask_max(0)), (L_WO, o_low), (L_ATT, mask_max(1)), (L_ATT, p_out),
                                 (L_ATT, mask_max(2)), (L_QK, scale_qk), (L_PROJ, scale_table), (L_PROJ, rotate(0)), (L_PROJ, rotate(1)),
                                 (L_ATT, mask_max(3)), (L_TURN, h_low), (L_PROJ, sum_squares),
                                 (L_WO, residual), (L_ATT, o_out)], 4)(dve)

            @block.tensor
            def _(pe):
                pe.wait_ge(cleared, 4)

                def turn_h(n, u):
                    pe.wait_ge(h_ready, n + 1)
                    free(pe, 2, 0, n)
                    for k in range(KD):
                        last = nc.tensor.transpose(bank[2][:, k * P:(k + 1) * P], h[:, u % 2, k * P:(k + 1) * P],
                                                   ident[:, :])
                    last.then_inc(h_turned, 1)

                def project(i, done):
                    def stage(n, u):
                        if isinstance(n, int) and n == 0:
                            pe.wait_ge(w_low, 4)
                        if i == 0:
                            pe.wait_ge(hT_low, n * 2 + 2)
                        if i == 2:
                            if isinstance(n, int):
                                if n >= 3:
                                    pe.wait_ge(o_ready, min(n - 2, NT))
                            else:
                                pe.wait_ge(o_ready, n - 2)
                        else:
                            wait_reuse(pe, cos_done, n, 1, 2)
                            wait_reuse(pe, sin_done, n, 1, 2)
                            wait_reuse(pe, squared, n, 1, 2)
                        out = ps_vo[:, :] if i == 2 else ps_qk[:, i, :]
                        add_products(nc, out, [
                            (hT[a][:, u, k, 1 - k:1 - k + P], wqkv[b][:, (3 * k + i) * IN:(3 * k + i + 1) * IN])
                            for k in range(KD) for a, b in PARTS_OF]).then_inc(done, 1)
                    return stage

                def turn_qk(i, b, done):
                    def stage(n, u):
                        pe.wait_ge(qk_ready, n + 1)
                        free(pe, b, 2, n)
                        for j in range(4):
                            last = nc.tensor.transpose(bank[b][:, j * P:(j + 1) * P],
                                                       qk[:, u % 2, i, j * P:(j + 1) * P], ident[:, :])
                        last.then_inc(done, 1)
                    return stage

                def scores(j):
                    def stage(n, u):
                        if j == 0:
                            pe.wait_ge(kT_ready, n * 2 + 2)
                            pe.wait_ge(qT_ready, n + 1)
                        if j >= 2:
                            pe.wait_ge(max_done, n * 8 + 2 * j - 2)
                        else:
                            wait_reuse(pe, max_done, n, 1, 8)
                        for e in range(2):
                            keys = kT[:, u % 2, 2 * j + e, :, :].rearrange("p s t -> p (s t)")
                            last = nc.tensor.matmul(ps_s[j % 2][:, e, :], qT[:, u % 2, j, :], keys,
                                                    start=True, stop=True)
                        last.then_inc(s_done, 1)
                    return stage

                def turn_p(j, b, i):
                    def stage(n, u):
                        pe.wait_ge(p_ready, n * 8 + 2 * j + 2)
                        free(pe, b, i, n)
                        for e in range(2):
                            for blk in range(2):
                                at = (2 * e + blk) * P
                                last = nc.tensor.transpose(bank[b][:, at:at + P],
                                                           pr[:, (2 * j + e) % 4, blk * P:(blk + 1) * P], ident[:, :])
                        last.then_inc(p_turned, 1)
                    return stage

                def weigh(j):
                    def stage(n, u):
                        if j == 0:
                            pe.wait_ge(v_ready, n + 1)
                            pe.wait_ge(v_copied, min(n + 3, NT) if isinstance(n, int) else n + 3)
                        pe.wait_ge(pT_odd if j % 2 else pT_even, n * 2 + j // 2 + 1)
                        for e in range(2):
                            hd = 2 * j + e
                            for slot in range(2):
                                vals = v[:, (u % 2) + 2 * slot, hd * DL:(hd + 1) * DL]
                                last = nc.tensor.matmul(ps_vo[:, hd * DL:(hd + 1) * DL], pT[:, j % 2, 2 * e + slot, :],
                                                        vals, start=(slot == 0), stop=(slot == 1))
                        last.then_inc(pv_done, 1)
                    return stage

                def turn_o(n, u):
                    pe.wait_ge(o_ready, n + 1)
                    free(pe, 2, 2, n)
                    for j in range(4):
                        last = nc.tensor.transpose(bank[2][:, j * P:(j + 1) * P], o[:, u % 2, j * P:(j + 1) * P],
                                                   ident[:, :])
                    last.then_inc(o_turned, 1)

                def times_wo(n, u):
                    pe.wait_ge(oT_low, n + 1)
                    free(pe, 1, 1, n)
                    add_products(nc, bank[1][:, 0:D], [
                        (oT[a][:, u % 2 if a == 0 else 0, j, :], wo[b][:, j * D:(j + 1) * D])
                        for j in range(4) for a, b in PARTS_OF]).then_inc(wo_done, 1)

                pipeline(NT, 4, [
                    (L_ATT, scores(0)), (L_PROJ, project(0, q_done)), (L_ATT, scores(1)), (L_PROJ, project(2, v_done)),
                    (L_ATT, turn_p(0, 0, 0)), (L_ATT, scores(2)), (L_PROJ, project(1, k_done)), (L_ATT, weigh(0)),
                    (L_ATT, turn_p(1, 1, 0)), (L_ATT, scores(3)), (L_TURN, turn_h), (L_ATT, weigh(1)),
                    (L_ATT, turn_p(2, 0, 1)), (L_WO, times_wo), (L_ATT, weigh(2)), (L_ATT, turn_p(3, 2, 1)),
                    (L_QK, turn_qk(0, 0, q_turned)), (L_QK, turn_qk(1, 1, k_turned)), (L_ATT, weigh(3)),
                    (L_OUT, turn_o)], 4)(pe)

        S.close()


PARTS_OF = ((0, 0), (0, 1), (1, 0))


def add_products(nc, out, pairs):
    for i, (lhs, rhs) in enumerate(pairs):
        last = nc.tensor.matmul(out, lhs, rhs, start=(i == 0), stop=(i == len(pairs) - 1))
    return last


def gated_mlp(nc, inner, ident, consts, w, layer):
    MT = 6
    HID = 682
    LAST = HID - (MT - 1) * P
    RING = MT + MT // 2
    tag = f"gm{Sems.phases}_"
    with ExitStack() as c:
        sb = lambda name, shape, dt=F32: c.enter_context(nc.sbuf_tensor(tag + name, shape, dt))
        ps = lambda name, n: c.enter_context(nc.psum_tensor(tag + "ps_" + name, [P, n, 512], F32))
        stage = sb("stage", [P, KD, 2 * MT * P])
        w1 = [sb(f"w1_{part}", [P, KD, 2 * MT * P], F32R) for part in ("high", "low")]
        w2 = [sb(f"w2_{part}", [P, MT * D], F32R) for part in ("high", "low")]
        cols = sb("cols", [P, 2 * KD + 2 * MT])
        late = sb("late", [P, B * WT * P])
        parts = sb("parts", [P, 2, G, 12])
        ln = LnBuffers(sb, "mlp")
        z = sb("z", [P, 2, G, D])
        zT = sb("zT", [P, KD, GT])
        zT_cut = [sb(f"zT_{part}", [P, 2, KD, GT], F32R) for part in ("high", "low")]
        gelu = sb("gelu", [P, 2, GT])
        u_ = sb("u", [P, 4, GT])
        u_cut = [sb(f"u_{part}", [P, RING, GT], F32R) for part in ("high", "low")]
        ps_t, ps_g, ps_a, ps_o = ps("t", KD), ps("g", 2), ps("a", 2), ps("o", 2)
        S = Sems(nc)
        w1_in, w2_in, cols_in = [S("w1_in0"), S("w1_in1")], S("w2_in"), S("cols_in")
        w_high, w_low = S("w_high"), S("w_low")
        shifted, ones_set = [S("shifted0"), S("shifted1")], S("ones_set")
        z_high, z_low, u_high, u_low = S("z_high"), S("z_low"), S("u_high"), S("u_low")
        s = LnSems(S)
        z_ready, z_turned, zT_ready = S("z_ready"), S("z_turned"), S("zT_ready")
        g_done, a_done, gelu_ready, u_ready = S("g_done"), S("a_done"), S("gelu_ready"), S("u_ready")
        out_done, inner_done = S("out_done"), S("inner_done")
        ring = lambda n, m: (n * MT + m) % RING
        u_slot = lambda m: m % 3 if m < MT - 1 else 3
        at = lambda n, j: ((n // 4) * SLOTS + 1 + (n % 4) * G + j) * D
        with nc.Block() as block:

            @block.sync
            def _(sp):
                tiles = inner[:, :].rearrange("p (b s d) -> p b s d", b=B, s=SLOTS)
                to = late[:, :].rearrange("p (b s d) -> p b s d", b=B, s=WT)
                for b in range(B):
                    sp.dma_start(to[1:P, b, :, :], tiles[0:P - 1, b, 1:, P:D]).then_inc(shifted[b], 16)
                    sp.dma_start(to[0:1, b, :, :], tiles[P - 1:P, b, 0:WT, P:D]).then_inc(shifted[b], 16)
                    if b == 0:
                        sp.dma_start(cols[:, :], w["mlp_cols"][layer]).then_inc(cols_in, 16)
                        for k in range(KD):
                            sp.dma_start(stage[:, k, :].rearrange("p (i m) -> p i m", i=2),
                                         w["w1"][layer][:, k, :, :]).then_inc(w1_in[k], 16)
                sp.wait_ge(w_low, 1)
                sp.dma_start(stage[:, 0, :].rearrange("p (m d) -> p m d", d=D), w["w2"][layer]).then_inc(w2_in, 16)

            @block.gpsimd
            def _(pool):
                nc.gpsimd.memset(u_[:, 3, :], 1.0).then_inc(ones_set, 1)
                pipeline(NG, 2, [(0, lambda n, p: ln_scale(nc, pool, ln, s, consts, n, p))], NG)(pool)

            @block.vector
            def _(dve):
                dve.wait_ge(cols_in, 16)
                dve.wait_ge(ones_set, 1)

                def cut_w1(n, p):
                    if n == 0:
                        for k in range(KD):
                            dve.wait_ge(w_high, k + 1)
                            nc.vector.tensor_tensor(w1[1][:, k, :], stage[:, k, :], w1[0][:, k, :],
                                                    ALU.subtract).then_inc(w_low, 1)

                def cut_w2(n, p):
                    if n == 0:
                        dve.wait_ge(w_high, KD + 1)
                        nc.vector.tensor_tensor(w2[1][:, :], stage[:, 0, :], w2[0][:, :], ALU.subtract).then_inc(w_low, 1)

                def cut_z(n, p):
                    for k in range(KD):
                        dve.wait_ge(z_high, n * KD + k + 1)
                        nc.vector.tensor_tensor(zT_cut[1][:, p, k, :], zT[:, k, :], zT_cut[0][:, p, k, :],
                                                ALU.subtract).then_inc(z_low, 1)

                def stats(n, p):
                    dve.wait_ge(shifted[n // 4], 32)
                    for j in range(G):
                        for half, src in enumerate((inner[:, at(n, j):at(n, j) + P],
                                                    late[:, (n * G + j) * P:(n * G + j + 1) * P])):
                            nc.vector.bn_stats(parts[:, p, j, 6 * half:6 * half + 6], src).then_inc(s.parts, 1)
                    dve.wait_ge(s.parts, n * 2 * G + 2 * G)
                    for j in range(G):
                        nc.vector.bn_aggr(ln.mean_var[:, p, j, :], parts[:, p, j, :]).then_inc(s.mean_var, 1)

                def normalise(n, p):
                    wait_reuse(dve, z_turned, n, 2)
                    dve.wait_ge(s.rstd, n + 1)
                    for j in range(G):
                        for half, src in enumerate((inner[:, at(n, j):at(n, j) + P],
                                                    late[:, (n * G + j) * P:(n * G + j + 1) * P])):
                            nc.vector.tensor_scalar(z[:, p, j, half * P:half * P + P], src,
                                                    ln.mean_var[:, p, j, 0:1], ln.rstd[:, p, j:j + 1],
                                                    ALU.subtract, ALU.mult).then_inc(z_ready, 1)

                def gate(first, last):
                    def stage(n, p):
                        for m in range(first, last + 1):
                            if m < last:
                                rows = P if m < MT - 1 else LAST
                                dve.wait_ge(gelu_ready, n * MT + m + 1)
                                dve.wait_ge(a_done, n * MT + m + 1)
                                before = (n * MT + m - 3) if 3 <= m < MT - 1 else ((n - 1) * MT + (3, 4, 2, 0, 0, 5)[m])
                                if before >= 0:
                                    dve.wait_ge(u_low, before + 1)
                                b_a = cols[0:rows, 2 * KD + m:2 * KD + m + 1]
                                nc.vector.scalar_tensor_tensor(
                                    u_[0:rows, u_slot(m), :], ps_a[0:rows, m % 2, :], b_a, gelu[0:rows, m % 2, :],
                                    ALU.add, ALU.mult).then_inc(u_ready, 1)
                            if m > first:
                                dve.wait_ge(u_high, n * MT + m)
                                nc.vector.tensor_tensor(u_cut[1][:, ring(n, m - 1), :], u_[:, u_slot(m - 1), :],
                                                        u_cut[0][:, ring(n, m - 1), :], ALU.subtract).then_inc(u_low, 1)
                    return stage

                def residual(n, p):
                    for j in range(2):
                        dve.wait_ge(out_done, n * 2 + j + 1)
                        here = inner[:, at(n, 2 * j):at(n, 2 * j) + 2 * D]
                        nc.vector.tensor_tensor(here, ps_o[:, j, :], here, ALU.add).then_inc(inner_done, 1)

                pipeline(NG, 2, [(1, normalise), (1, cut_w1), (2, gate(0, MT // 2)), (1, cut_z), (1, cut_w2), (0, stats),
                                 (2, gate(MT // 2, MT)), (3, residual)], NG)(dve)

            @block.scalar
            def _(act):
                act.wait_ge(cols_in, 16)

                def high_w1(n, p):
                    if n == 0:
                        for k in range(KD):
                            act.wait_ge(w1_in[k], 16)
                            nc.scalar.activation(w1[0][:, k, :], stage[:, k, :], ACT.Identity).then_inc(w_high, 1)

                def high_w2(n, p):
                    if n == 0:
                        act.wait_ge(w2_in, 16)
                        nc.scalar.activation(w2[0][:, :], stage[:, 0, :], ACT.Identity).then_inc(w_high, 1)

                def turned(n, p):
                    wait_reuse(act, a_done, n, 2, MT)
                    act.wait_ge(z_turned, n + 1)
                    wait_reuse(act, z_low, n, 1, KD)
                    for k in range(KD):
                        nc.scalar.activation(zT[:, k, :], ps_t[:, k, :], ACT.Identity, scale=cols[:, k:k + 1],
                                             bias=cols[:, KD + k:KD + k + 1]).then_inc(zT_ready, 1)
                    for k in range(KD):
                        act.wait_ge(zT_ready, n * KD + k + 1)
                        nc.scalar.activation(zT_cut[0][:, p, k, :], zT[:, k, :], ACT.Identity).then_inc(z_high, 1)

                def gelus(first, last):
                    def stage(n, p):
                        for m in range(first, last + 1):
                            if m < last:
                                rows = P if m < MT - 1 else LAST
                                act.wait_ge(g_done, n * MT + m + 1)
                                if n * MT + m >= 2:
                                    act.wait_ge(u_ready, n * MT + m - 1)
                                b_g = cols[0:rows, 2 * KD + MT + m:2 * KD + MT + m + 1]
                                nc.scalar.activation(gelu[0:rows, m % 2, :], ps_g[0:rows, m % 2, :], ACT.Gelu,
                                                     bias=b_g).then_inc(gelu_ready, 1)
                            if m > first:
                                act.wait_ge(u_ready, n * MT + m)
                                if n * MT + m - 1 >= RING:
                                    act.wait_ge(out_done, ((n * MT + m - 1 - RING) // MT + 1) * 2)
                                nc.scalar.activation(u_cut[0][:, ring(n, m - 1), :], u_[:, u_slot(m - 1), :],
                                                     ACT.Identity).then_inc(u_high, 1)
                    return stage

                pipeline(NG, 2, [(0, high_w1), (2, gelus(0, MT // 2)), (1, turned), (1, high_w2),
                                 (2, gelus(MT // 2, MT))], NG)(act)

            @block.tensor
            def _(pe):
                def turn(n, p):
                    wait_reuse(pe, zT_ready, n, 1, KD)
                    pe.wait_ge(z_ready, (n + 1) * 2 * G)
                    turn_group(nc, ps_t, z, ident, p).then_inc(z_turned, 1)

                def hidden(first, last):
                    def stage(n, p):
                        if n == 0:
                            pe.wait_ge(w_low, KD)
                        pe.wait_ge(z_low, n * KD + KD)
                        for m in range(first, last):
                            for which, out, done, read in ((1, ps_g, g_done, gelu_ready), (0, ps_a, a_done, u_ready)):
                                if n * MT + m >= 2:
                                    pe.wait_ge(read, n * MT + m - 1)
                                at = (which * MT + m) * P
                                last_mm = add_products(nc, out[:, m % 2, :], [
                                    (w1[i][:, k, at:at + P], zT_cut[j][:, p, k, :]) for k in range(KD) for i, j in PARTS_OF])
                                last_mm.then_inc(done, 1)
                    return stage

                def outwards(n, p):
                    if n == 0:
                        pe.wait_ge(w_low, KD + 1)
                    pe.wait_ge(u_low, n * MT + MT)
                    for t in range(G):
                        if t % 2 == 0:
                            wait_reuse(pe, inner_done, n, 1, 2)
                        last = add_products(nc, ps_o[:, t // 2, (t % 2) * D:(t % 2 + 1) * D], [
                            (u_cut[i][:, ring(n, m), t * P:(t + 1) * P], w2[j][:, m * D:(m + 1) * D])
                            for m in range(MT) for i, j in PARTS_OF])
                        if t % 2 == 1:
                            last.then_inc(out_done, 1)

                pipeline(NG, 2, [(2, hidden(0, MT // 2)), (1, turn), (3, outwards), (2, hidden(MT // 2, MT))], NG)(pe)

        S.close()


HF, DF = 16, 16
NU = B * HF
ROWS_Q = (0, 0, 1, 1, 0, 2)
ROWS_K = (0, 1, 0, 1, 2, 0)
DEPTH_S = 16 * len(ROWS_Q)


def full_attention(nc, x, ident, consts, w):
    tag = f"fa{Sems.phases}_"
    q_parts = nc.dram_tensor(tag + "q_parts", [NU, 3, DF, T], BF16).ap()
    k_parts = nc.dram_tensor(tag + "k_parts", [NU, 3, DF, T], BF16).ap()
    with ExitStack() as c:
        v_all = c.enter_context(nc.sbuf_tensor(tag + "v_all", [P, NU * WT * DF], F32))
        attention_inputs(nc, x, ident, consts, w, q_parts, k_parts, v_all)
        o_all = c.enter_context(nc.sbuf_tensor(tag + "o_all", [P, NU * WT * DF], F32))
        attention_heads(nc, ident, q_parts, k_parts, v_all, o_all)
        attention_out(nc, x, ident, w, o_all)


def attention_inputs(nc, x, ident, consts, w, q_parts, k_parts, v_all):
    with ExitStack() as c:
        sb = lambda name, shape, dt=F32: c.enter_context(nc.sbuf_tensor("ai_" + name, shape, dt))
        ps = lambda name, n: c.enter_context(nc.psum_tensor("ai_ps_" + name, [P, n, 512], F32))
        wp = sb("wp", [P, KD, 3, D])
        ln = LnBuffers(sb, "ai")
        z = sb("z", [P, 2, G, D])
        zT = sb("zT", [P, 2, KD, GT])
        parts = sb("parts", [P, 4, 3, GT], BF16)
        rest = sb("rest", [P, 2, GT])
        ps_t, ps_q, ps_v = ps("t", KD), ps("q", 4), ps("v", 2)
        S = Sems(nc)
        loaded, s = S("loaded"), LnSems(S)
        z_ready, z_turned, zT_ready = S("z_ready"), S("z_turned"), S("zT_ready")
        qk_done, v_done, top_ready, rest_ready, mid_ready, low_ready = (
            S(y) for y in ("qk_done", "v_done", "top_ready", "rest_ready", "mid_ready", "low_ready"))
        v_ready = S("v_ready")
        stored = [S(f"stored{m}") for m in range(4)]
        with nc.Block() as block:

            @block.sync
            def _(sp):
                sp.dma_start(wp[:, :, :, :], w["proj"]).then_inc(loaded, 16)

                def store(n, p):
                    b, at = n // (NG // B), n % (NG // B) * GT
                    for m in range(4):
                        to = q_parts if m < 2 else k_parts
                        first = b * HF + (m % 2) * 8
                        sp.wait_ge(low_ready, n * 4 + m + 1)
                        for part in range(3):
                            sp.dma_start(to[first:first + 8, part, :, at:at + GT],
                                         parts[:, m, part, :]).then_inc(stored[m], 16)

                for n in range(NG):
                    store(n, n % 2)
                for m in range(4):
                    sp.wait_ge(stored[m], 48 * NG)

            @block.gpsimd
            def _(pool):
                pipeline(NG, 2, [(0, lambda n, p: ln_scale(nc, pool, ln, s, consts, n, p))], NG)(pool)

            @block.scalar
            def _(act):
                def turned(n, p):
                    wait_reuse(act, v_done, n, 2, 2)
                    act.wait_ge(z_turned, n + 1)
                    for k in range(KD):
                        nc.scalar.activation(zT[:, p, k, :], ps_t[:, k, :], ACT.Identity).then_inc(zT_ready, 1)

                def tops(n, p):
                    for m in range(4):
                        act.wait_ge(qk_done, n * 4 + m + 1)
                        wait_reuse(act, stored[m], n, 1, 48)
                        nc.scalar.activation(parts[:, m, 0, :], ps_q[:, m, :], ACT.Identity).then_inc(top_ready, 1)

                def v_out(n, p):
                    b, first = n // (NG // B), n % (NG // B) * G
                    to = v_all[:, :].rearrange("p (b h t d) -> p b t h d", b=B, h=HF, t=WT)
                    for j in range(G):
                        if j % 2 == 0:
                            act.wait_ge(v_done, n * 2 + j // 2 + 1)
                        nc.scalar.activation(to[:, b, first + j, :, :],
                                             ps_v[:, j // 2, (j % 2) * D:(j % 2 + 1) * D].rearrange(
                                                 "p (h d) -> p h d", h=HF), ACT.Identity).then_inc(v_ready, 1)

                pipeline(NG, 2, [(1, turned), (2, tops), (2, v_out)], NG)(act)

            @block.vector
            def _(dve):
                def normalise(n, p):
                    wait_reuse(dve, z_turned, n, 2)
                    ln_apply(nc, dve, ln, s, x, z, n, p, z_ready)

                def cut(n, p):
                    for m in range(4):
                        at = n * 4 + m
                        dve.wait_ge(top_ready, at + 1)
                        if at >= 2:
                            dve.wait_ge(low_ready, at - 1)
                        nc.vector.tensor_tensor(rest[:, m % 2, :], ps_q[:, m, :], parts[:, m, 0, :],
                                                ALU.subtract).then_inc(rest_ready, 1)
                        dve.wait_ge(rest_ready, at + 1)
                        nc.vector.tensor_copy(parts[:, m, 1, :], rest[:, m % 2, :]).then_inc(mid_ready, 1)
                        dve.wait_ge(mid_ready, at + 1)
                        nc.vector.tensor_tensor(parts[:, m, 2, :], rest[:, m % 2, :], parts[:, m, 1, :],
                                                ALU.subtract).then_inc(low_ready, 1)

                pipeline(NG, 2, [(1, normalise), (0, lambda n, p: ln_stats(nc, dve, ln, s, x, n, p)),
                                 (2, cut)], NG)(dve)

            @block.tensor
            def _(pe):
                pe.wait_ge(loaded, 16)

                def turn(n, p):
                    wait_reuse(pe, zT_ready, n, 1, KD)
                    pe.wait_ge(z_ready, n * G + G)
                    turn_group(nc, ps_t, z, ident, p).then_inc(z_turned, 1)

                def products(n, p):
                    pe.wait_ge(zT_ready, n * KD + KD)
                    for m in range(4):
                        if n:
                            pe.wait_ge(rest_ready, (n - 1) * 4 + m + 1)
                        for k in range(KD):
                            last = nc.tensor.matmul(ps_q[:, m, :], wp[:, k, m // 2, (m % 2) * P:(m % 2 + 1) * P],
                                                    zT[:, p, k, :], start=(k == 0), stop=(k == KD - 1))
                        last.then_inc(qk_done, 1)
                    for j in range(G):
                        if j % 2 == 0 and n:
                            pe.wait_ge(v_ready, (n - 1) * G + j + 2)
                        for k in range(KD):
                            last = nc.tensor.matmul(ps_v[:, j // 2, (j % 2) * D:(j % 2 + 1) * D],
                                                    zT[:, p, k, j * P:(j + 1) * P], wp[:, k, 2, :],
                                                    start=(k == 0), stop=(k == KD - 1))
                        if j % 2:
                            last.then_inc(v_done, 1)

                pipeline(NG, 2, [(1, turn), (2, products)], NG)(pe)

        S.close()


def attention_heads(nc, ident, q_parts, k_parts, v_all, o_all):
    CH = T // GT
    PM = 8
    with ExitStack() as c:
        sb = lambda name, shape, dt=F32: c.enter_context(nc.sbuf_tensor("ah_" + name, shape, dt))
        q_st = sb("q_st", [P, 4, T], BF16)
        k_st = sb("k_st", [P, 4, T], BF16)
        va = sb("va", [P, 2, WT, 32])
        pm = sb("pm", [P, PM, 2 * GT])
        mpart = sb("mpart", [P, 2, WT, CH])
        mtop = sb("mtop", [P, 2, WT])
        mrest = sb("mrest", [P, 2, 2, WT])
        m3 = sb("m3", [P, WT, 32], BF16)
        m3T = sb("m3T", [P, WT, 32], BF16)
        num = sb("num", [P, GT])
        den = sb("den", [P, 2, WT])
        ps_m = [c.enter_context(nc.psum_tensor(f"ah_ps_m{i}", [P, GT], F32)) for i in range(3)]
        ps_s = [c.enter_context(nc.psum_tensor(f"ah_ps_s{i}", [P, 2, GT], F32)) for i in range(2)]
        ps_o = c.enter_context(nc.psum_tensor("ah_ps_o", [P, GT], F32))
        S = Sems(nc)
        q_in, k_in = [S(f"q_in{i}") for i in range(4)], [S(f"k_in{i}") for i in range(4)]
        cleared, va_ready, m_done, max_done, top_ready = (
            S(y) for y in ("cleared", "va_ready", "m_done", "max_done", "top_ready"))
        m_step, m3_ready, m3T_ready, m_placed = S("m_step"), S("m3_ready"), S("m3T_ready"), S("m_placed")
        s_done, p_ready, pv_done, pv_all, num_ready = (
            S(y) for y in ("s_done", "p_ready", "pv_done", "pv_all", "num_ready"))
        num_turned, den_step, o_done = S("num_turned"), S("den_step"), S("o_done")
        L_MAX, L_PLACE, L_EXP, L_OUT = 0, 1, 2, 3
        NM = WT * CH
        with nc.Block() as block:

            @block.sync
            def _(sp):
                def load(n, u):
                    wait_reuse(sp, s_done, n, 4, 2 * WT)
                    for i in range(len(ROWS_Q)):
                        rows = slice(DF * i, DF * i + DF)
                        for st, parts, which, arrived in ((q_st, q_parts, ROWS_Q[i], q_in), (k_st, k_parts, ROWS_K[i], k_in)):
                            src = parts[ds(n, 1), which, :, :].rearrange("a d t -> (a d) t")
                            sp.dma_start(st[rows, u, :], src).then_inc(arrived[u], 16)

                pipeline(NU, 4, [(0, load)], 4)(sp)

            @block.gpsimd
            def _(pool):
                for i, (area, value) in enumerate(((m3[:, :, :], 0.0), (k_st[96:P, :, :], 1.0), (va[:, :, :, :], 1.0))):
                    if i:
                        pool.wait_ge(cleared, i)
                    nc.gpsimd.memset(area, value).then_inc(cleared, 1)
                pool.wait_ge(cleared, 3)

                def copy_v(n, u):
                    wait_apart(pool, (cleared, 3), (pv_all, n - 1))
                    nc.gpsimd.tensor_copy(va[:, u % 2, :, 0:DF], v_all[:, ds(n * (WT * DF), WT * DF)].rearrange(
                        "p (t d) -> p t d", t=WT)).then_inc(va_ready, 1)

                def cut_max(n, u):
                    neg, mid = mrest[:, u % 2, 0, :], mrest[:, u % 2, 1, :]
                    wait_apart(pool, (cleared, 3), (top_ready, n + 1))
                    nc.gpsimd.tensor_scalar(neg, mtop[:, u % 2, :], -1.0, None, ALU.mult).then_inc(m_step, 1)
                    wait_apart(pool, (cleared, 3), (m_step, n * 4 + 1), (m3T_ready, n))
                    nc.gpsimd.tensor_copy(m3[:, :, 0], neg).then_inc(m_step, 1)
                    pool.wait_ge(m_step, n * 4 + 2)
                    nc.gpsimd.tensor_tensor(mid, neg, m3[:, :, 0], ALU.subtract).then_inc(m_step, 1)
                    wait_apart(pool, (cleared, 3), (m_step, n * 4 + 3))
                    nc.gpsimd.tensor_copy(m3[:, :, 1], mid).then_inc(m_step, 1)
                    pool.wait_ge(m_step, n * 4 + 4)
                    nc.gpsimd.tensor_tensor(m3[:, :, 2], mid, m3[:, :, 1], ALU.subtract).then_inc(m3_ready, 1)

                pipeline(NU, 4, [(L_EXP, copy_v), (L_MAX, cut_max)], 4)(pool)

            @block.scalar
            def _(act):
                def place_max(n, u):
                    act.wait_ge(m3T_ready, n + 1)
                    for a in range(4):
                        nc.scalar.activation(
                            q_st[96:99, u, :].rearrange("p (t a j) -> p t a j", t=WT, a=4)[:, :, a, :],
                            m3T[32 * a:32 * a + 3, :, :], ACT.Identity).then_inc(m_placed, 1)

                def exps(first, last):
                    def stage(n, u):
                        for i in range(first, last):
                            act.wait_ge(s_done, n * (2 * WT) + i + 1)
                            if i >= PM:
                                act.wait_ge(pv_done, n * (WT - 1) + (i - PM) // 2 + 1)
                            else:
                                wait_reuse(act, pv_all, n, 1)
                            nc.scalar.activation(pm[:, i % PM, :], ps_s[i % 2][:, :, :].rearrange("p a t -> p (a t)"),
                                                 ACT.Exp, scale=DF ** -0.5).then_inc(p_ready, 1)
                    return stage

                def numerators(n, u):
                    act.wait_ge(pv_all, n + 1)
                    wait_reuse(act, num_turned, n, 1)
                    nc.scalar.activation(num[:, :], ps_o[:, :], ACT.Identity).then_inc(num_ready, 1)

                pipeline(NU, 4, [(L_EXP, exps(0, 2)), (L_OUT, numerators), (L_EXP, exps(2, WT)), (L_PLACE, place_max),
                                 (L_EXP, exps(WT, 2 * WT))], 4)(act)

            @block.vector
            def _(dve):
                turned = ps_o[:, :].rearrange("p (j c r) -> p j c r", j=4, c=CH)
                d = lambda i: den[:, i, :].rearrange("p (j c) -> p j c", j=4)

                def finish_sum(n, u):
                    dve.wait_ge(num_turned, n + 1)
                    nc.vector.tensor_scalar(d(0), turned[:, :, :, DF], 1e-8, None, ALU.add).then_inc(den_step, 1)

                def finish_inverse(n, u):
                    dve.wait_ge(den_step, n * 2 + 1)
                    nc.vector.reciprocal(den[:, 1, :], den[:, 0, :]).then_inc(den_step, 1)

                def finish(n, u):
                    dve.wait_ge(den_step, n * 2 + 2)
                    to = o_all[:, :].rearrange("p (c j r) -> p j c r", c=CH, j=4)[:, :, :, ds(n * DF, DF)]
                    nc.vector.tensor_tensor(to, turned[:, :, :, 0:DF], d(1).unsqueeze(3).to_broadcast([P, 4, CH, DF]),
                                            ALU.mult).then_inc(o_done, 1)

                def maxima(first, last):
                    def stage(n, u):
                        for i in range(first, last):
                            dve.wait_ge(m_done, n * NM + i + 1)
                            nc.vector.reduce_max(mpart[:, u % 2, i // CH, i % CH:i % CH + 1], ps_m[i % 3][:, :],
                                                 AX_X).then_inc(max_done, 1)
                        if last < NM:
                            return
                        dve.wait_ge(max_done, n * NM + NM)
                        wait_reuse(dve, m_step, n, 2, 4)
                        nc.vector.reduce_max(mtop[:, u % 2, :], mpart[:, u % 2, :, :], AX_X).then_inc(top_ready, 1)
                    return stage

                def turn_max(n, u):
                    dve.wait_ge(m3_ready, n + 1)
                    wait_reuse(dve, m_placed, n, 1, 4)
                    nc.vector.transpose(m3T[:, :, :].rearrange("p t j -> p (t j)"),
                                        m3[:, :, :].rearrange("p t j -> p (t j)")).then_inc(m3T_ready, 1)

                pipeline(NU, 4, [(L_MAX, maxima(0, 8)), (L_OUT, finish_sum), (L_MAX, maxima(8, 9)),
                                 (L_OUT, finish_inverse), (L_MAX, maxima(9, 10)), (L_OUT, finish),
                                 (L_MAX, maxima(10, 20)), (L_PLACE, turn_max), (L_MAX, maxima(20, NM))], 4)(dve)

            @block.tensor
            def _(pe):
                def for_max(t, lo, hi):
                    def stage(n, u):
                        if t == 0 and lo == 0:
                            for arrived in (q_in, k_in):
                                pe.wait_ge(arrived[u], (n - u) * (16 * len(ROWS_Q) // 4) + 16 * len(ROWS_Q))
                        for ch in range(lo, hi):
                            i = t * CH + ch
                            if i >= 3:
                                pe.wait_ge(max_done, n * NM + i - 2)
                            else:
                                wait_reuse(pe, max_done, n, 1, NM)
                            nc.tensor.matmul(ps_m[i % 3][:, :], q_st[0:DEPTH_S, u, t * P:(t + 1) * P],
                                             k_st[0:DEPTH_S, u, ch * GT:(ch + 1) * GT], start=True,
                                             stop=True).then_inc(m_done, 1)
                    return stage

                def for_exp(t, half):
                    def stage(n, u):
                        i = 2 * t + half
                        if i == 0:
                            if isinstance(n, int) and n == 0:
                                pe.wait_ge(cleared, 3)
                            pe.wait_ge(m_placed, n * 4 + 4)
                        if i >= 2:
                            pe.wait_ge(p_ready, n * (2 * WT) + i - 1)
                        else:
                            wait_reuse(pe, p_ready, n, 1, 2 * WT)
                        for ch in range(2):
                            at = (2 * half + ch) * GT
                            last = nc.tensor.matmul(ps_s[i % 2][:, ch, :], k_st[0:DEPTH_S + 3, u, t * P:(t + 1) * P],
                                                    q_st[0:DEPTH_S + 3, u, at:at + GT], start=True, stop=True)
                        last.then_inc(s_done, 1)
                    return stage

                def weigh(t):
                    def stage(n, u):
                        if t == 0:
                            pe.wait_ge(va_ready, n + 1)
                            wait_reuse(pe, o_done, n, 1)
                        pe.wait_ge(p_ready, n * (2 * WT) + 2 * t + 2)
                        for ch in range(CH):
                            last = nc.tensor.matmul(ps_o[32 * ch:32 * ch + 32, :], va[:, u % 2, t, :],
                                                    pm[:, (2 * t + ch // 2) % PM, ch % 2 * GT:(ch % 2 + 1) * GT],
                                                    start=(t == 0), stop=(t == WT - 1))
                        last.then_inc(pv_done if t < WT - 1 else pv_all, 1)
                    return stage

                def turn_out(n, u):
                    pe.wait_ge(num_ready, n + 1)
                    for j in range(4):
                        last = nc.tensor.transpose(ps_o[:, j * P:(j + 1) * P], num[:, j * P:(j + 1) * P], ident[:, :])
                    last.then_inc(num_turned, 1)

                order = []
                for t in range(WT):
                    order += [(L_EXP, for_exp(t, 0)), (L_MAX, for_max(t, 0, 2)), (L_EXP, for_exp(t, 1)),
                              (L_MAX, for_max(t, 2, 3))]
                    if t == 1:
                        order.append((L_OUT, turn_out))
                    weighed = {0: [], 1: [], 2: [], 3: [0], 4: [1], 5: [2, 3], 6: [4, 5]}
                    order += [(L_EXP, weigh(i)) for i in weighed.get(t, [t - 1])]
                    order.append((L_MAX, for_max(t, 3, 4)))
                order.append((L_EXP, weigh(WT - 1)))
                pipeline(NU, 4, order, 4)(pe)

        S.close()


def attention_out(nc, x, ident, w, o_all):
    with ExitStack() as c:
        sb = lambda name, shape, dt=F32: c.enter_context(nc.sbuf_tensor("ao_" + name, shape, dt))
        ps = lambda name, n: c.enter_context(nc.psum_tensor("ao_ps_" + name, [P, n, 512], F32))
        wo = sb("wo", [P, KD, D])
        bo = sb("bo", [P, D])
        oT = sb("oT", [P, 2, KD, GT])
        out = sb("out", [P, 4, 2 * D])
        ps_t, ps_o = ps("t", 2 * KD), ps("o", 2 * B)
        S = Sems(nc)
        loaded, o_turned, oT_ready, out_done, out_ready, x_done = (
            S(y) for y in ("loaded", "o_turned", "oT_ready", "out_done", "out_ready", "x_done"))
        with nc.Block() as block:

            @block.sync
            def _(sp):
                sp.dma_start(wo[:, :, :], w["wo"]).then_inc(loaded, 16)
                sp.dma_start(bo[:, :], w["bo"].to_broadcast([P, D])).then_inc(loaded, 16)

            @block.tensor
            def _(pe):
                pe.wait_ge(loaded, 32)

                def turn(n, p):
                    wait_reuse(pe, oT_ready, n, 2, KD)
                    for j in range(2 * B):
                        for k in range(KD):
                            at = (n * 2 * B + j) * D + k * P
                            last = nc.tensor.transpose(ps_t[:, p * KD + k, j * P:(j + 1) * P], o_all[:, at:at + P],
                                                       ident[:, :])
                    last.then_inc(o_turned, 1)

                def project(n, p):
                    pe.wait_ge(oT_ready, n * KD + KD)
                    wait_reuse(pe, out_ready, n, 2, B)
                    for b in range(B):
                        for t in range(2):
                            at = (t * B + b) * P
                            for k in range(KD):
                                last = nc.tensor.matmul(ps_o[:, p * B + b, t * D:(t + 1) * D], oT[:, p, k, at:at + P],
                                                        wo[:, k, :], start=(k == 0), stop=(k == KD - 1))
                        last.then_inc(out_done, 1)

                pipeline(NG, 2, [(1, project), (0, turn)], NG)(pe)

            @block.scalar
            def _(act):
                def turned(n, p):
                    wait_reuse(act, out_done, n, 2, B)
                    act.wait_ge(o_turned, n + 1)
                    for k in range(KD):
                        nc.scalar.activation(oT[:, p, k, :], ps_t[:, p * KD + k, :], ACT.Identity).then_inc(oT_ready, 1)

                pipeline(NG, 2, [(0, turned)], NG)(act)

            @block.vector
            def _(dve):
                dve.wait_ge(loaded, 32)

                def add(n, p):
                    for b in range(B):
                        dve.wait_ge(out_done, n * B + b + 1)
                        wait_reuse(dve, x_done, n, 2, B)
                        nc.vector.tensor_tensor(out[:, p * B + b, :].rearrange("p (t d) -> p t d", t=2),
                                                ps_o[:, p * B + b, :].rearrange("p (t d) -> p t d", t=2),
                                                bo[:, :].unsqueeze(1).to_broadcast([P, 2, D]),
                                                ALU.add).then_inc(out_ready, 1)
                    for b in range(B):
                        xs = x[:, (b * WT + n * 2) * D:(b * WT + n * 2 + 2) * D]
                        dve.wait_ge(out_ready, n * B + b + 1)
                        nc.vector.tensor_tensor(xs, xs, out[:, p * B + b, :], ALU.add).then_inc(x_done, 1)

                pipeline(NG, 2, [(0, add)], NG)(dve)

        S.close()


def build(nc, ins, out):
    Sems.phases = 0
    with ExitStack() as c:
        x = c.enter_context(nc.sbuf_tensor("x_tiles", [P, NT * D], F32))
        ident = c.enter_context(nc.sbuf_tensor("identity", [P, P], F32))
        consts = c.enter_context(nc.sbuf_tensor("consts", [P, 3, 16], F32))
        rows = lambda dram: dram.rearrange("b (n p) d -> p (b n) d", p=P)
        S = Sems(nc)
        arrived = [S(f"x_in{n}") for n in range(NG)] + [S("ident_in")]
        with nc.Block() as block:

            @block.sync
            def _(sp):
                for n in range(NG):
                    sp.dma_start(x[:, n * G * D:(n + 1) * G * D].rearrange("p (n d) -> p n d", d=D),
                                 rows(ins["x"])[:, n * G:(n + 1) * G, :]).then_inc(arrived[n], 16)
                    if n == 0:
                        sp.dma_start(ident[:, :], ins["ident"]).then_inc(arrived[NG], 16)

            @block.gpsimd
            def _(pool):
                nc.gpsimd.memset(consts[:, 0, :], -0.5)
                nc.gpsimd.memset(consts[:, 1, :], EPS)
                nc.gpsimd.memset(consts[:, 2, :], -1.0)

        of = lambda prefix: {k[2:]: v for k, v in ins.items() if k.startswith(prefix)}
        token_wise_kan(nc, x, ident, of("k_"), consts, arrived)
        S.close()
        decay_memory(nc, x, ident, consts, of("m_"))
        token_wise_kan(nc, x, ident, of("k_"), consts)
        local_transformer(nc, x, ident, consts, of("l_"))
        full_attention(nc, x, ident, consts, of("f_"))
        local_transformer(nc, x, ident, consts, of("l_"), rows(out))




def by_block(w, k=P):
    return np.ascontiguousarray(w.reshape(-1, k, w.shape[-1]).transpose(1, 0, 2))


def kan_arrays(Win, bin_, W1, b1, W2, b2, Wout, bout):
    m = np.arange(64)
    place = 32 * (m // 8 % 4) + 8 * (m // 32) + m % 8
    pairs = lambda a: np.ascontiguousarray(a.reshape(8, 128).T)
    g_bias = np.zeros((P, 1), np.float32)
    g_bias[place, 0] = b2
    g_bias[16, 0] = 1.0
    wout = np.zeros((P, D), np.float32)
    wout[place] = Wout
    wout[16] = bout
    cols = np.concatenate([np.concatenate([bin_, bin_])[:, None], g_bias, pairs(W1), pairs(b1), pairs(W2)], 1)
    row, col = np.arange(P)[:, None, None], np.arange(P)[None, None, :]
    j = np.arange(8)[None, :, None]
    sel = (row % 64 == 8 * j + col // 16).astype(np.float32)
    w2_mask = (np.arange(32)[None, None, :] == 8 * (j // 4) + row // 16).astype(np.float32)
    return {"k_win": by_block(Win), "k_cols": cols, "k_sel": sel, "k_w2_mask": w2_mask, "k_wout": wout}


def memory_arrays(q_w, k_w, v_w, Wq, Wk, g_w, g_b, base_decay_logits, out_w, out_b, ln_g, ln_b):
    proj = np.stack([by_block(a.T) for a in (q_w, k_w, v_w, g_w)], 2)
    rank = np.zeros((P, 8, P), np.float32)
    for m, (w, hf) in enumerate(((Wq, 0), (Wq, 1), (Wk, 0), (Wk, 1))):
        for h in range(8):
            at = slice(16 * h, 16 * h + 16)
            rank[at, m, at] = w[8 * hf + h].T
            rank[at, m + 4, at] = w[8 * hf + h].T[np.arange(16) ^ 1]
    halves = lambda a: np.ascontiguousarray(a.reshape(2, P).T)
    cols = np.concatenate([halves(g_b), np.repeat(halves(base_decay_logits.reshape(-1)), B, 1)], 1)
    row, col, d = np.arange(P)[:, None, None], np.arange(P)[None, None, :], np.arange(16)[None, :, None]
    spread = ((row // 16 == col // 16) & (row % 16 == d)).astype(np.float32)
    sum_r = (np.arange(32)[None, None, :] == 8 * np.arange(4)[None, :, None] + row // 16).astype(np.float32)
    y_row = np.arange(P)
    feature = 16 * (y_row % 8) + 4 * (y_row % 32 // 8) + y_row // 32
    w_out = np.stack([np.ascontiguousarray(out_w.T[P * hf + feature]) for hf in range(2)], 1)
    return {"m_proj": proj, "m_rank": rank, "m_cols": cols, "m_rope": rope_table(), "m_spread": spread,
            "m_sum_r": sum_r, "m_out_w": w_out, "m_out_b": out_b[None], "m_ln_g": ln_g[None], "m_ln_b": ln_b[None]}


def rope_table():
    f = np.float32
    inv = f(1.0) / f(10000.0) ** (np.arange(8, dtype=f) / f(8))
    angle = (np.arange(T, dtype=f)[:, None] * inv[None, :]).astype(f)
    d = np.arange(P) % 16
    cos, sin = np.cos(angle).T[d // 2], np.sin(angle).T[d // 2]
    return np.ascontiguousarray(np.stack([cos, np.where(d % 2, -1, 1)[:, None] * sin], 1).astype(f))


def local_arrays(wqkv, q_scale, k_scale, wo, ln_g, ln_b, w1, b1, w2, b2):
    turn = (np.arange(64) + 32) % 64
    scales = np.stack([np.stack([np.concatenate([q, k]), np.concatenate([q[turn], k[turn]])])[None]
                       for q, k in zip(q_scale, k_scale)])
    hid = w2.shape[1]
    w1p = np.zeros((2, P, KD, 2, 6 * P), np.float32)
    for i in range(2):
        w1p[i, :, :, 0, :hid] = by_block(w1[i][:, :hid])
        w1p[i, :, :, 1, :hid] = by_block(w1[i][:, hid:])
    w2p = np.zeros((2, 6 * P, D), np.float32)
    w2p[:, :hid] = w2
    w2p[:, hid] = b2
    cols = np.zeros((2, P, 4 + 12), np.float32)
    cols[:, :, 0:2] = ln_g.reshape(2, 2, P).transpose(0, 2, 1)
    cols[:, :, 2:4] = ln_b.reshape(2, 2, P).transpose(0, 2, 1)
    b1p = np.zeros((2, 2, 6 * P), np.float32)
    b1p[:, :, :hid] = b1.reshape(2, 2, hid)
    cols[:, :, 4:] = b1p.reshape(2, 12, P).transpose(0, 2, 1)
    blocks = lambda a: np.stack([by_block(v) for v in a])
    return {"l_wqkv": blocks(wqkv), "l_scales": scales, "l_wo": blocks(wo), "l_w1": w1p, "l_w2": blocks(w2p),
            "l_mlp_cols": cols, "l_table": rotary_table(), "l_mask": window_mask()}


def rotary_table():
    f = np.float32
    half = np.arange(0, 64, 2, dtype=f)
    inv = f(1.0) / f(10000.0) ** (half / f(64))
    t = np.arange(T, dtype=f)
    angle = t[:, None] * inv[None, :]
    angle = np.concatenate([angle, angle], 1)
    base = (half + f(0.4 * 64)) / f(1.4 * 64)
    power = (t - f(T // 2)) / f(64.0)
    scale = base[None, :] ** power[:, None]
    scale = np.concatenate([scale, scale], 1)
    sign = np.where(np.arange(64) < 32, -1, 1).astype(f)
    cos, sin = np.cos(angle), np.sin(angle) * sign
    table = np.stack([np.stack([f(8) * cos * scale, cos / scale], 1), np.stack([f(8) * sin * scale, sin / scale], 1)], 1)
    table = table.reshape(WT, P, 2, 2 * 64).transpose(1, 0, 2, 3)
    return np.ascontiguousarray(table.astype(f))


def window_mask():
    i, j = np.arange(P)[:, None], np.arange(P)[None, :]
    far = np.float32(-3e38)
    own, before = np.where(j <= i, 0, far), np.where(j >= i, 0, far)
    none = np.full((P, P), far)
    return np.stack([np.concatenate(x, 1) for x in ((own, before), (before, own), (own, none))], 1).astype(np.float32)


def full_arrays(Wq, Wk, Wv, Wo, bo):
    return {"f_proj": np.stack([by_block(a.T) for a in (Wq, Wk, Wv)], 2), "f_wo": by_block(Wo.T), "f_bo": bo[None]}


def arrays_of(i):
    pick = lambda prefix, names: [i[prefix + n] for n in names.split()]
    arrays = {"x": i["L0_attn_x"], "ident": np.eye(P, dtype=np.float32)}
    arrays.update(kan_arrays(*pick("L0_ffn_", "Win bin_ W1 b1 W2 b2 Wout bout")))
    arrays.update(memory_arrays(*pick("L0_attn_", "q_w k_w v_w Wq Wk g_w g_b base_decay_logits out_w out_b ln_g ln_b")))
    arrays.update(local_arrays(*pick("L1_ffn_", "wqkv q_scale k_scale wo ln_g ln_b w1 b1 w2 b2")))
    arrays.update(full_arrays(*pick("L1_attn_", "Wq Wk Wv Wo bo")))
    return arrays


def kernel(**inputs):
    import concourse.bacc as bacc
    from concourse.bass_utils import run_bass_kernel_spmd

    nc = bacc.Bacc("TRN2", target_bir_lowering=False, num_devices=1)
    arrays, ins = {}, {}
    for name, a in arrays_of({name: np.asarray(a) for name, a in inputs.items()}).items():
        a = np.ascontiguousarray(a)
        arrays[f"in_{name}_dram"] = a
        ins[name] = nc.dram_tensor(f"in_{name}_dram", a.shape, mybir.dt.from_np(a.dtype), kind="ExternalInput").ap()
    out = nc.dram_tensor("out_0_dram", (B, T, D), F32, kind="ExternalOutput").ap()
    build(nc, ins, out)
    r = run_bass_kernel_spmd(nc, [arrays], core_ids=[0])
    return r.results[0]["out_0_dram"]
```
